# Optimizing a Trainium2 kernel written in Bass

```python
import numpy as np
import jax
import jax.numpy as jnp

def _softmax(x, axis=-1):
    return jax.nn.softmax(x, axis=axis)

def _gelu(x):
    return jax.nn.gelu(x, approximate=True)

def _silu(x):
    return jax.nn.silu(x)

def _sigmoid(x):
    return jax.nn.sigmoid(x)

def _layernorm(x, axis=-1, eps=1e-05):
    m = jnp.mean(x, axis=axis, keepdims=True)
    v = jnp.var(x, axis=axis, keepdims=True)
    return (x - m) / jnp.sqrt(v + eps)

def _scatter_add(tgt, idx, src, axis=0):
    return tgt.at[idx].add(src)

def _segment_sum(src, seg, n):
    return jax.ops.segment_sum(src, seg, n)
kernel_name = 'mk_gnn_resnorm_d4_gnn_r64_b95909'

def setup_inputs(seed: int=0):
    np.random.seed(seed)
    _w = jnp.asarray

    def _rec_inputs():
        import jax
        import jax.numpy as jnp
        _gk = jax.random.key(seed)
        x = -0.0003713 + 1 * jax.random.normal(jax.random.fold_in(_gk, 1), (50000, 128), jnp.float32)
        src = jax.random.randint(jax.random.fold_in(_gk, 2), (25000,), 0, 50000, jnp.int32)
        dst = jax.random.randint(jax.random.fold_in(_gk, 3), (25000,), 0, 50000, jnp.int32)
        _o = jnp.argsort(dst, stable=True)
        src = src[_o]
        dst = dst[_o]
        edge_attr_128 = -4.21973e-05 + 0.999841 * jax.random.normal(jax.random.fold_in(_gk, 12), (25000, 128), jnp.float32)
        return (x, src, dst, edge_attr_128)
    x, src, dst, edge_attr_128 = _rec_inputs()

    def _L0_gnn_setup():
        import jax, jax.numpy as jnp
        import numpy as np
        N_NODES = 100000
        N_EDGES = 9375
        D = 128
        key = jax.random.key(seed)
        ks = jax.random.split(key, 6)
        node_feat = jax.random.normal(ks[0], (N_NODES, D), dtype=jnp.float32)
        edge_feat = jax.random.normal(ks[1], (N_EDGES, D), dtype=jnp.float32)
        src = jax.random.randint(ks[2], (N_EDGES,), 0, N_NODES, dtype=jnp.int32)
        dst = jax.random.randint(ks[3], (N_EDGES,), 0, N_NODES, dtype=jnp.int32)
        lim = 1.0 / np.sqrt(D)
        W1 = jax.random.uniform(ks[4], (D, D), jnp.float32, -lim, lim)
        b1 = jnp.zeros((D,), jnp.float32)
        W2 = jax.random.uniform(ks[5], (D, D), jnp.float32, -lim, lim)
        b2 = jnp.zeros((D,), jnp.float32)
        return {'node_feat': node_feat, 'edge_feat': edge_feat, 'src': src, 'dst': dst, 'W1': W1, 'b1': b1, 'W2': W2, 'b2': b2}
    _L0_gnn_all = _L0_gnn_setup()
    _L0_gnn_in = {k: v for k, v in _L0_gnn_all.items() if k in ('W1', 'b1', 'W2', 'b2')}
    del _L0_gnn_all

    def _L1_gnn_setup():
        import jax, jax.numpy as jnp
        import numpy as np
        N_NODES = 50000
        N_EDGES = 12500
        IN_C = 128
        HID_C = 2 * IN_C
        OUT_C = 128
        NEG_SLOPE = 0.2

        def _gat_layer(x, edge_src, edge_dst, W, a_src, a_dst, b, n_nodes):
            h = x @ W
            alpha_src = h @ a_src
            alpha_dst = h @ a_dst
            e = alpha_src[edge_src] + alpha_dst[edge_dst]
            e = jnp.where(e > 0, e, NEG_SLOPE * e)
            m = jax.ops.segment_max(e, edge_dst, num_segments=n_nodes)
            w = jnp.exp(e - m[edge_dst])
            z = jax.ops.segment_sum(w, edge_dst, num_segments=n_nodes)
            alpha = w / z[edge_dst]
            out = jax.ops.segment_sum(alpha[:, None] * h[edge_src], edge_dst, num_segments=n_nodes)
            return out + b
        key = jax.random.key(seed)
        ks = jax.random.split(key, 12)
        x = jax.random.normal(ks[0], (N_NODES, IN_C), dtype=jnp.float32)
        edge_index = jax.random.randint(ks[1], (2, N_EDGES), 0, N_NODES, dtype=jnp.int32)

        def glorot(k, shape):
            fan_in = shape[0] if len(shape) == 2 else shape[0]
            return jax.random.normal(k, shape, dtype=jnp.float32) / np.sqrt(fan_in)
        W1 = glorot(ks[2], (IN_C, HID_C))
        a1_src = glorot(ks[3], (HID_C,))
        a1_dst = glorot(ks[4], (HID_C,))
        b1 = jnp.zeros((HID_C,), dtype=jnp.float32)
        W2 = glorot(ks[5], (HID_C, OUT_C))
        a2_src = glorot(ks[6], (OUT_C,))
        a2_dst = glorot(ks[7], (OUT_C,))
        b2 = jnp.zeros((OUT_C,), dtype=jnp.float32)
        return {'x': x, 'edge_index': edge_index, 'W1': W1, 'a1_src': a1_src, 'a1_dst': a1_dst, 'b1': b1, 'W2': W2, 'a2_src': a2_src, 'a2_dst': a2_dst, 'b2': b2}
    _L1_gnn_all = _L1_gnn_setup()
    _L1_gnn_in = {k: v for k, v in _L1_gnn_all.items() if k in ('W1', 'a1_src', 'a1_dst', 'b1', 'W2', 'a2_src', 'a2_dst', 'b2')}
    del _L1_gnn_all

    def _L2_gnn_setup():
        import jax, jax.numpy as jnp
        import numpy as np
        N = 50000
        E = 25000
        F_IN = 128
        HID = 128
        OUT = 128
        NEG_SLOPE = 0.2

        def _gat_layer(x, src, dst, W, a_src, a_dst, b, n_nodes):
            h = x @ W
            alpha_src = h @ a_src
            alpha_dst = h @ a_dst
            e = jax.nn.leaky_relu(alpha_src[src] + alpha_dst[dst], NEG_SLOPE)
            m = jax.ops.segment_max(e, dst, num_segments=n_nodes)
            e = jnp.exp(e - m[dst])
            s = jax.ops.segment_sum(e, dst, num_segments=n_nodes)
            alpha = e / s[dst]
            out = jax.ops.segment_sum(alpha[:, None] * h[src], dst, num_segments=n_nodes)
            return out + b
        key = jax.random.key(seed)
        ks = jax.random.split(key, 11)
        sW1 = 1.0 / np.sqrt(F_IN)
        sW2 = 1.0 / np.sqrt(HID)
        return {'x': jax.random.normal(ks[0], (N, F_IN), dtype=jnp.float32), 'edge_index': jax.random.randint(ks[1], (2, E), 0, N, dtype=jnp.int64 if jax.config.jax_enable_x64 else jnp.int32), 'W1': jax.random.normal(ks[2], (F_IN, HID), dtype=jnp.float32) * sW1, 'a1_src': jax.random.normal(ks[3], (HID,), dtype=jnp.float32) * sW2, 'a1_dst': jax.random.normal(ks[4], (HID,), dtype=jnp.float32) * sW2, 'b1': jnp.zeros((HID,), dtype=jnp.float32), 'W2': jax.random.normal(ks[5], (HID, OUT), dtype=jnp.float32) * sW2, 'a2_src': jax.random.normal(ks[6], (OUT,), dtype=jnp.float32) * sW2, 'a2_dst': jax.random.normal(ks[7], (OUT,), dtype=jnp.float32) * sW2, 'b2': jnp.zeros((OUT,), dtype=jnp.float32)}
    _L2_gnn_all = _L2_gnn_setup()
    _L2_gnn_in = {k: v for k, v in _L2_gnn_all.items() if k in ('W1', 'a1_src', 'a1_dst', 'b1', 'W2', 'a2_src', 'a2_dst', 'b2')}
    del _L2_gnn_all

    def _L3_gnn_setup():
        import jax, jax.numpy as jnp
        import numpy as np
        N = 50000
        E = 25000
        IN_DIM = 128
        HEADS = 4
        OUT_DIM = 32
        NEG_SLOPE = 0.2
        key = jax.random.key(seed)
        k1, k2, k3, k4, k5, k6 = jax.random.split(key, 6)
        x = jax.random.normal(k1, (N, IN_DIM), dtype=jnp.float32)
        src = jax.random.randint(k2, (E,), 0, N)
        dst = jax.random.randint(k3, (E,), 0, N)
        edge_index = jnp.stack([src, dst], axis=0).astype(jnp.int64)
        W = jax.random.normal(k4, (IN_DIM, HEADS * OUT_DIM), dtype=jnp.float32) * 0.08
        att = jax.random.normal(k5, (HEADS, 2 * OUT_DIM), dtype=jnp.float32) * 0.1
        bias = jnp.zeros((HEADS * OUT_DIM,), dtype=jnp.float32)
        return {'x': x, 'edge_index': edge_index, 'W': W, 'att': att, 'bias': bias}
    _L3_gnn_all = _L3_gnn_setup()
    _L3_gnn_in = {k: v for k, v in _L3_gnn_all.items() if k in ('W', 'att', 'bias')}
    del _L3_gnn_all
    return {'x': x, 'src': src, 'dst': dst, 'edge_attr_128': edge_attr_128, 'L0_gnn_W1': _L0_gnn_in['W1'], 'L0_gnn_b1': _L0_gnn_in['b1'], 'L0_gnn_W2': _L0_gnn_in['W2'], 'L0_gnn_b2': _L0_gnn_in['b2'], 'L1_gnn_W1': _L1_gnn_in['W1'], 'L1_gnn_a1_src': _L1_gnn_in['a1_src'], 'L1_gnn_a1_dst': _L1_gnn_in['a1_dst'], 'L1_gnn_b1': _L1_gnn_in['b1'], 'L1_gnn_W2': _L1_gnn_in['W2'], 'L1_gnn_a2_src': _L1_gnn_in['a2_src'], 'L1_gnn_a2_dst': _L1_gnn_in['a2_dst'], 'L1_gnn_b2': _L1_gnn_in['b2'], 'L2_gnn_W1': _L2_gnn_in['W1'], 'L2_gnn_a1_src': _L2_gnn_in['a1_src'], 'L2_gnn_a1_dst': _L2_gnn_in['a1_dst'], 'L2_gnn_b1': _L2_gnn_in['b1'], 'L2_gnn_W2': _L2_gnn_in['W2'], 'L2_gnn_a2_src': _L2_gnn_in['a2_src'], 'L2_gnn_a2_dst': _L2_gnn_in['a2_dst'], 'L2_gnn_b2': _L2_gnn_in['b2'], 'L3_gnn_W': _L3_gnn_in['W'], 'L3_gnn_att': _L3_gnn_in['att'], 'L3_gnn_bias': _L3_gnn_in['bias']}

def reference(x, src, dst, edge_attr_128, L0_gnn_W1, L0_gnn_b1, L0_gnn_W2, L0_gnn_b2, L1_gnn_W1, L1_gnn_a1_src, L1_gnn_a1_dst, L1_gnn_b1, L1_gnn_W2, L1_gnn_a2_src, L1_gnn_a2_dst, L1_gnn_b2, L2_gnn_W1, L2_gnn_a1_src, L2_gnn_a1_dst, L2_gnn_b1, L2_gnn_W2, L2_gnn_a2_src, L2_gnn_a2_dst, L2_gnn_b2, L3_gnn_W, L3_gnn_att, L3_gnn_bias):
    import jax
    import jax.numpy as jnp

    def _L0_gnn_ref(node_feat, edge_feat, src, dst, W1, b1, W2, b2):
        import jax, jax.numpy as jnp
        import numpy as np
        N_NODES = 100000
        N_EDGES = 9375
        D = 128
        m = node_feat[src] + edge_feat
        neigh = jax.ops.segment_sum(m, dst, num_segments=node_feat.shape[0])
        h = 2.0 * node_feat + neigh
        h = h @ W1 + b1
        h = jnp.where(h > 0, h, 0.01 * h)
        return h @ W2 + b2

    def _L1_gnn_ref(x, edge_index, W1, a1_src, a1_dst, b1, W2, a2_src, a2_dst, b2):
        import jax, jax.numpy as jnp
        import numpy as np
        N_NODES = 50000
        N_EDGES = 12500
        IN_C = 128
        HID_C = 2 * IN_C
        OUT_C = 128
        NEG_SLOPE = 0.2

        def _gat_layer(x, edge_src, edge_dst, W, a_src, a_dst, b, n_nodes):
            h = x @ W
            alpha_src = h @ a_src
            alpha_dst = h @ a_dst
            e = alpha_src[edge_src] + alpha_dst[edge_dst]
            e = jnp.where(e > 0, e, NEG_SLOPE * e)
            m = jax.ops.segment_max(e, edge_dst, num_segments=n_nodes)
            w = jnp.exp(e - m[edge_dst])
            z = jax.ops.segment_sum(w, edge_dst, num_segments=n_nodes)
            alpha = w / z[edge_dst]
            out = jax.ops.segment_sum(alpha[:, None] * h[edge_src], edge_dst, num_segments=n_nodes)
            return out + b
        n = x.shape[0]
        loops = jnp.arange(n, dtype=edge_index.dtype)
        src = jnp.concatenate([edge_index[0], loops])
        dst = jnp.concatenate([edge_index[1], loops])
        h = _gat_layer(x, src, dst, W1, a1_src, a1_dst, b1, n)
        h = jax.nn.relu(h)
        out = _gat_layer(h, src, dst, W2, a2_src, a2_dst, b2, n)
        return out

    def _L2_gnn_ref(x, edge_index, W1, a1_src, a1_dst, b1, W2, a2_src, a2_dst, b2):
        import jax, jax.numpy as jnp
        import numpy as np
        N = 50000
        E = 25000
        F_IN = 128
        HID = 128
        OUT = 128
        NEG_SLOPE = 0.2

        def _gat_layer(x, src, dst, W, a_src, a_dst, b, n_nodes):
            h = x @ W
            alpha_src = h @ a_src
            alpha_dst = h @ a_dst
            e = jax.nn.leaky_relu(alpha_src[src] + alpha_dst[dst], NEG_SLOPE)
            m = jax.ops.segment_max(e, dst, num_segments=n_nodes)
            e = jnp.exp(e - m[dst])
            s = jax.ops.segment_sum(e, dst, num_segments=n_nodes)
            alpha = e / s[dst]
            out = jax.ops.segment_sum(alpha[:, None] * h[src], dst, num_segments=n_nodes)
            return out + b
        n = x.shape[0]
        loop = jnp.arange(n, dtype=edge_index.dtype)
        src = jnp.concatenate([edge_index[0], loop])
        dst = jnp.concatenate([edge_index[1], loop])
        h = _gat_layer(x, src, dst, W1, a1_src, a1_dst, b1, n)
        h = jax.nn.relu(h)
        out = _gat_layer(h, src, dst, W2, a2_src, a2_dst, b2, n)
        return out

    def _L3_gnn_ref(x, edge_index, W, att, bias):
        import jax, jax.numpy as jnp
        import numpy as np
        N = 50000
        E = 25000
        IN_DIM = 128
        HEADS = 4
        OUT_DIM = 32
        NEG_SLOPE = 0.2
        src, dst = (edge_index[0], edge_index[1])
        n = x.shape[0]
        Wh = (x @ W).reshape(n, HEADS, OUT_DIM)
        a_src = jnp.einsum('nhf,hf->nh', Wh, att[:, :OUT_DIM])
        a_dst = jnp.einsum('nhf,hf->nh', Wh, att[:, OUT_DIM:])
        logits = jax.nn.leaky_relu(a_src[src] + a_dst[dst], negative_slope=NEG_SLOPE)
        seg_max = jax.ops.segment_max(logits, dst, num_segments=n)
        exp_s = jnp.exp(logits - seg_max[dst])
        denom = jnp.clip(jax.ops.segment_sum(exp_s, dst, num_segments=n), 1e-09, None)
        alpha = exp_s / denom[dst]
        messages = alpha[:, :, None] * Wh[src]
        out = jax.ops.segment_sum(messages.reshape(-1, HEADS * OUT_DIM), dst, num_segments=n)
        return out + bias
    edge_index = jnp.stack([src, dst])
    x = _layernorm(x + _L0_gnn_ref(x, edge_attr_128, src, dst, L0_gnn_W1, L0_gnn_b1, L0_gnn_W2, L0_gnn_b2), axis=-1)
    x = _layernorm(x + _L1_gnn_ref(x, edge_index, L1_gnn_W1, L1_gnn_a1_src, L1_gnn_a1_dst, L1_gnn_b1, L1_gnn_W2, L1_gnn_a2_src, L1_gnn_a2_dst, L1_gnn_b2), axis=-1)
    x = _layernorm(x + _L2_gnn_ref(x, edge_index, L2_gnn_W1, L2_gnn_a1_src, L2_gnn_a1_dst, L2_gnn_b1, L2_gnn_W2, L2_gnn_a2_src, L2_gnn_a2_dst, L2_gnn_b2), axis=-1)
    x = _layernorm(x + _L3_gnn_ref(x, edge_index, L3_gnn_W, L3_gnn_att, L3_gnn_bias), axis=-1)
    return x

_drawn_inputs = setup_inputs


def setup_inputs(seed=0):
    import zlib

    import numpy as np

    out = dict(_drawn_inputs(seed))
    spreads = {'L0_gnn_b1': (0.0, 0.275),
     'L0_gnn_b2': (0.0, 0.1),
     'L1_gnn_b1': (0.0, 0.1),
     'L1_gnn_b2': (0.0, 0.1),
     'L2_gnn_b1': (0.0, 0.1),
     'L2_gnn_b2': (0.0, 0.1),
     'L3_gnn_bias': (0.0, 0.1)}
    factors = {'L1_gnn_a1_dst': 14.568,
     'L1_gnn_a2_src': 3.121,
     'L1_gnn_a2_dst': 40.163,
     'L2_gnn_a1_dst': 18.613,
     'L2_gnn_a2_src': 3.726,
     'L2_gnn_a2_dst': 27.996,
     'L3_gnn_att': 3.391}
    for name, (base, spread) in spreads.items():
        noise = np.random.default_rng([zlib.crc32(name.encode()), seed]).standard_normal(out[name].shape)
        drawn = base * np.exp(spread * noise) if base else spread * noise
        out[name] = jnp.asarray(drawn.astype(out[name].dtype))
    for name, factor in factors.items():
        out[name] = (out[name] * factor).astype(out[name].dtype)
    return out
```

```python
import concourse.bass as bass
from concourse import mybir
from contextlib import ExitStack

F32 = mybir.dt.float32
I32 = mybir.dt.int32
ALU = mybir.AluOpType
ACT = mybir.ActivationFunctionType
AX = mybir.AxisListType

P = 128
D = 128
NODES = 50000
EDGES = 25000
MR = 4
NODE_MACROS = -(-NODES // (P * MR))
NODE_ROWS = NODE_MACROS * P * MR
TILES = -(-EDGES // (P * MR)) * MR
EDGE_MACROS = TILES // MR
SLOTS = TILES * P
TB = TILES // 2
BIG = 1.0e30
SKIP = 1.0e6
EPS = 1e-5
SLOPE = 0.2

PHASES = 6
HEADS = [1, 1, 1, 1, 1, 4]
HW = [D, D + 1, D + 1, D + 1, D + 1, D // 4 + 1]
WID = [HEADS[k] * HW[k] for k in range(PHASES)]
ROW = 132
MLP_LAYER = {0: 0, 1: 1, 3: 2, 4: 3}
HALVES = [1, 2, 1, 0]
DENSE_LAYER = [0, 1, 2, 3]


class Plan:

    def __init__(self):
        self.base, self.per, self.n = {}, {}, {}
        self.last, self.before, self.stores = {}, {}, {}
        self.total = {}
        self.ring_size, self.ring_seq, self.ring_full, self.ring_k = {}, {}, {}, {}
        self.now_seq, self.now_full = {}, {}

    def loop(self, name, n, steps, rings, last):
        self.before[name] = self.last
        self.stores[name] = {r: list(v) for r, v in self.now_full.items()}
        self.n[name] = n
        for step, k in steps:
            self.base[name, step] = self.total.get(step, 0)
            self.per[name, step] = k
            self.total[step] = self.total.get(step, 0) + n * k
        for ring, size, k in rings:
            self.ring_size[ring] = size
            seq = self.now_seq.get(ring, 0)
            full = self.now_full.get(ring, [0] * size)
            self.ring_seq[name, ring], self.ring_full[name, ring] = seq, list(full)
            self.ring_k[name, ring] = k
            for i in range(n):
                full[(seq + i) % size] += 16 * k
            self.now_seq[ring], self.now_full[ring] = seq + n, full
        self.last = {e: (s, self.total[s]) for e, s in last.items()}

    def seen(self, name, step, j, c, i=None, back=0):
        k = self.per[name, step]
        i = k - 1 if i is None else i
        return self.base[name, step] + k * c + i + 1 - k * back + j * (MR * k)

    def slot(self, name, ring, c):
        return (self.ring_seq[name, ring] + c) % self.ring_size[ring]

    def full(self, name, ring, j, c):
        size, k = self.ring_size[ring], self.ring_k[name, ring]
        s = self.slot(name, ring, c)
        first = (s - self.ring_seq[name, ring]) % size
        return self.ring_full[name, ring][s] + 16 * k * ((c - first) // size + 1) + j * (16 * k * (MR // size))

    def parity(self, name, step, c):
        return (self.base[name, step] + c) % 2


def make_plan():
    plan = Plan()

    def local(k):
        steps = [("sel_ready", 1), ("u_done", 2), ("u_out", 2), ("idx_up", 2 if k == 0 else 1)]
        rings = [("gat", 4, MR), ("dstb", 2, 1), ("ulo", 2, 1)]
        last = dict(pe="u_done", act="u_out", dve="sel_ready")
        if k == 0:
            steps += [("ea_added", 1)]
            rings += [("ea", 2, 1), ("own_in", 2, MR), ("own_out", 2, 1)]
        else:
            steps += [("sc", 1), ("esum", 1), ("e_ready", 1), ("eT", 1), ("scans", 1), ("mrow", 1),
                      ("mT", 1), ("d_ready", 1), ("w_ready", 1), ("m_kept", 1)]
            rings += [("pen", 2, HEADS[k])]
            if k == 5:
                steps += [("prod", 1)]
        plan.loop(f"L{k}", EDGE_MACROS, steps, rings, last)

    def mlp(layer):
        nh = HALVES[layer]
        return [("xT_ps", 1), ("xT", 1), ("y_ps", 1), ("y_used", 1)] + ([("h_ps", nh), ("hT", nh)] if nh else []) + ([("z", 1)] if layer == 0 else [])

    norm = [("res2", 1), ("stats", 1), ("aggr", 1), ("dev", 1), ("rstd", 1), ("x_ready", 1)]

    def dense(i):
        steps = mlp(i) + norm
        rings = [("xin", 4, 1), ("xst", 4, 1)]
        if i > 0:
            steps += [("res1", 1)] if i < 3 else []
            rings += [("gst", 2, 1)]
        plan.loop(f"D{i}", NODE_MACROS, steps, rings, dict(pe="y_ps", act="dev", dve="x_ready"))

    def post(k):
        steps = [("p_ps", 2), ("p_used", 2)]
        rings = [("uin", 2, 1), ("car", 2, 2)]
        last = dict(pe="p_ps", dve="own_sum")
        if k < 5:
            rings += [("xs", 2, 1)]
        if k in (1, 2, 3, 4):
            steps += [("selfed", 1), ("rz", 1)]
        if k == 5:
            steps += [("zmax", 1), ("rz", 1)]
            last["dve"] = "x_ready"
        if k in (2, 4, 5):
            rings += [("xr", 2, 1)]
            steps += [("un", 1), ("res1", 1)]
        if k in (0, 1, 3):
            steps += [("u_ready", 1)]
        if k in MLP_LAYER:
            steps += mlp(MLP_LAYER[k])
            last.update(pe="y_ps", act="y_used" if k else "hT")
        if k in (0, 2, 4, 5):
            steps += norm
            if k != 4:
                last["act"] = "dev"
            if k < 5:
                rings += [("xst", 4, 1)]
            else:
                rings += [("out_sc", 4, MR)]
                steps += [("idx_up", 1)]
        if k in (1, 3, 4):
            rings += [("gst", 2, 1)]
        if k == 4:
            steps += [("own_prod", 1)]
        if k < 5:
            steps += [("own_sc", 1), ("own_sum", 1)]
        plan.loop(f"P{k}", EDGE_MACROS, steps, rings, last)

    def combine(k):
        h = HEADS[k]
        steps = [("c_colb", 2 * h), ("c_row", 2 * h), ("c_mm", 2 * h), ("c_mb", 2 * h), ("c_dm", 2 * h),
                 ("c_wt", 2 * h), ("c_wtT_ps", 2 * h), ("c_wtT", 2 * h), ("c_sum_ps", 4 * h), ("c_sum", 4 * h),
                 ("c_mT", h + 1), ("c_arg", 2 * h), ("c_exp", 2 * h)]
        if k:
            steps += [("c_mT_ps", h + (k < 5)), ("c_t", 8 * h), ("c_back_ps", 2 * h), ("c_back", 2 * h)]
        plan.loop(f"C{k}", 1, steps, [("c_in", 1, 4), ("c_car", 1, 4), ("c_w0", 1, h), ("c_w1", 1, h)],
                  dict(pe="c_back_ps" if k else "c_sum_ps", act="c_exp", dve="c_back" if k else "c_arg"))

    local(0)
    dense(0)
    combine(0)
    post(0)
    for i in (1, 2, 3):
        dense(i)
    for k in range(1, PHASES):
        local(k)
        combine(k)
        post(k)
    return plan


def table_rows(table, first, count_per_partition):
    return table[bass.ds(first, P * MR), :].rearrange("(p u) d -> p u d", u=count_per_partition)


def edge_rows(table, first):
    return table[bass.ds(first, P * MR), :].rearrange("(u p) d -> p u d", p=P)


def wait(eng, semaphore, value, turn=None):
    if isinstance(value, int) and value <= 0:
        return
    eng.wait_ge(semaphore, value)
    if turn is not None and not isinstance(value, int):
        eng.sem_inc(turn, 1)


def groups(eng, n, body, peel):
    whole = n // MR
    if peel:
        body(0, MR)
    with eng.Fori(1 if peel else 0, whole) as j:
        body(j, MR)
    if n % MR:
        body(whole, n % MR)


FIRST = {"L0", "D0", "P0", "D1", "L1", "P1", "P2", "P4", "L5", "P5"}


def build(nc, x, src, dst, ea, w):
    plan = make_plan()
    out = w["out"]

    with ExitStack() as ctx:
        def sb(name, shape, dt=F32):
            return ctx.enter_context(nc.sbuf_tensor(name, shape, dt))

        def ps(name, shape):
            return ctx.enter_context(nc.psum_tensor(name, shape, F32))

        def sem(name):
            return ctx.enter_context(nc.semaphore(name))

        def dram(name, shape, dt=F32):
            return nc.dram_tensor(name, shape, dt, kind="Internal").ap()

        table = {n: dram(f"table_{n}", (NODE_ROWS + SLOTS, D)) for n in ("x1", "g2", "x2", "g3", "x3", "g5")}
        x0_own = dram("x0_own", (SLOTS, D))
        node_map = dram("node_map", (NODE_ROWS, 1), I32)
        dst_f = dram("dst_f", (TILES, P))
        pens = dram("pens", (TILES, 2, P))
        tile_sums = dram("tile_sums", (SLOTS, ROW))
        carry = dram("carry", (2, TILES, ROW))
        carry_w = dram("carry_w", (2, TILES, 4, P))
        GATHER_FROM = [x, table["x1"], table["g2"], table["x2"], table["g3"], table["g5"]]
        OWN_FROM = [x0_own] + [table[n][NODE_ROWS:NODE_ROWS + SLOTS, :] for n in ("x1", "g2", "x2", "g3")]
        RES_FROM = {k: table[n][NODE_ROWS:NODE_ROWS + SLOTS, :] for k, n in ((2, "x1"), (4, "x2"), (5, "x3"))}
        X_TO = {0: "x1", 2: "x2", 4: "x3"}
        G_TO = {1: "g2", 3: "g3", 4: "g5"}

        ident = sb("ident", [P, P])
        W1 = {0: sb("w1_0", [P, 1, P]), 1: sb("w1_1", [P, 2, P]), 2: sb("w1_2", [P, 1, P])}
        W2 = {0: sb("w2_0", [P, 1, P]), 1: sb("w2_1", [P, 2, P]), 2: sb("w2_2", [P, 1, P])}
        W3 = sb("w3", [P, P])
        B1 = sb("b1", [P, 4])
        BCOL = {0: 0, 1: 1, 2: 3}
        BB = sb("bb", [P, 4, 1, P])
        VB = sb("vb", [P, 8, P])
        A5 = sb("a5", [P, 2, P])
        src_i = sb("src_i", [P, TILES], I32)
        dstm_i = sb("dstm_i", [P, TILES], I32)
        scat_i = sb("scat_i", [P, TILES], I32)
        row_i = sb("row_i", [P, TILES], I32)
        src_row = sb("src_row", [P, TILES], I32)
        dcol = sb("dcol", [P, TILES])
        a_dst = sb("a_dst", [P, 4, TILES])
        e_self = sb("e_self", [P, TILES])
        m_loc = sb("m_loc", [P, 4, TILES])
        c_loc = sb("c_loc", [P, 4, TILES])
        c_self = sb("c_self", [P, TILES])
        seg = sb("seg", [TB, 2, 2, P])
        cross = sb("cross", [TB, 2, 2, TILES])
        mT = sb("mT", [TB, 5, 2, P])
        ends = sb("ends", [TB, 2, 2, ROW])
        csum = sb("csum", [TB, 2, 2, ROW])
        colb = sb("colb", [TB, 2, TB])
        mm = sb("mm", [TB, 2, TILES])
        mB = sb("mB", [TB, 2, 2, 4])
        wt = sb("wt", [TB, 2, TILES])
        wtT = sb("wtT", [TB, 2, 2, TB])
        tmax = sb("tmax", [TB, 3, P])
        arg = sb("arg", [TB, 4, P])
        coef = sb("coef", [TB, 2, 4, P])
        gat = sb("gat", [P, 4, MR, ROW])
        gw = sb("gw", [P, 2, MR, ROW])
        own_in = sb("own_in", [P, 2, MR, P])
        eab = sb("eab", [P, 2, MR, P])
        dstb = sb("dstb", [P, 2, MR, P])
        pen = sb("pen", [MR * 4, 2, 2, P])
        sel = sb("sel", [P, 2, MR, P])
        junk = sb("junk", [P, 2 * MR, P])
        sc = sb("sc", [P, 4, MR, 1])
        es = sb("es", [P, 4, MR, 1])
        eb = sb("eb", [P, 4, MR, 1])
        db = sb("db", [P, 4, MR, 1])
        wb = sb("wb", [P, 4, MR, 1])
        scan = sb("scan", [MR * 4, 2, P])
        mrow = sb("mrow", [MR * 4, P])
        ulo = sb("ulo", [P, 2, MR, ROW])
        xin = sb("xin", [P, 4, MR, P])
        xT = sb("xT", [P, 2, MR * P])
        zb = sb("zb", [P, 2, MR * P])
        hT = sb("hT", [P, 2, 2, MR * P])
        gst = sb("gst", [P, 2, MR, P])
        rb = sb("rb", [P, 2, MR, P])
        st = sb("st", [P, 2, MR, 6])
        eps_c = sb("eps_c", [P, 1])
        mv = sb("mv", [P, 2, MR, 2])
        rstd = sb("rstd", [P, 2, MR, 1])
        xst = sb("xst", [P, 4, MR, P])
        uin = sb("uin", [P, 2, MR, ROW])
        xs = sb("xs", [P, 2, MR, ROW])
        xr = sb("xr", [P, 2, MR, P])
        car_w = sb("car_w", [2, 2, MR, 4, P])
        car = sb("car", [2, 2, MR, ROW])
        t1 = sb("t1", [P, 2, MR, ROW])
        rz = sb("rz", [P, MR, 4, 1])
        own_s = sb("own_s", [P, 2, MR])
        own_m = sb("own_m", [P, 4, MR])
        idx_st = sb("idx_st", [P, 4, MR], I32)
        idx_st2 = sb("idx_st2", [P, 2, MR], I32)
        map_ix = sb("map_ix", [P, 16], I32)
        map_v = sb("map_v", [P, 16], I32)
        pi = sb("pi", [TB, 3, 2, P], I32)
        pf = sb("pf", [TB, 4, 2, P])
        peq = sb("peq", [TB, 2, 2, P])
        ppen = sb("ppen", [TB, 2, 2, P])
        w1T = sb("w1T", [P, 3, P])
        acol = sb("acol", [P, 6, 1])
        ab = sb("ab", [P, 6, P])
        ti_i = sb("ti_i", [TB, TILES], I32)
        tc_i = sb("tc_i", [TB, 1], I32)
        id_i = sb("id_i", [P, P], I32)
        map_i = sb("map_i", [P, NODE_ROWS // P], I32)
        ti = sb("ti", [TB, TILES])
        tcf = sb("tcf", [TB, 2])
        id_f = sb("id_f", [P, P])

        psT = [ps(f"psT{i}", [P, 512]) for i in range(2)]
        psH = [ps(f"psH{i}", [P, 512]) for i in range(2)]
        psY = ps("psY", [P, 512])
        psU = [ps(f"psU{i}", [P, 512]) for i in range(2)]
        psS = ps("psS", [P, 512])

        names = sorted({s for _, s in plan.base})
        S = {n: sem(n) for n in names}
        R = {r: [sem(f"{r}_full{i}") for i in range(size)] for r, size in plan.ring_size.items()}
        pre_fill, pre_load, w_load, pre_f, pre_v = map(sem, ("pre_fill", "pre_load", "w_load", "pre_f", "pre_v"))
        pre_ps, pre_tab, pre_st, pre_iota = map(sem, ("pre_ps", "pre_tab", "pre_st", "pre_iota"))
        pre_done, map_init, map_idx, map_dma = map(sem, ("pre_done", "map_init", "map_idx", "map_dma"))
        pre_pe = sem("pre_pe")
        map_read = sem("map_read")
        turn = {e: sem(f"turn_{e}") for e in ("pe", "act", "dve", "pool", "sp")}

        def enter(eng, name):
            for step, value in plan.before[name].values():
                wait(eng, S[step], value)

        def stored(eng, name, rings):
            for ring in rings:
                for i, value in enumerate(plan.stores[name].get(ring, [])):
                    wait(eng, R[ring][i], value)

        def own(eng, e):
            eng.sem_inc(turn[e], 1)

        def sp_turn(eng):
            return turn["sp"] if eng.engine == mybir.EngineType.SP else None

        def seen(eng, name, step, j, c, i=None, back=0):
            wait(eng, S[step], plan.seen(name, step, j, c, i, back), sp_turn(eng))

        def full(eng, name, ring, j, c):
            wait(eng, R[ring][plan.slot(name, ring, c)], plan.full(name, ring, j, c), sp_turn(eng))

        def left(eng, name, ring, j, c):
            k = plan.ring_k[name, ring]
            wait(eng, R[ring][plan.slot(name, ring, c)], plan.full(name, ring, j, c) - 16 * k)

        b1s = (w["L0_gnn_b1"], w["L1_gnn_b1"][0:P], w["L1_gnn_b1"][P:2 * P], w["L2_gnn_b1"])
        a1s = (w["L1_gnn_a1_src"][0:P], w["L1_gnn_a1_src"][P:2 * P], w["L1_gnn_a1_dst"][0:P],
               w["L1_gnn_a1_dst"][P:2 * P], w["L2_gnn_a1_src"], w["L2_gnn_a1_dst"])
        att = w["L3_gnn_att"]
        weight_loads = [
            (W1[0][:, 0, :], w["L0_gnn_W1"]), (W2[0][:, 0, :], w["L0_gnn_W2"]),
            (W1[1][:].rearrange("p a d -> p (a d)"), w["L1_gnn_W1"]),
            (W2[1][:], w["L1_gnn_W2"].rearrange("(a p) d -> p a d", p=P)),
            (W1[2][:, 0, :], w["L2_gnn_W1"]), (W2[2][:, 0, :], w["L2_gnn_W2"]), (W3[:], w["L3_gnn_W"]),
        ]
        weight_loads += [(B1[:, i:i + 1], b.rearrange("(p o) -> p o", o=1)) for i, b in enumerate(b1s)]
        weight_loads += [(acol[:, i, :], a.rearrange("(p o) -> p o", o=1)) for i, a in enumerate(a1s)]
        weight_loads += [(BB[:, i, 0, :], w[n].rearrange("(o d) -> o d", o=1).to_broadcast([P, P]))
                         for i, n in enumerate(("L0_gnn_b2", "L1_gnn_b2", "L2_gnn_b2", "L3_gnn_bias"))]
        weight_loads += [(VB[:, i, :], w[n].rearrange("(o d) -> o d", o=1).to_broadcast([P, P]))
                         for i, n in ((2, "L1_gnn_a2_src"), (3, "L1_gnn_a2_dst"), (6, "L2_gnn_a2_src"),
                                      (7, "L2_gnn_a2_dst"))]
        weight_loads += [(A5[:, s, 32 * h:32 * h + 32], att[h:h + 1, 32 * s:32 * s + 32].to_broadcast([P, 32]))
                         for s in range(2) for h in range(4)]

        TAIL = EDGES - (TILES - 1) * P
        index_loads = []
        for i, (a, shift) in enumerate(((dst, 0), (dst, 1), (src, 0))):
            index_loads += [
                (pi[:, i, 0, :], a[shift:shift + TB * P].rearrange("(t i) -> t i", i=P)),
                (pi[0:TB - 1, i, 1, :], a[TB * P + shift:(TILES - 1) * P + shift].rearrange("(t i) -> t i", i=P)),
                (pi[TB - 1:TB, i, 1, 0:TAIL - shift],
                 a[(TILES - 1) * P + shift:EDGES].rearrange("(t i) -> t i", t=1)),
            ]

        block = ctx.enter_context(nc.Block())

        @block.sync
        def _(sp):
            for to, a in weight_loads:
                sp.dma_start(to, a, allow_slow_non_contiguous=True).then_inc(w_load, 16)
            sp.wait_ge(pre_fill, 3)
            for to, a in index_loads:
                sp.dma_start(to, a).then_inc(pre_load, 16)
            sp.wait_ge(pre_tab, 1)
            for b in range(2):
                sp.dma_start(dst_f[TB * b:TB * b + TB, :], pf[:, 0, b, :]).then_inc(pre_st, 16)
                sp.dma_start(pens[TB * b:TB * b + TB, :, :], ppen[:, b, :, :]).then_inc(pre_st, 16)
            sp.wait_ge(pre_st, 64)

            def lagged(name, load, store, lag=2):
                n = plan.n[name]

                def body(j, cs):
                    for c in range(cs):
                        load(j, c)
                        if not isinstance(j, int) or MR * j + c >= lag:
                            if isinstance(j, int):
                                m = MR * j + c - lag
                                store(m // MR, m % MR)
                            else:
                                store(j if c >= lag else j - 1, (c - lag) % MR)
                groups(sp, n, body, True)
                for m in range(n - lag, n):
                    store(m // MR, m % MR)

            def first_row(j, c, start=0):
                return start + P * MR * c + j * (P * MR * MR)

            def local(k):
                name = f"L{k}"
                enter(sp, name)
                rings = ("ulo", "own_out") if k == 0 else ("ulo",)

                def load(j, c):
                    early = isinstance(j, int) and j == 0 and c < 2
                    if not early:
                        seen(sp, name, "sel_ready", j, c, back=2)
                    t = MR * c + j * (MR * MR)
                    s = plan.slot(name, "dstb", c)
                    sp.dma_start(dstb[:, s, :, :],
                                 dst_f[bass.ds(t, MR), :].rearrange("(o t) i -> o t i", o=1)
                                 .to_broadcast([P, MR, P])).then_inc(R["dstb"][s], 16)
                    if k == 0:
                        s = plan.slot(name, "ea", c)
                        if isinstance(j, int) and MR * j + c == EDGE_MACROS - 1:
                            whole = (EDGES - (EDGE_MACROS - 1) * MR * P) // P
                            r0 = (EDGE_MACROS - 1) * MR * P
                            assert whole == MR - 1
                            sp.dma_start(eab[:, s, 0:whole, :],
                                         ea[r0:r0 + whole * P, :].rearrange("(u p) d -> p u d", p=P)
                                         ).then_inc(R["ea"][s], 16)
                            sp.dma_start(eab[0:TAIL, s, whole, :], ea[r0 + whole * P:EDGES, :]
                                         ).then_inc(R["ea"][s], 16)
                        else:
                            sp.dma_start(eab[:, s, :, :], edge_rows(ea, first_row(j, c))
                                         ).then_inc(R["ea"][s], 16)
                    else:
                        if not early:
                            seen(sp, name, "scans", j, c, back=2)
                        s = plan.slot(name, "pen", c)
                        for h in range(HEADS[k]):
                            sp.dma_start(pen[MR * h:MR * h + MR, s, :, :], pens[bass.ds(t, MR), :, :]
                                         ).then_inc(R["pen"][s], 16)

                def store(j, c):
                    seen(sp, name, "u_out", j, c)
                    s = plan.slot(name, "ulo", c)
                    sp.dma_start(edge_rows(tile_sums, first_row(j, c)), ulo[:, s, :, :]).then_inc(R["ulo"][s], 16)
                    if k == 0:
                        full(sp, name, "own_in", j, c)
                        s = plan.slot(name, "own_out", c)
                        sp.dma_start(edge_rows(x0_own, first_row(j, c)), own_in[:, s, :, :]
                                     ).then_inc(R["own_out"][s], 16)
                lagged(name, load, store)

            def dense(i):
                name = f"D{i}"
                enter(sp, name)
                stored(sp, name, ("xst", "gst"))
                source = (x, table["x1"], table["x2"], table["x3"])[i]
                x_to = (table["x1"], table["x2"], table["x3"], out)[i]
                g_to = (None, table["g2"], table["g3"], table["g5"])[i]
                last_parts = (NODES - (NODE_MACROS - 1) * P * MR) // MR

                def load(j, c):
                    if not (isinstance(j, int) and j == 0):
                        seen(sp, name, "y_used" if i == 0 else "res2" if i == 3 else "res1", j, c, back=4)
                        seen(sp, name, "xT_ps", j, c, back=4)
                    s = plan.slot(name, "xin", c)
                    if i == 0 and isinstance(j, int) and MR * j + c == NODE_MACROS - 1:
                        sp.dma_start(xin[0:last_parts, s, :, :],
                                     x[NODES - last_parts * MR:NODES, :].rearrange("(p u) d -> p u d", u=MR)
                                     ).then_inc(R["xin"][s], 16)
                    else:
                        sp.dma_start(xin[:, s, :, :], table_rows(source, first_row(j, c), MR)
                                     ).then_inc(R["xin"][s], 16)

                def store(j, c):
                    if i > 0:
                        seen(sp, name, "y_used", j, c)
                        s = plan.slot(name, "gst", c)
                        sp.dma_start(table_rows(g_to, first_row(j, c), MR), gst[:, s, :, :]
                                     ).then_inc(R["gst"][s], 16)
                    seen(sp, name, "x_ready", j, c)
                    s = plan.slot(name, "xst", c)
                    if i == 3 and isinstance(j, int) and MR * j + c == NODE_MACROS - 1:
                        sp.dma_start(out[NODES - last_parts * MR:NODES, :].rearrange("(p u) d -> p u d", u=MR),
                                     xst[0:last_parts, s, :, :]).then_inc(R["xst"][s], 16)
                    else:
                        sp.dma_start(table_rows(x_to, first_row(j, c), MR), xst[:, s, :, :]
                                     ).then_inc(R["xst"][s], 16)
                lagged(name, load, store)

            def combine(k):
                name = f"C{k}"
                enter(sp, name)
                stored(sp, name, ("ulo", "own_out") if k == 0 else ("ulo",))
                sums = tile_sums.rearrange("(t p) w -> t p w", p=P)
                for d in range(2):
                    for b in range(2):
                        row = P - 1 if d == 0 else 0
                        sp.dma_start(ends[:, d, b, :], sums[TB * b:TB * b + TB, row, :]).then_inc(R["c_in"][0], 16)
                for d in range(2):
                    wait(sp, S["c_sum"], plan.seen(name, "c_sum", 0, 0, 4 * HEADS[k] - 1))
                    for b in range(2):
                        sp.dma_start(carry[d, TB * b:TB * b + TB, :], csum[:, d, b, :]).then_inc(R["c_car"][0], 16)
                for h in range(HEADS[k]):
                    for b in range(2):
                        r = 2 * h + b
                        wait(sp, S["c_exp"], plan.seen(name, "c_exp", 0, 0, r))
                        sp.dma_start(carry_w[:, TB * b:TB * b + TB, h, :].rearrange("d t i -> t d i"),
                                     coef[:, r % 2, 1:3, :]).then_inc(R[f"c_w{r % 2}"][0], 16)

            def post(k):
                name = f"P{k}"
                enter(sp, name)
                stored(sp, name, ("xst", "gst"))
                stored(sp, name, ("c_car", "c_w0", "c_w1"))

                def load(j, c):
                    early = isinstance(j, int) and j == 0 and c < 2
                    if not early:
                        seen(sp, name, "p_used", j, c, back=2)
                    s = plan.slot(name, "uin", c)
                    sp.dma_start(uin[:, s, :, :], edge_rows(tile_sums, first_row(j, c))).then_inc(R["uin"][s], 16)
                    t = MR * c + j * (MR * MR)
                    s = plan.slot(name, "car", c)
                    nh = HEADS[k]
                    sp.dma_start(car_w[:, s, :, 0:nh, :], carry_w[:, bass.ds(t, MR), 0:nh, :]
                                 ).then_inc(R["car"][s], 16)
                    sp.dma_start(car[:, s, :, :], carry[:, bass.ds(t, MR), :]).then_inc(R["car"][s], 16)
                    if k < 5:
                        if not early:
                            seen(sp, name, "y_used" if k == 0 else "selfed", j, c, back=2)
                        s = plan.slot(name, "xs", c)
                        sp.dma_start(xs[:, s, :, 0:P], edge_rows(OWN_FROM[k], first_row(j, c))
                                     ).then_inc(R["xs"][s], 16)
                    if k in RES_FROM:
                        if not early:
                            seen(sp, name, "res1", j, c, back=2)
                        s = plan.slot(name, "xr", c)
                        sp.dma_start(xr[:, s, :, :], edge_rows(RES_FROM[k], first_row(j, c))
                                     ).then_inc(R["xr"][s], 16)

                def store(j, c):
                    if k in X_TO:
                        seen(sp, name, "x_ready", j, c)
                        s = plan.slot(name, "xst", c)
                        sp.dma_start(edge_rows(table[X_TO[k]], first_row(j, c, NODE_ROWS)), xst[:, s, :, :]
                                     ).then_inc(R["xst"][s], 16)
                    if k in G_TO:
                        seen(sp, name, "y_used", j, c)
                        s = plan.slot(name, "gst", c)
                        sp.dma_start(edge_rows(table[G_TO[k]], first_row(j, c, NODE_ROWS)), gst[:, s, :, :]
                                     ).then_inc(R["gst"][s], 16)
                lagged(name, load, store)

            local(0)
            dense(0)
            combine(0)
            post(0)
            for i in (1, 2, 3):
                dense(i)
            for k in range(1, PHASES):
                local(k)
                combine(k)
                post(k)
            for slots in (R["xst"], R["gst"], R["ulo"], R["own_out"], R["out_sc"]):
                for i, q in enumerate(slots):
                    ring = next(r for r in R if R[r] is slots)
                    wait(sp, q, plan.now_full[ring][i])

        @block.gpsimd
        def _(pool):
            nc.gpsimd.iota(id_i[:], pattern=[[1, P]], base=0, channel_multiplier=-1).then_inc(pre_iota, 1)
            nc.gpsimd.iota(ti_i[:], pattern=[[1, TILES]], base=0, channel_multiplier=0).then_inc(pre_iota, 1)
            nc.gpsimd.iota(tc_i[:], pattern=[[1, 1]], base=0, channel_multiplier=1).then_inc(pre_iota, 1)
            nc.gpsimd.iota(row_i[:], pattern=[[P, TILES]], base=NODE_ROWS, channel_multiplier=1).then_inc(pre_iota, 1)
            nc.gpsimd.iota(map_i[:], pattern=[[1, NODE_ROWS // P]], base=0, channel_multiplier=NODE_ROWS // P
                           ).then_inc(pre_iota, 1)
            pool.wait_ge(pre_iota, 5)
            pool.dma_start(node_map.rearrange("(p n) o -> p (n o)", p=P), map_i[:]).then_inc(map_init, 16)
            pool.wait_ge(pre_done, 1)

            def gathers(k):
                name = f"L{k}"
                index = src_i if k == 0 else src_row
                if k:
                    stored(pool, name, ("xst", "gst"))
                    own(pool, "pool")

                def body(j, cs):
                    for c in range(cs):
                        cols = bass.ds(MR * c + j * (MR * MR), MR)
                        s = plan.slot(name, "gat", c)
                        seen(pool, name, "u_done", j, c, back=4)
                        if k == 0:
                            left(pool, name, "own_out", j, c)
                        own(pool, "pool")
                        nc.gpsimd.tensor_copy(idx_st[:, s, :], index[:, cols]).then_inc(S["idx_up"], 1)
                        if k == 0:
                            s2 = plan.slot(name, "own_in", c)
                            nc.gpsimd.tensor_copy(idx_st2[:, s2, :], dstm_i[:, cols]).then_inc(S["idx_up"], 1)
                        seen(pool, name, "idx_up", j, c)
                        own(pool, "pool")
                        for u in range(MR):
                            nc.gpsimd.indirect_dma_start(
                                out=gat[:, s, u, 0:P], out_offset=None, in_=GATHER_FROM[k],
                                in_offset=bass.IndirectOffsetOnAxis(ap=idx_st[:, s, u:u + 1], axis=0)
                            ).then_inc(R["gat"][s], 16)
                        if k == 0:
                            for u in range(MR):
                                nc.gpsimd.indirect_dma_start(
                                    out=own_in[:, s2, u, :], out_offset=None, in_=x,
                                    in_offset=bass.IndirectOffsetOnAxis(ap=idx_st2[:, s2, u:u + 1], axis=0)
                                ).then_inc(R["own_in"][s2], 16)
                groups(pool, EDGE_MACROS, body, name in FIRST)

            def scatter_out():
                name = "P5"

                def body(j, cs):
                    for c in range(cs):
                        s = plan.slot(name, "out_sc", c)
                        seen(pool, name, "x_ready", j, c)
                        left(pool, name, "out_sc", j, c)
                        own(pool, "pool")
                        nc.gpsimd.tensor_copy(idx_st[:, s, :], scat_i[:, bass.ds(MR * c + j * (MR * MR), MR)]
                                              ).then_inc(S["idx_up"], 1)
                        seen(pool, name, "idx_up", j, c)
                        own(pool, "pool")
                        for u in range(MR):
                            nc.gpsimd.indirect_dma_start(
                                out=out, out_offset=bass.IndirectOffsetOnAxis(ap=idx_st[:, s, u:u + 1], axis=0),
                                in_=xst[:, s, u, :], in_offset=None, bounds_check=NODES - 1, oob_is_err=False
                            ).then_inc(R["out_sc"][s], 16)
                groups(pool, EDGE_MACROS, body, True)

            def map_round(scatter, start, n, done):
                cols = bass.ds(start, n)
                index = scat_i if scatter else src_i
                nc.gpsimd.tensor_copy(map_ix[:, 0:n], index[:, cols]).then_inc(map_idx, 1)
                if scatter:
                    nc.gpsimd.tensor_copy(map_v[:, 0:n], row_i[:, cols]).then_inc(map_idx, 1)
                k = 2 if scatter else 1
                pool.wait_ge(map_idx, done * k + (0 if scatter else 2 * ROUNDS) + k)
                own(pool, "pool")
                for u in range(n):
                    off = bass.IndirectOffsetOnAxis(ap=map_ix[:, u:u + 1], axis=0)
                    if scatter:
                        nc.gpsimd.indirect_dma_start(out=node_map, out_offset=off, in_=map_v[:, u:u + 1],
                                                     in_offset=None, bounds_check=NODE_ROWS - 1, oob_is_err=False
                                                     ).then_inc(map_dma, 16)
                    else:
                        nc.gpsimd.indirect_dma_start(out=map_v[:, u:u + 1], out_offset=None, in_=node_map,
                                                     in_offset=off).then_inc(map_dma, 16)
                pool.wait_ge(map_dma, done * (256) + 16 * n + (0 if scatter else 16 * TILES))
                own(pool, "pool")
                if not scatter:
                    nc.gpsimd.tensor_copy(src_row[:, cols], map_v[:, 0:n]).then_inc(map_read, 1)

            ROUNDS = TILES // 16 + 1
            gathers(0)
            pool.wait_ge(map_init, 16)
            for scatter in (True, False):
                with pool.Fori(0, ROUNDS - 1) as r:
                    map_round(scatter, r * 16, 16, r)
                map_round(scatter, (ROUNDS - 1) * 16, TILES - 16 * (ROUNDS - 1), ROUNDS - 1)
            pool.wait_ge(map_read, ROUNDS)
            for k in range(1, PHASES):
                gathers(k)
            stored(pool, "P5", ("xst",))
            scatter_out()

        @block.tensor
        def _(pe):
            pe.wait_ge(pre_v, 1)
            pe.wait_ge(w_load, 16 * len(weight_loads))
            for i in range(2):
                nc.tensor.transpose(psH[0][:, P * i:P * i + P], W1[1][:, i, :], ident[:])
            nc.tensor.transpose(psH[0][:, 2 * P:3 * P], W1[2][:, 0, :], ident[:]).then_inc(pre_ps, 1)
            pe.wait_ge(pre_v, 2)
            for i in range(4):
                o = psH[1][:, P * i:P * i + P]
                if i < 2:
                    nc.tensor.matmul(o, ab[:, 2 * i, :], w1T[:, 0, :], start=True, stop=False)
                    last = nc.tensor.matmul(o, ab[:, 2 * i + 1, :], w1T[:, 1, :], start=False, stop=True)
                else:
                    last = nc.tensor.matmul(o, ab[:, 2 + i, :], w1T[:, 2, :], start=True, stop=True)
            last.then_inc(pre_ps, 1)
            pe.wait_ge(pre_v, 3)
            for i in range(4):
                for b in range(2):
                    last = nc.tensor.transpose(psT[i // 2][:, TILES * (i % 2) + TB * b:TILES * (i % 2) + TB * b + TB],
                                               pf[:, i, b, :], ident[0:TB, 0:TB])
            last.then_inc(pre_ps, 1)
            for d in range(2):
                pe.wait_ge(pre_v, 4 + d)
                for b in range(2):
                    last = nc.tensor.matmul((psS, psY)[d][0:TB, TB * b:TB * b + TB], colb[:, b, :],
                                            ident[0:TB, 0:TB], start=True, stop=True)
                last.then_inc(pre_ps, 1)
            pe.wait_ge(pre_done, 1)

            def local(k):
                name = f"L{k}"
                H, hw, wid = HEADS[k], HW[k], WID[k]
                enter(pe, name)

                def body(j, cs):
                    for c in range(cs):
                        s2 = c % 2
                        if k:
                            seen(pe, name, "e_ready", j, c)
                            own(pe, "pe")
                            nc.tensor.transpose(psS[0:MR * H, 0:P], eb[:, 0:H, :, 0].rearrange("p h u -> p (h u)"),
                                                ident[:]).then_inc(S["eT"], 1)
                            seen(pe, name, "mrow", j, c)
                            own(pe, "pe")
                            nc.tensor.transpose(psS[:, P:P + MR * H], mrow[0:MR * H, :],
                                                ident[0:MR * H, 0:MR * H]).then_inc(S["mT"], 1)
                        seen(pe, name, "sel_ready", j, c)
                        g = plan.slot(name, "gat", c)
                        for q in range(2):
                            if not (isinstance(j, int) and j == 0 and c == 0):
                                seen(pe, name, "u_out", j, c, i=q, back=1)
                            for i in range(2):
                                u = 2 * q + i
                                rhs = gw[:, s2, u, 0:wid] if k == 5 else gat[:, g, u, 0:wid]
                                last = nc.tensor.matmul(psU[q][:, ROW * i:ROW * i + wid], sel[:, s2, u, :], rhs,
                                                        start=True, stop=True)
                            last.then_inc(S["u_done"], 1)
                groups(pe, EDGE_MACROS, body, name in FIRST)

            def mlp(name, layer, j, cs, source, ready):
                nh = HALVES[layer]
                early = isinstance(j, int) and j == 0
                for c in cs:
                    s = plan.parity(name, "xT_ps", c)
                    ready(c)
                    if not (early and c < 2):
                        seen(pe, name, "xT", j, c, back=2)
                    for u in range(MR):
                        last = nc.tensor.transpose(psT[s][:, P * u:P * u + P], source(c, u), ident[:])
                    last.then_inc(S["xT_ps"], 1)
                for c in cs:
                    s = plan.parity(name, "xT_ps", c)
                    for half in range(nh):
                        if half == 0:
                            seen(pe, name, "xT", j, c)
                        off = nh * c + half
                        if not (early and off < 2):
                            wait(pe, S["hT"], plan.base[name, "hT"] + off - 1 + j * (nh * MR))
                        nc.tensor.matmul(psH[(plan.base[name, "h_ps"] + off) % 2][:], W1[layer][:, half, :],
                                         xT[:, s, :], start=True, stop=True).then_inc(S["h_ps"], 1)
                for c in cs:
                    s = plan.parity(name, "xT_ps", c)
                    seen(pe, name, "hT" if nh else "xT", j, c)
                    if not (early and c == 0):
                        seen(pe, name, "y_used", j, c, back=1)
                    for u in range(MR):
                        cols = slice(P * u, P * u + P)
                        if nh:
                            for half in range(nh):
                                last = nc.tensor.matmul(psY[:, cols], hT[:, s, half, cols], W2[layer][:, half, :],
                                                        start=half == 0, stop=half == nh - 1)
                        else:
                            last = nc.tensor.matmul(psY[:, cols], xT[:, s, cols], W3[:], start=True, stop=True)
                    last.then_inc(S["y_ps"], 1)

            def pairs(cs):
                return [list(range(cs))[a:a + 2] for a in range(0, cs, 2)]

            def dense(i):
                name = f"D{i}"
                enter(pe, name)

                def body(j, cs):
                    for two in pairs(cs):
                        mlp(name, i, j, two, lambda c, u: xin[:, plan.slot(name, "xin", c), u, :],
                            lambda c: full(pe, name, "xin", j, c))
                groups(pe, NODE_MACROS, body, name in FIRST)

            def combine(k):
                name = f"C{k}"
                H, hw = HEADS[k], HW[k]
                enter(pe, name)
                if k:
                    for h in list(range(H)) + ([4] if k < 5 else []):
                        r = h if h < 4 else H
                        if r >= 2:
                            wait(pe, S["c_mT"], plan.seen(name, "c_mT", 0, 0, r - 2))
                        for b in range(2):
                            a = e_self[:, TB * b:TB * b + TB] if h == 4 else m_loc[:, h, TB * b:TB * b + TB]
                            last = nc.tensor.transpose(psT[r % 2][0:TB, P * b:P * b + P], a, ident[:])
                        last.then_inc(S["c_mT_ps"], 1)
                wait(pe, R["c_in"][0], plan.full(name, "c_in", 0, 0))
                for r in range(2 * H):
                    h, d = r // 2, r % 2
                    wait(pe, S["c_colb"], plan.seen(name, "c_colb", 0, 0, r))
                    for b in range(2):
                        last = nc.tensor.matmul(psS[0:TB, TB * b:TB * b + TB], colb[:, b, :], ident[0:TB, 0:TB],
                                                start=True, stop=True)
                    last.then_inc(S["c_row"], 1)
                    wait(pe, S["c_wt"], plan.seen(name, "c_wt", 0, 0, r))
                    for bt in range(2):
                        for b in range(2):
                            last = nc.tensor.transpose(psT[bt][0:TB, TB * b:TB * b + TB], wt[:, bt, TB * b:TB * b + TB],
                                                       ident[0:TB, 0:TB])
                    last.then_inc(S["c_wtT_ps"], 1)
                    wait(pe, S["c_wtT"], plan.seen(name, "c_wtT", 0, 0, r))
                    for bt in range(2):
                        if r:
                            wait(pe, S["c_sum"], plan.seen(name, "c_sum", 0, 0, 2 * (r - 1) + bt))
                        o = psH[bt][0:TB, 0:hw]
                        for b in range(2):
                            last = nc.tensor.matmul(o, wtT[:, bt, b, :], ends[:, d, b, hw * h:hw * h + hw],
                                                    start=b == 0, stop=b == 1)
                        last.then_inc(S["c_sum_ps"], 1)
                if k:
                    for r in range(2 * H):
                        wait(pe, S["c_exp"], plan.seen(name, "c_exp", 0, 0, r))
                        if r >= 2:
                            wait(pe, S["c_back"], plan.seen(name, "c_back", 0, 0, r - 2))
                        last = nc.tensor.transpose(psT[r % 2][:, 0:TB], coef[:, r % 2, 0, :], ident[0:TB, 0:TB])
                        if k < 5:
                            last = nc.tensor.transpose(psT[r % 2][:, P:P + TB], coef[:, r % 2, 3, :],
                                                       ident[0:TB, 0:TB])
                        last.then_inc(S["c_back_ps"], 1)

            def post(k):
                name = f"P{k}"
                H, hw, wid = HEADS[k], HW[k], WID[k]
                enter(pe, name)

                def body(j, cs):
                    for two in pairs(cs):
                        for c in two:
                            full(pe, name, "car", j, c)
                            s = plan.slot(name, "car", c)
                            for q in range(2):
                                if not (isinstance(j, int) and j == 0 and c == 0):
                                    seen(pe, name, "p_used", j, c, i=q, back=1)
                                own(pe, "pe")
                                for i in range(2):
                                    u = 2 * q + i
                                    for h in range(H):
                                        last = nc.tensor.matmul(
                                            psU[q][:, ROW * i + hw * h:ROW * i + hw * h + hw], car_w[:, s, u, h, :],
                                            car[:, s, u, hw * h:hw * h + hw], start=True, stop=True)
                                last.then_inc(S["p_ps"], 1)
                        if k in (0, 1, 3):
                            mlp(name, MLP_LAYER[k], j, two, lambda c, u: xin[:, c, u, :],
                                lambda c: seen(pe, name, "u_ready", j, c))
                        if k == 4:
                            mlp(name, 3, j, two, lambda c, u: xst[:, plan.slot(name, "xst", c), u, :],
                                lambda c: seen(pe, name, "x_ready", j, c))
                groups(pe, EDGE_MACROS, body, name in FIRST)

            local(0)
            dense(0)
            combine(0)
            post(0)
            for i in (1, 2, 3):
                dense(i)
            for k in range(1, PHASES):
                local(k)
                combine(k)
                post(k)

        @block.scalar
        def _(act):
            act.wait_ge(w_load, 16 * len(weight_loads))
            act.wait_ge(pre_v, 1)

            def local(k):
                name = f"L{k}"
                H, wid = HEADS[k], WID[k]
                enter(act, name)

                def body(j, cs):
                    for c in range(cs):
                        if k:
                            seen(act, name, "d_ready", j, c)
                            nc.scalar.activation(wb[:, 0:H, :, :], db[:, 0:H, :, :], ACT.Exp
                                                 ).then_inc(S["w_ready"], 1)
                        s = plan.slot(name, "ulo", c)
                        for q in range(2):
                            if q == 0 and not (isinstance(j, int) and j == 0 and c < 2):
                                left(act, name, "ulo", j, c)
                            seen(act, name, "u_done", j, c, i=q)
                            nc.scalar.copy(ulo[:, s, 2 * q:2 * q + 2, 0:wid],
                                           psU[q][:, 0:2 * ROW].rearrange("p (u w) -> p u w", u=2)[:, :, 0:wid]
                                           ).then_inc(S["u_out"], 1)
                groups(act, EDGE_MACROS, body, name in FIRST)

            def mlp(name, layer, j, cs, g_free):
                nh = HALVES[layer]
                early = isinstance(j, int) and j == 0
                for c in cs:
                    s = plan.parity(name, "xT_ps", c)
                    seen(act, name, "xT_ps", j, c)
                    if not (early and c < 2):
                        seen(act, name, "h_ps" if nh else "y_ps", j, c, back=2)
                    nc.scalar.copy(xT[:, s, :], psT[s][:]).then_inc(S["xT"], 1)
                for c in cs:
                    s = plan.parity(name, "xT_ps", c)
                    for half in range(nh):
                        off = nh * c + half
                        seen(act, name, "h_ps", j, c, i=half)
                        if half == 0 and not (early and c < 2):
                            seen(act, name, "hT" if layer == 0 else "y_ps", j, c, back=2)
                        bank = psH[(plan.base[name, "h_ps"] + off) % 2]
                        bias = B1[:, BCOL[layer] + half:BCOL[layer] + half + 1]
                        if layer == 0:
                            nc.scalar.activation(zb[:, s, :], bank[:], ACT.Identity, bias=bias, scale=2.0
                                                 ).then_inc(S["z"], 1)
                        else:
                            nc.scalar.activation(hT[:, s, half, :], bank[:], ACT.Relu, bias=bias, scale=1.0
                                                 ).then_inc(S["hT"], 1)
                if g_free is not None:
                    for c in cs:
                        s = plan.slot(name, "gst", c)
                        if not (early and c < 2):
                            g_free(j, c)
                        left(act, name, "gst", j, c)
                        seen(act, name, "y_ps", j, c)
                        nc.scalar.copy(gst[:, s, :, :], psY[:].rearrange("p (u d) -> p u d", u=MR)
                                       ).then_inc(S["y_used"], 1)

            def pairs(cs):
                return [list(range(cs))[a:a + 2] for a in range(0, cs, 2)]

            def deviation(name, j, cs):
                for c in cs:
                    seen(act, name, "aggr", j, c)
                    nc.scalar.activation(rstd[:, c % 2, :, 0], mv[:, c % 2, :, 1], ACT.Sqrt, bias=eps_c[:],
                                         scale=1.0).then_inc(S["dev"], 1)

            def dense(i):
                name = f"D{i}"
                enter(act, name)

                def g_free(j, c):
                    if i < 3:
                        seen(act, name, "res1", j, c, back=2)

                def body(j, cs):
                    for two in pairs(cs):
                        mlp(name, i, j, two, g_free if i else None)
                        deviation(name, j, two)
                groups(act, NODE_MACROS, body, name in FIRST)

            def combine(k):
                name = f"C{k}"
                H = HEADS[k]
                enter(act, name)
                for r in range(2 * H):
                    wait(act, S["c_dm"], plan.seen(name, "c_dm", 0, 0, r))
                    nc.scalar.activation(wt[:], mm[:], ACT.Exp).then_inc(S["c_wt"], 1)
                for r in range(2 * H):
                    wait(act, S["c_arg"], plan.seen(name, "c_arg", 0, 0, r))
                    if r >= 2:
                        if k:
                            wait(act, S["c_back_ps"], plan.seen(name, "c_back_ps", 0, 0, r - 2))
                        ring = f"c_w{r % 2}"
                        wait(act, R[ring][0], plan.full(name, ring, 0, 0) - 16 * H + 16 * (r // 2))
                    lo, hi = (1, 3) if k == 0 else (0, 3) if k == 5 else (0, 4)
                    nc.scalar.activation(coef[:, r % 2, lo:hi, :], arg[:, lo:hi, :], ACT.Exp).then_inc(S["c_exp"], 1)

            def post(k):
                name = f"P{k}"
                enter(act, name)

                def g_free(j, c):
                    seen(act, name, "own_prod" if k == 4 else "own_sc", j, c, back=2)

                def body(j, cs):
                    for two in pairs(cs):
                        if k in (2, 4, 5):
                            deviation(name, j, two)
                        if k in MLP_LAYER:
                            mlp(name, MLP_LAYER[k], j, two, g_free if k else None)
                        if k == 0:
                            deviation(name, j, two)
                groups(act, EDGE_MACROS, body, name in FIRST)

            local(0)
            dense(0)
            combine(0)
            post(0)
            for i in (1, 2, 3):
                dense(i)
            for k in range(1, PHASES):
                local(k)
                combine(k)
                post(k)

        @block.vector
        def _(dve):
            vec = nc.vector
            vec.memset(pi[:, 0:2, :, :], NODES)
            vec.memset(pi[:, 2, :, :], 0)
            vec.memset(ulo[:], 0.0).then_inc(pre_fill, 3)
            vec.memset(gat[:, :, :, P:ROW], 1.0)
            vec.memset(xs[:, :, :, P:ROW], 1.0)
            vec.memset(mT[:], 0.0)
            vec.memset(csum[:], 0.0)
            vec.memset(ppen[:], -BIG)
            vec.memset(eps_c[:], EPS)
            dve.wait_ge(pre_iota, 5)
            vec.tensor_copy(id_f[:], id_i[:])
            vec.tensor_copy(ti[:], ti_i[:])
            vec.tensor_copy(tcf[:, 0:1], tc_i[:]).then_inc(pre_f, 1)
            dve.wait_ge(pre_f, 1)
            vec.tensor_scalar(tcf[:, 1:2], tcf[:, 0:1], float(TB), None, ALU.add).then_inc(pre_f, 1)
            vec.tensor_scalar(ident[:], id_f[:], 0.0, None, ALU.is_equal).then_inc(pre_v, 1)
            dve.wait_ge(w_load, 16 * len(weight_loads))
            vec.tensor_copy(ab[:], acol[:].to_broadcast([P, 6, P]))
            dve.wait_ge(pre_ps, 1)
            vec.tensor_copy(w1T[:].rearrange("p a d -> p (a d)"), psH[0][:, 0:3 * P]).then_inc(pre_v, 1)
            dve.wait_ge(pre_ps, 2)
            vec.tensor_copy(VB[:, 0:2, :].rearrange("p a d -> p (a d)"), psH[1][:, 0:2 * P])
            vec.tensor_copy(VB[:, 4:6, :].rearrange("p a d -> p (a d)"), psH[1][:, 2 * P:4 * P]).then_inc(pre_f, 1)
            dve.wait_ge(pre_load, 16 * len(index_loads))
            dve.wait_ge(pre_f, 3)
            vec.tensor_copy(pf[:, 0, :, :], pi[:, 0, :, :])
            vec.tensor_copy(pf[:, 1, :, :], pi[:, 1, :, :])
            vec.tensor_copy(pf[:, 3, :, :], pi[:, 2, :, :]).then_inc(pre_f, 1)
            dve.wait_ge(pre_f, 4)
            vec.tensor_tensor(peq[:, 0, :, :], pf[:, 0, :, :], pf[:, 1, :, :], ALU.is_equal).then_inc(pre_f, 1)
            dve.wait_ge(pre_f, 5)
            vec.scalar_tensor_tensor(out=pf[:, 1, :, :], in0=peq[:, 0, :, :], scalar=SKIP, in1=pf[:, 0, :, :],
                                     op0=ALU.mult, op1=ALU.add)
            vec.tensor_scalar(pf[:, 2, :, :], pf[:, 0, :, :], float(NODES - 1), None, ALU.min).then_inc(pre_v, 1)
            vec.tensor_tensor(peq[:, 1, :, 1:P], pf[:, 0, :, 1:P], pf[:, 0, :, 0:P - 1], ALU.not_equal
                              ).then_inc(pre_f, 1)
            dve.wait_ge(pre_f, 6)
            vec.tensor_scalar(ppen[:, :, 0, 1:P], peq[:, 1, :, 1:P], -BIG, None, ALU.mult)
            vec.tensor_scalar(ppen[:, :, 1, 0:P - 1], peq[:, 1, :, 1:P], -BIG, None, ALU.mult).then_inc(pre_tab, 1)
            for d in range(2):
                col = 0 if d == 0 else P - 1
                for b in range(2):
                    vec.tensor_scalar(seg[:, d, b, :], pf[:, 0, b, :], pf[:, 0, b, col:col + 1], -BIG,
                                      ALU.not_equal, ALU.mult)
            dve.wait_ge(pre_ps, 3)
            vec.tensor_copy(dcol[:], psT[0][:, 0:TILES])
            vec.tensor_copy(scat_i[:], psT[0][:, TILES:2 * TILES])
            vec.tensor_copy(dstm_i[:], psT[1][:, 0:TILES])
            vec.tensor_copy(src_i[:], psT[1][:, TILES:2 * TILES]).then_inc(pre_f, 1)
            for d in range(2):
                col = P - 1 if d == 0 else 0
                for b in range(2):
                    last = vec.tensor_copy(colb[:, b, :], pf[:, 0, b, col:col + 1].to_broadcast([TB, TB]))
                last.then_inc(pre_v, 1)
                dve.wait_ge(pre_ps, 4 + d)
                bank = (psS, psY)[d]
                other = 0 if d == 0 else P - 1
                for b in range(2):
                    vec.tensor_scalar(mm[:, b, :], bank[0:TB, 0:TILES], pf[:, 0, b, other:other + 1], -BIG,
                                      ALU.not_equal, ALU.mult)
                    last = vec.tensor_scalar(wt[:, b, :], ti[:], tcf[:, b:b + 1], -BIG,
                                             ALU.is_ge if d == 0 else ALU.is_le, ALU.mult)
                last.then_inc(pre_f, 1)
                dve.wait_ge(pre_f, 8 + 2 * d)
                vec.tensor_tensor(cross[:, d, :, :], mm[:], wt[:], ALU.add).then_inc(pre_f, 1)
                dve.wait_ge(pre_f, 9 + 2 * d)
            vec.memset(id_f[:, 0:1], 0.0).then_inc(pre_done, 1)

            def local(k):
                name = f"L{k}"
                H = HEADS[k]
                enter(dve, name)

                def body(j, cs):
                    for c in range(cs):
                        g = plan.slot(name, "gat", c)
                        s2 = c % 2
                        cols = bass.ds(MR * c + j * (MR * MR), MR)
                        early = isinstance(j, int) and j == 0
                        full(dve, name, "gat", j, c)
                        if k == 0:
                            full(dve, name, "ea", j, c)
                            if isinstance(j, int) and MR * j + c == EDGE_MACROS - 1:
                                s = plan.slot(name, "ea", c)
                                dve.wait_ge(R["ea"][s], plan.full(name, "ea", j, c) + 16)
                            vec.tensor_tensor(gat[:, g, :, 0:P], gat[:, g, :, 0:P],
                                              eab[:, plan.slot(name, "ea", c), :, :], ALU.add
                                              ).then_inc(S["ea_added"], 1)
                            seen(dve, name, "ea_added", j, c)
                        elif k < 5:
                            for u in range(MR):
                                last = vec.tensor_tensor_reduce(junk[:, u, :], gat[:, g, u, 0:P],
                                                                VB[:, 2 * (k - 1), :], 1.0, 0.0, ALU.mult, ALU.add,
                                                                sc[:, 0, u, :])
                            last.then_inc(S["sc"], 1)
                        else:
                            vec.tensor_tensor(junk[:, 0:MR, :], gat[:, g, :, 0:P], A5[:, 0:1, :].to_broadcast([P, MR, P]),
                                              ALU.mult).then_inc(S["prod"], 1)
                            seen(dve, name, "prod", j, c)
                            vec.tensor_reduce(sc[:, :, :, 0].rearrange("p h u -> p u h"),
                                              junk[:, 0:MR, :].rearrange("p u (h e) -> p u h e", h=4), AX.X, ALU.add
                                              ).then_inc(S["sc"], 1)
                        if k:
                            seen(dve, name, "sc", j, c)
                            vec.tensor_tensor(es[:, 0:H, :, 0], sc[:, 0:H, :, 0], a_dst[:, 0:H, cols], ALU.add
                                              ).then_inc(S["esum"], 1)
                            seen(dve, name, "esum", j, c)
                            vec.scalar_tensor_tensor(out=eb[:, 0:H, :, 0], in0=es[:, 0:H, :, 0], scalar=SLOPE,
                                                     in1=es[:, 0:H, :, 0], op0=ALU.mult, op1=ALU.max
                                                     ).then_inc(S["e_ready"], 1)
                            full(dve, name, "pen", j, c)
                            seen(dve, name, "eT", j, c)
                            sp_ = plan.slot(name, "pen", c)
                            n = MR * H
                            vec.tensor_tensor_scan(scan[0:n, 0, :], pen[0:n, sp_, 0, :], psS[0:n, 0:P], -BIG,
                                                   ALU.add, ALU.max)
                            vec.tensor_tensor_scan(scan[0:n, 1, ::-1], pen[0:n, sp_, 1, ::-1], psS[0:n, 0:P][:, ::-1],
                                                   -BIG, ALU.add, ALU.max).then_inc(S["scans"], 1)
                            seen(dve, name, "scans", j, c)
                            vec.tensor_tensor(mrow[0:n, :], scan[0:n, 0, :], scan[0:n, 1, :], ALU.max
                                              ).then_inc(S["mrow"], 1)
                            seen(dve, name, "mT", j, c)
                            back = psS[:, P:P + n].rearrange("p (h u) -> p h u", h=H)
                            vec.tensor_tensor(db[:, 0:H, :, 0], eb[:, 0:H, :, 0], back, ALU.subtract
                                              ).then_inc(S["d_ready"], 1)
                            vec.tensor_scalar(m_loc[:, 0:H, cols], back, 0.0, None, ALU.add).then_inc(S["m_kept"], 1)
                        full(dve, name, "dstb", j, c)
                        if not (early and c < 2):
                            seen(dve, name, "u_done", j, c, back=2)
                        if k:
                            seen(dve, name, "w_ready", j, c)
                        sd = plan.slot(name, "dstb", c)
                        if k == 5:
                            o = gw[:, s2, :, :].rearrange("p u (h e) -> p u h e", h=4)
                            vec.tensor_tensor(o[:, :, :, 0:32],
                                              gat[:, g, :, 0:P].rearrange("p u (h e) -> p u h e", h=4),
                                              wb[:].rearrange("p h u o -> p u h o").to_broadcast([P, MR, 4, 32]),
                                              ALU.mult)
                            vec.tensor_copy(o[:, :, :, 32:33], wb[:].rearrange("p h u o -> p u h o"))
                        for u in range(MR):
                            col = dcol[:, bass.ds(MR * c + u + j * (MR * MR), 1)]
                            if k in (0, 5):
                                last = vec.tensor_scalar(sel[:, s2, u, :], dstb[:, sd, u, :], col, None, ALU.is_equal)
                            else:
                                last = vec.tensor_scalar(sel[:, s2, u, :], dstb[:, sd, u, :], col, wb[:, 0, u, :],
                                                         ALU.is_equal, ALU.mult)
                        last.then_inc(S["sel_ready"], 1)
                groups(dve, EDGE_MACROS, body, name in FIRST)

            def norm_stats(name, j, c):
                s2 = c % 2
                seen(dve, name, "res2", j, c)
                for u in range(MR):
                    last = vec.bn_stats(st[:, s2, u, :], rb[:, s2, u, :])
                last.then_inc(S["stats"], 1)
                seen(dve, name, "stats", j, c)
                own(dve, "dve")
                for u in range(MR):
                    last = vec.bn_aggr(mv[:, s2, u, :], st[:, s2, u, :])
                last.then_inc(S["aggr"], 1)

            def norm(name, ring, j, c):
                s = plan.slot(name, ring, c)
                s2 = c % 2
                seen(dve, name, "dev", j, c)
                vec.reciprocal(rstd[:, s2, :, :], rstd[:, s2, :, :]).then_inc(S["rstd"], 1)
                left(dve, name, ring, j, c)
                seen(dve, name, "rstd", j, c)
                for u in range(MR):
                    last = vec.tensor_scalar(xst[:, s, u, :], rb[:, s2, u, :], mv[:, s2, u, 0:1],
                                             rstd[:, s2, u, :], ALU.subtract, ALU.mult)
                last.then_inc(S["x_ready"], 1)

            def pairs(cs):
                return [list(range(cs))[a:a + 2] for a in range(0, cs, 2)]

            def leaky(name, j, c):
                s = plan.parity(name, "xT_ps", c)
                seen(dve, name, "z", j, c)
                if not (isinstance(j, int) and j == 0 and c < 2):
                    seen(dve, name, "y_ps", j, c, back=2)
                vec.scalar_tensor_tensor(out=hT[:, s, 0, :], in0=zb[:, s, :], scalar=0.01, in1=zb[:, s, :],
                                         op0=ALU.mult, op1=ALU.max).then_inc(S["hT"], 1)

            def dense(i):
                name = f"D{i}"
                enter(dve, name)

                def body(j, cs):
                    for two in pairs(cs):
                        if i == 0:
                            for c in two:
                                leaky(name, j, c)
                        for c in two:
                            residual(j, c)
                            norm_stats(name, j, c)
                        for c in two:
                            norm(name, "xst", j, c)

                def residual(j, c):
                        s2 = c % 2
                        xi = xin[:, plan.slot(name, "xin", c), :, :]
                        bias = BB[:, i, :, :].to_broadcast([P, MR, P])
                        r = rb[:, s2, :, :]
                        if i == 0:
                            seen(dve, name, "y_ps", j, c)
                            vec.tensor_tensor(r, psY[:].rearrange("p (u d) -> p u d", u=MR), xi, ALU.add
                                              ).then_inc(S["y_used"], 1)
                            seen(dve, name, "y_used", j, c)
                            vec.tensor_tensor(r, r, bias, ALU.add).then_inc(S["res2"], 1)
                        elif i < 3:
                            seen(dve, name, "y_used", j, c)
                            vec.tensor_tensor(r, gst[:, plan.slot(name, "gst", c), :, :], xi, ALU.add
                                              ).then_inc(S["res1"], 1)
                            seen(dve, name, "res1", j, c)
                            vec.tensor_tensor(r, r, bias, ALU.add).then_inc(S["res2"], 1)
                        else:
                            full(dve, name, "xin", j, c)
                            vec.tensor_tensor(r, xi, bias, ALU.add).then_inc(S["res2"], 1)
                groups(dve, NODE_MACROS, body, name in FIRST)

            def combine(k):
                name = f"C{k}"
                H, hw = HEADS[k], HW[k]
                enter(dve, name)

                def at(step, r):
                    wait(dve, S[step], plan.seen(name, step, 0, 0, r))

                if k:
                    for h in list(range(H)) + ([4] if k < 5 else []):
                        r = h if h < 4 else H
                        at("c_mT_ps", r)
                        vec.tensor_copy(mT[:, h, :, :].rearrange("p b i -> p (b i)"), psT[r % 2][0:TB, 0:2 * P]
                                        ).then_inc(S["c_mT"], 1)
                    if k == 5:
                        vec.memset(mT[:, 4, :, :], -BIG).then_inc(S["c_mT"], 1)
                    at("c_mT", H)
                else:
                    vec.memset(mT[:], 0.0).then_inc(S["c_mT"], 2)
                    at("c_mT", H)
                for r in range(2 * H):
                    h, d = r // 2, r % 2
                    col = P - 1 if d == 0 else 0
                    for b in range(2):
                        last = vec.tensor_copy(colb[:, b, :], mT[:, h, b, col:col + 1].to_broadcast([TB, TB]))
                    last.then_inc(S["c_colb"], 1)
                    at("c_row", r)
                    for bt in range(2):
                        last = vec.tensor_tensor(mm[:, bt, :], psS[0:TB, 0:TILES], cross[:, d, bt, :], ALU.add)
                    last.then_inc(S["c_mm"], 1)
                    at("c_mm", r)
                    if k:
                        vec.tensor_reduce(mB[:, d, :, h:h + 1], mm[:], AX.X, ALU.max).then_inc(S["c_mb"], 1)
                    else:
                        vec.memset(mB[:, d, :, h:h + 1], 0.0).then_inc(S["c_mb"], 1)
                    at("c_mb", r)
                    for bt in range(2):
                        last = vec.tensor_scalar(mm[:, bt, :], mm[:, bt, :], mB[:, d, bt, h:h + 1], None, ALU.subtract)
                    last.then_inc(S["c_dm"], 1)
                    at("c_wtT_ps", r)
                    for bt in range(2):
                        last = vec.tensor_copy(wtT[:, bt, :, :].rearrange("p b t -> p (b t)"), psT[bt][0:TB, 0:2 * TB])
                    last.then_inc(S["c_wtT"], 1)
                    for bt in range(2):
                        at("c_sum_ps", 2 * r + bt)
                        vec.tensor_copy(csum[:, d, bt, hw * h:hw * h + hw], psH[bt][0:TB, 0:hw]
                                        ).then_inc(S["c_sum"], 1)
                for r in range(2 * H):
                    h, b = r // 2, r % 2
                    if r:
                        at("c_exp", r - 1)
                    if k == 0:
                        last = vec.tensor_copy(arg[:, 1, :], seg[:, 0, b, :])
                        vec.tensor_copy(arg[:, 2, :], seg[:, 1, b, :]).then_inc(S["c_arg"], 1)
                        continue
                    for d in range(2):
                        last = vec.tensor_scalar(tmax[:, d, :], seg[:, d, b, :], mB[:, d, b, h:h + 1], None, ALU.add)
                    last.then_inc(S["c_t"], 1)
                    at("c_t", 4 * r)
                    for i, other in enumerate((tmax[:, 0, :], tmax[:, 1, :], mT[:, 4, b, :])):
                        vec.tensor_tensor(tmax[:, 2, :], mT[:, h, b, :] if i == 0 else tmax[:, 2, :], other, ALU.max
                                          ).then_inc(S["c_t"], 1)
                        at("c_t", 4 * r + 1 + i)
                    vec.tensor_tensor(arg[:, 0, :], mT[:, h, b, :], tmax[:, 2, :], ALU.subtract)
                    if k < 5:
                        vec.tensor_tensor(arg[:, 3, :], mT[:, 4, b, :], tmax[:, 2, :], ALU.subtract)
                    vec.tensor_tensor(arg[:, 1, :], tmax[:, 0, :], tmax[:, 2, :], ALU.subtract)
                    vec.tensor_tensor(arg[:, 2, :], tmax[:, 1, :], tmax[:, 2, :], ALU.subtract).then_inc(S["c_arg"], 1)
                    at("c_back_ps", r)
                    if k < 5:
                        vec.tensor_copy(c_self[:, TB * b:TB * b + TB], psT[r % 2][:, P:P + TB])
                    vec.tensor_copy(c_loc[:, h, TB * b:TB * b + TB], psT[r % 2][:, 0:TB]).then_inc(S["c_back"], 1)

            def post(k):
                name = f"P{k}"
                H, hw, wid = HEADS[k], HW[k], WID[k]
                layer = {0: 0, 2: 1, 4: 2, 5: 3}.get(k)
                enter(dve, name)
                if k == 5:
                    stored(dve, name, ("xst",))

                def tcol(a, j, c, u):
                    return a[:, bass.ds(MR * c + u + j * (MR * MR), 1)]

                def add_up(j, c):
                    s2 = c % 2
                    early = isinstance(j, int) and j == 0
                    su = plan.slot(name, "uin", c)
                    full(dve, name, "uin", j, c)
                    for q in range(2):
                        seen(dve, name, "p_ps", j, c, i=q)
                        for i in range(2):
                            u = 2 * q + i
                            for h in range(H):
                                a, z = hw * h, hw * h + hw
                                if k == 0:
                                    last = vec.tensor_tensor(t1[:, s2, u, a:z], uin[:, su, u, a:z],
                                                             psU[q][:, ROW * i + a:ROW * i + z], ALU.add)
                                else:
                                    last = vec.scalar_tensor_tensor(
                                        out=t1[:, s2, u, a:z], in0=uin[:, su, u, a:z],
                                        scalar=tcol(c_loc[:, h, :], j, c, u), in1=psU[q][:, ROW * i + a:ROW * i + z],
                                        op0=ALU.mult, op1=ALU.add)
                        last.then_inc(S["p_used"], 1)
                    if k < 5:
                        full(dve, name, "xs", j, c)
                        sx = plan.slot(name, "xs", c)
                    seen(dve, name, "p_used", j, c)
                    if k == 0:
                        if not (early and c < 4):
                            seen(dve, name, "xT_ps", j, c, back=4)
                        vec.scalar_tensor_tensor(out=xin[:, c, :, :], in0=t1[:, s2, :, 0:P], scalar=0.5,
                                                 in1=xs[:, sx, :, 0:P], op0=ALU.mult, op1=ALU.add
                                                 ).then_inc(S["u_ready"], 1)
                        return
                    if k < 5:
                        for u in range(MR):
                            last = vec.scalar_tensor_tensor(
                                out=t1[:, s2, u, 0:wid], in0=xs[:, sx, u, 0:wid], scalar=tcol(c_self, j, c, u),
                                in1=t1[:, s2, u, 0:wid], op0=ALU.mult, op1=ALU.add)
                        last.then_inc(S["selfed"], 1)
                        seen(dve, name, "selfed", j, c)
                        vec.reciprocal(rz[:, :, 0, :], t1[:, s2, :, P:P + 1]).then_inc(S["rz"], 1)
                        seen(dve, name, "rz", j, c)
                        if k in (1, 3):
                            if not early:
                                seen(dve, name, "xT_ps", j, c, back=4)
                            vec.tensor_tensor(xin[:, c, :, :], t1[:, s2, :, 0:P],
                                              rz[:, :, 0, :].to_broadcast([P, MR, P]), ALU.mult
                                              ).then_inc(S["u_ready"], 1)
                            return
                        vec.tensor_tensor(rb[:, s2, :, :], t1[:, s2, :, 0:P],
                                          rz[:, :, 0, :].to_broadcast([P, MR, P]), ALU.mult).then_inc(S["un"], 1)
                    else:
                        t = t1[:, s2, :, :].rearrange("p u (h e) -> p u h e", h=4)
                        vec.tensor_scalar(rz[:], t[:, :, :, 32:33], 1e-9, None, ALU.max).then_inc(S["zmax"], 1)
                        seen(dve, name, "zmax", j, c)
                        vec.reciprocal(rz[:], rz[:]).then_inc(S["rz"], 1)
                        seen(dve, name, "rz", j, c)
                        vec.tensor_tensor(rb[:, s2, :, :].rearrange("p u (h e) -> p u h e", h=4), t[:, :, :, 0:32],
                                          rz[:].to_broadcast([P, MR, 4, 32]), ALU.mult).then_inc(S["un"], 1)
                    full(dve, name, "xr", j, c)
                    seen(dve, name, "un", j, c)
                    vec.tensor_tensor(rb[:, s2, :, :], rb[:, s2, :, :], xr[:, plan.slot(name, "xr", c), :, :], ALU.add
                                      ).then_inc(S["res1"], 1)
                    seen(dve, name, "res1", j, c)
                    vec.tensor_tensor(rb[:, s2, :, :], rb[:, s2, :, :], BB[:, layer, :, :].to_broadcast([P, MR, P]),
                                      ALU.add).then_inc(S["res2"], 1)

                def scores(j, c, rows, vs, vd):
                    cols = bass.ds(MR * c + j * (MR * MR), MR)
                    for i, v in enumerate((vs, vd)):
                        for u in range(MR):
                            last = vec.tensor_tensor_reduce(junk[:, MR * i + u, :], rows[:, u, :], v, 1.0, 0.0, ALU.mult,
                                                            ALU.add, own_s[:, i, u:u + 1])
                    last.then_inc(S["own_sc"], 1)
                    seen(dve, name, "own_sc", j, c)
                    vec.tensor_scalar(a_dst[:, 0, cols], own_s[:, 1, :], 0.0, None, ALU.add)
                    vec.tensor_tensor(own_m[:, 0, :], own_s[:, 0, :], own_s[:, 1, :], ALU.add).then_inc(S["own_sum"], 1)
                    seen(dve, name, "own_sum", j, c)
                    vec.scalar_tensor_tensor(out=e_self[:, cols], in0=own_m[:, 0, :], scalar=SLOPE,
                                             in1=own_m[:, 0, :], op0=ALU.mult, op1=ALU.max)

                def body(j, cs):
                    for two in pairs(cs):
                        for c in two:
                            add_up(j, c)
                        if k == 0:
                            for c in two:
                                leaky(name, j, c)
                        for c in two:
                            s2 = c % 2
                            if k == 0:
                                seen(dve, name, "y_ps", j, c)
                                vec.tensor_tensor(rb[:, s2, :, :], psY[:].rearrange("p (u d) -> p u d", u=MR),
                                                  xs[:, plan.slot(name, "xs", c), :, 0:P], ALU.add
                                                  ).then_inc(S["y_used"], 1)
                                seen(dve, name, "y_used", j, c)
                                vec.tensor_tensor(rb[:, s2, :, :], rb[:, s2, :, :],
                                                  BB[:, layer, :, :].to_broadcast([P, MR, P]), ALU.add
                                                  ).then_inc(S["res2"], 1)
                            if k in (0, 2, 4, 5):
                                norm_stats(name, j, c)
                        for c in two:
                            if k in (0, 2, 4, 5):
                                if k == 4 and not (isinstance(j, int) and j == 0):
                                    seen(dve, name, "xT_ps", j, c, back=4)
                                norm(name, "out_sc" if k == 5 else "xst", j, c)
                            if k in (0, 2):
                                seen(dve, name, "x_ready", j, c)
                                scores(j, c, xst[:, plan.slot(name, "xst", c), :, :], VB[:, 2 * k, :],
                                       VB[:, 2 * k + 1, :])
                            if k in (1, 3):
                                seen(dve, name, "y_used", j, c)
                                scores(j, c, gst[:, plan.slot(name, "gst", c), :, :], VB[:, 2 * k, :],
                                       VB[:, 2 * k + 1, :])
                        if k == 4:
                            for c in two:
                                seen(dve, name, "y_used", j, c)
                                vec.tensor_tensor(junk[:, 0:MR, :], gst[:, plan.slot(name, "gst", c), :, :],
                                                  A5[:, 1:2, :].to_broadcast([P, MR, P]), ALU.mult
                                                  ).then_inc(S["own_prod"], 1)
                                seen(dve, name, "own_prod", j, c)
                                vec.tensor_reduce(own_m[:].rearrange("p h u -> p u h"),
                                                  junk[:, 0:MR, :].rearrange("p u (h e) -> p u h e", h=4), AX.X, ALU.add
                                                  ).then_inc(S["own_sc"], 1)
                                seen(dve, name, "own_sc", j, c)
                                vec.tensor_scalar(a_dst[:, :, bass.ds(MR * c + j * (MR * MR), MR)], own_m[:], 0.0,
                                                  None, ALU.add).then_inc(S["own_sum"], 1)
                groups(dve, EDGE_MACROS, body, name in FIRST)

            local(0)
            dense(0)
            combine(0)
            post(0)
            for i in (1, 2, 3):
                dense(i)
            for k in range(1, PHASES):
                local(k)
                combine(k)
                post(k)


_WEIGHTS = ["L0_gnn_W1", "L0_gnn_b1", "L0_gnn_W2", "L0_gnn_b2",
            "L1_gnn_W1", "L1_gnn_a1_src", "L1_gnn_a1_dst", "L1_gnn_b1",
            "L1_gnn_W2", "L1_gnn_a2_src", "L1_gnn_a2_dst", "L1_gnn_b2",
            "L2_gnn_W1", "L2_gnn_a1_src", "L2_gnn_a1_dst", "L2_gnn_b1",
            "L2_gnn_W2", "L2_gnn_a2_src", "L2_gnn_a2_dst", "L2_gnn_b2",
            "L3_gnn_W", "L3_gnn_att", "L3_gnn_bias"]


def kernel(**inputs):
    import numpy as _np
    import concourse.bacc as _bacc
    from concourse import mybir as _mybir
    from concourse.bass_utils import run_bass_kernel_spmd as _run

    nc = _bacc.Bacc("TRN2", target_bir_lowering=False, num_devices=1)
    arrays, aps = {}, {}
    for name in ["x", "src", "dst", "edge_attr_128"] + _WEIGHTS:
        a = _np.ascontiguousarray(inputs[name])
        arrays[f"in_{name}"] = a
        aps[name] = nc.dram_tensor(f"in_{name}", a.shape, _mybir.dt.from_np(a.dtype), kind="ExternalInput").ap()
    w = {name: aps[name] for name in _WEIGHTS}
    w["out"] = nc.dram_tensor("out_0", (NODES, D), F32, kind="ExternalOutput").ap()
    build(nc, aps["x"], aps["src"], aps["dst"], aps["edge_attr_128"], w)
    r = _run(nc, [arrays], core_ids=[0])
    return r.results[0]["out_0"]
```

```python
import concourse.bass as bass
from concourse import mybir
from contextlib import ExitStack

F32 = mybir.dt.float32
I32 = mybir.dt.int32
ALU = mybir.AluOpType
ACT = mybir.ActivationFunctionType
AX = mybir.AxisListType

P = 128
D = 128
NODES = 50000
EDGES = 25000
MR = 4
NODE_MACROS = -(-NODES // (P * MR))
NODE_ROWS = NODE_MACROS * P * MR
TILES = -(-EDGES // (P * MR)) * MR
EDGE_MACROS = TILES // MR
SLOTS = TILES * P
TB = TILES // 2
BIG = 1.0e30
SKIP = 1.0e6
EPS = 1e-5
SLOPE = 0.2

PHASES = 6
HEADS = [1, 1, 1, 1, 1, 4]
HW = [D, D + 1, D + 1, D + 1, D + 1, D // 4 + 1]
WID = [HEADS[k] * HW[k] for k in range(PHASES)]
ROW = 132
MLP_LAYER = {0: 0, 1: 1, 3: 2, 4: 3}
HALVES = [1, 2, 1, 0]
DENSE_LAYER = [0, 1, 2, 3]
XIN = 8


class Plan:

    def __init__(self):
        self.base, self.per, self.n, self.group = {}, {}, {}, {}
        self.last, self.before, self.stores = {}, {}, {}
        self.total = {}
        self.ring_size, self.ring_seq, self.ring_full, self.ring_k = {}, {}, {}, {}
        self.now_seq, self.now_full = {}, {}

    def loop(self, name, n, steps, rings, last, group=MR):
        self.group[name] = group
        self.before[name] = self.last
        self.stores[name] = {r: list(v) for r, v in self.now_full.items()}
        self.n[name] = n
        for step, k in steps:
            self.base[name, step] = self.total.get(step, 0)
            self.per[name, step] = k
            self.total[step] = self.total.get(step, 0) + n * k
        for ring, size, k in rings:
            self.ring_size[ring] = size
            seq = self.now_seq.get(ring, 0)
            full = self.now_full.get(ring, [0] * size)
            self.ring_seq[name, ring], self.ring_full[name, ring] = seq, list(full)
            self.ring_k[name, ring] = k
            for i in range(n):
                full[(seq + i) % size] += 16 * k
            self.now_seq[ring], self.now_full[ring] = seq + n, full
        self.last = {e: (s, self.total[s]) for e, s in last.items()}

    def seen(self, name, step, j, c, i=None, back=0):
        k = self.per[name, step]
        i = k - 1 if i is None else i
        return self.base[name, step] + k * c + i + 1 - k * back + j * (self.group[name] * k)

    def slot(self, name, ring, c):
        return (self.ring_seq[name, ring] + c) % self.ring_size[ring]

    def full(self, name, ring, j, c):
        size, k = self.ring_size[ring], self.ring_k[name, ring]
        s = self.slot(name, ring, c)
        first = (s - self.ring_seq[name, ring]) % size
        return self.ring_full[name, ring][s] + 16 * k * ((c - first) // size + 1) + j * (16 * k * (self.group[name] // size))

    def parity(self, name, step, c):
        return (self.base[name, step] + c) % 2


def make_plan():
    plan = Plan()

    def local(k):
        steps = [("sel_ready", 1), ("u_done", 2), ("u_out", 2), ("idx_up", 2 if k == 0 else 1)]
        rings = [("gat", 4, MR), ("dstb", 2, 1), ("ulo", 2, 1)]
        last = dict(pe="u_done", act="u_out", dve="sel_ready")
        if k == 0:
            steps += [("ea_added", 1)]
            rings += [("ea", 2, 1), ("own_in", 2, MR), ("own_out", 2, 1)]
        else:
            steps += [("sc", 1), ("esum", 1), ("e_ready", 1), ("eT", 1), ("scans", 1), ("mrow", 1),
                      ("mT", 1), ("d_ready", 1), ("w_ready", 1), ("m_kept", 1)]
            rings += [("pen", 2, HEADS[k])]
            if k == 5:
                steps += [("prod", 1)]
        plan.loop(f"L{k}", EDGE_MACROS, steps, rings, last)

    def mlp(layer):
        nh = HALVES[layer]
        return [("xT_ps", 1), ("xT", 1), ("y_ps", 1), ("y_used", 1)] + ([("h_ps", nh), ("hT", nh)] if nh else []) + ([("z", 1)] if layer == 0 else [])

    norm = [("res2", 1), ("stats", 1), ("aggr", 1), ("lnv", 1), ("rstd", 1), ("shift", 1), ("x_ready", 1)]

    def dense(i):
        steps = mlp(i) + norm
        rings = [("xin", XIN, 1), ("xst", 4, 1)]
        if i > 0:
            steps += [("res1", 1)] if i < 3 else []
            rings += [("gst", 4, 1)]
        plan.loop(f"D{i}", NODE_MACROS, steps, rings, dict(pe="y_ps", act="x_ready", dve="shift"), 2 * MR)

    def post(k):
        steps = [("p_ps", 2), ("p_used", 2)]
        slots = 4 if HEADS[k] == 1 else 2
        rings = [("uin", 4, 1), (f"car{slots}", slots, 2)]
        last = dict(pe="p_ps", dve="own_sum")
        if k < 5:
            rings += [("xs", 8, 1)]
        if k in (1, 2, 3, 4):
            steps += [("selfed", 1), ("rz", 1)]
        if k == 5:
            steps += [("zmax", 1), ("rz", 1)]
            last["dve"] = "shift"
        if k in (2, 4, 5):
            rings += [("xr", 4, 1)]
            steps += [("un", 1), ("res1", 1)]
        if k in (0, 1, 3):
            steps += [("u_ready", 1)]
        if k in MLP_LAYER:
            steps += mlp(MLP_LAYER[k])
            last.update(pe="y_ps", act="y_used" if k else "x_ready")
        if k in (0, 2, 4, 5):
            steps += norm
            if k != 4:
                last["act"] = "x_ready"
            if k < 5:
                rings += [("xst", 4, 1)]
            else:
                rings += [("out_sc", 4, MR)]
                steps += [("idx_up", 1)]
        if k in (1, 3, 4):
            rings += [("gst", 4, 1)]
        if k == 4:
            steps += [("own_prod", 1)]
        if k < 5:
            steps += [("own_sc", 1), ("own_sum", 1)]
        plan.loop(f"P{k}", EDGE_MACROS, steps, rings, last, 2 * MR)

    def combine(k):
        h = HEADS[k]
        steps = [("c_colb", 2 * h), ("c_row", 2 * h), ("c_mm", 2 * h), ("c_mb", 2 * h), ("c_dm", 2 * h),
                 ("c_wt", 2 * h), ("c_wtT_ps", 2 * h), ("c_wtT", 2 * h), ("c_sum_ps", 4 * h), ("c_sum", 4 * h),
                 ("c_mT", h + 1), ("c_arg", 2 * h), ("c_exp", 2 * h)]
        if k:
            steps += [("c_mT_ps", h + (k < 5)), ("c_t", 8 * h), ("c_back_ps", 2 * h), ("c_back", 2 * h)]
        plan.loop(f"C{k}", 1, steps, [("c_in", 1, 4), ("c_car", 1, 4), ("c_w0", 1, h), ("c_w1", 1, h)],
                  dict(pe="c_back_ps" if k else "c_sum_ps", act="c_exp", dve="c_back" if k else "c_arg"))

    local(0)
    dense(0)
    combine(0)
    post(0)
    for i in (1, 2, 3):
        dense(i)
    for k in range(1, PHASES):
        local(k)
        combine(k)
        post(k)
    return plan


def table_rows(table, first, count_per_partition):
    return table[bass.ds(first, P * MR), :].rearrange("(p u) d -> p u d", u=count_per_partition)


def edge_rows(table, first):
    return table[bass.ds(first, P * MR), :].rearrange("(u p) d -> p u d", p=P)


def wait(eng, semaphore, value):
    if isinstance(value, int) and value <= 0:
        return
    eng.wait_ge(semaphore, value)


def groups(eng, n, body, peel):
    whole = n // MR
    if peel:
        body(0, MR)
    with eng.Fori(1 if peel else 0, whole) as j:
        body(j, MR)
    if n % MR:
        body(whole, n % MR)


def pipeline(eng, plan, name, depth, slot):
    n, size = plan.n[name], plan.group[name]
    assert depth <= size

    def peeled(t):
        def at(lag):
            return [((t - lag) // size, (t - lag) % size)] if 0 <= t - lag < n else []
        slot(at)

    def looped(j, t):
        def at(lag):
            return [(j, t - lag)]
        slot(at)

    first = 2 if name in ("D0", "P0") else 1
    for t in range(first * size):
        peeled(t)
    with eng.Fori(first, n // size) as j:
        for t in range(size):
            looped(j, t)
    for t in range(n // size * size, n + depth):
        peeled(t)


def before(j, c, n):
    return isinstance(j, int) and j == 0 and c < n


FIRST = {"L0", "D0", "P0", "D1", "L1", "P1", "P2", "P4", "L5", "P5"}


def build(nc, x, src, dst, ea, w):
    plan = make_plan()
    out = w["out"]

    with ExitStack() as ctx:
        def sb(name, shape, dt=F32):
            return ctx.enter_context(nc.sbuf_tensor(name, shape, dt))

        def ps(name, shape):
            return ctx.enter_context(nc.psum_tensor(name, shape, F32))

        def sem(name):
            return ctx.enter_context(nc.semaphore(name))

        def dram(name, shape, dt=F32):
            return nc.dram_tensor(name, shape, dt, kind="Internal").ap()

        table = {n: dram(f"table_{n}", (NODE_ROWS + SLOTS, D)) for n in ("x1", "g2", "x2", "g3", "x3", "g5")}
        x0_own = dram("x0_own", (SLOTS, D))
        node_map = dram("node_map", (NODE_ROWS, 1), I32)
        dst_f = dram("dst_f", (TILES, P))
        pens = dram("pens", (TILES, 2, P))
        tile_sums = dram("tile_sums", (SLOTS, ROW))
        carry = dram("carry", (2, TILES, ROW))
        carry_w = dram("carry_w", (2, TILES, 4, P))
        GATHER_FROM = [x, table["x1"], table["g2"], table["x2"], table["g3"], table["g5"]]
        OWN_FROM = [x0_own] + [table[n][NODE_ROWS:NODE_ROWS + SLOTS, :] for n in ("x1", "g2", "x2", "g3")]
        RES_FROM = {k: table[n][NODE_ROWS:NODE_ROWS + SLOTS, :] for k, n in ((2, "x1"), (4, "x2"), (5, "x3"))}
        X_TO = {0: "x1", 2: "x2", 4: "x3"}
        G_TO = {1: "g2", 3: "g3", 4: "g5"}

        ident = sb("ident", [P, P])
        W1 = {0: sb("w1_0", [P, 1, P]), 1: sb("w1_1", [P, 2, P]), 2: sb("w1_2", [P, 1, P])}
        W2 = {0: sb("w2_0", [P, 1, P]), 1: sb("w2_1", [P, 2, P]), 2: sb("w2_2", [P, 1, P])}
        W3 = sb("w3", [P, P])
        B1 = sb("b1", [P, 4])
        BCOL = {0: 0, 1: 1, 2: 3}
        BB = sb("bb", [P, 4, 1, P])
        VB = sb("vb", [P, 8, P])
        A5 = sb("a5", [P, 2, P])
        src_i = sb("src_i", [P, TILES], I32)
        dstm_i = sb("dstm_i", [P, TILES], I32)
        scat_i = sb("scat_i", [P, TILES], I32)
        row_i = sb("row_i", [P, TILES], I32)
        src_row = sb("src_row", [P, TILES], I32)
        dcol = sb("dcol", [P, TILES])
        a_dst = sb("a_dst", [P, 4, TILES])
        e_self = sb("e_self", [P, TILES])
        m_loc = sb("m_loc", [P, 4, TILES])
        c_loc = sb("c_loc", [P, 4, TILES])
        c_self = sb("c_self", [P, TILES])
        seg = sb("seg", [TB, 2, 2, P])
        cross = sb("cross", [TB, 2, 2, TILES])
        mT = sb("mT", [TB, 5, 2, P])
        ends = sb("ends", [TB, 2, 2, ROW])
        csum = sb("csum", [TB, 2, 2, ROW])
        colb = sb("colb", [TB, 2, TB])
        mm = sb("mm", [TB, 2, TILES])
        mB = sb("mB", [TB, 2, 2, 4])
        wt = sb("wt", [TB, 2, TILES])
        wtT = sb("wtT", [TB, 2, 2, TB])
        tmax = sb("tmax", [TB, 3, P])
        arg = sb("arg", [TB, 4, P])
        coef = sb("coef", [TB, 2, 4, P])
        gat = sb("gat", [P, 4, MR, ROW])
        pen = sb("pen", [MR * 4, 2, 2, P])
        sel = sb("sel", [P, 2, MR, P])
        junk = sb("junk", [P, 2 * MR, P])
        sc = sb("sc", [P, 4, MR, 1])
        es = sb("es", [P, 4, MR, 1])
        eb = sb("eb", [P, 4, MR, 1])
        db = sb("db", [P, 4, MR, 1])
        wb = sb("wb", [P, 4, MR, 1])
        scan = sb("scan", [MR * 4, 2, P])
        mrow = sb("mrow", [MR * 4, P])
        ulo = sb("ulo", [P, 2, MR, ROW])
        xin = sb("xin", [P, XIN, MR, P])
        xT = sb("xT", [P, 2, MR * P])
        zb = sb("zb", [P, 2, MR * P])
        hT = sb("hT", [P, 2, 2, MR * P])
        gst = sb("gst", [P, 4, MR, P])
        rb = sb("rb", [P, 4, MR, P])
        st = sb("st", [P, 4, MR, 6])
        eps_c = sb("eps_c", [P, 1])
        mv = sb("mv", [P, 4, MR, 2])
        lnv = sb("lnv", [P, 4, MR])
        rstd = sb("rstd", [P, 4, MR, 1])
        neg_mean = sb("neg_mean", [P, 4, MR, 1])
        xst = sb("xst", [P, 4, MR, P])
        uin = sb("uin", [P, 4, MR, ROW])
        xs = sb("xs", [P, 8, MR, ROW])
        xr = sb("xr", [P, 4, MR, P])
        car_w = sb("car_w", [2, 2 * MR * 4 * P])
        car = sb("car", [2, 4, MR, ROW])
        t1 = sb("t1", [P, 2, MR, ROW])
        own_in, eab, dstb, gw = uin[:, 0:2, :, 0:P], xr[:, 0:2], xr[:, 2:4], t1

        def car_ring(k):
            slots = 4 if HEADS[k] == 1 else 2
            return f"car{slots}", car_w[:, 0:slots * MR * HEADS[k] * P].rearrange(
                "d (s u h i) -> d s u h i", s=slots, u=MR, h=HEADS[k])
        rz = sb("rz", [P, MR, 4, 1])
        own_s = sb("own_s", [P, 2, MR])
        own_m = sb("own_m", [P, 4, MR])
        idx_st = sb("idx_st", [P, 4, MR], I32)
        idx_st2 = sb("idx_st2", [P, 2, MR], I32)
        map_ix = sb("map_ix", [P, 16], I32)
        map_v = sb("map_v", [P, 16], I32)
        pi = sb("pi", [TB, 3, 2, P], I32)
        pf = sb("pf", [TB, 4, 2, P])
        peq = xin[0:TB, 3].rearrange("t (a b) i -> t a b i", a=2)
        ppen = xin[0:TB, 4].rearrange("t (a b) i -> t a b i", a=2)
        w1T = xin[:, 0, 0:3, :]
        acol = sb("acol", [P, 6, 1])
        ab = xin[:, 1:3, :, :].rearrange("p s u d -> p (s u) d")[:, 0:6, :]
        ti_i = sb("ti_i", [TB, TILES], I32)
        tc_i = sb("tc_i", [TB, 1], I32)
        id_i = sb("id_i", [P, P], I32)
        map_i = sb("map_i", [P, NODE_ROWS // P], I32)
        ti = sb("ti", [TB, TILES])
        tcf = sb("tcf", [TB, 2])
        id_f = xin[:, 5, 0, :]

        psT = [ps(f"psT{i}", [P, 512]) for i in range(2)]
        psH = [ps(f"psH{i}", [P, 512]) for i in range(2)]
        psU = [ps(f"psU{i}", [P, 512]) for i in range(2)]
        psS, psY1 = ps("psS", [P, 512]), ps("psY1", [P, 512])
        psY = [psS, psY1]

        names = sorted({s for _, s in plan.base})
        S = {n: sem(n) for n in names}
        R = {r: [sem(f"{r}_full{i}") for i in range(size)] for r, size in plan.ring_size.items()}
        pre_fill, pre_load, w_load, pre_f, pre_v = map(sem, ("pre_fill", "pre_load", "w_load", "pre_f", "pre_v"))
        pre_ps, pre_tab, pre_st, pre_iota = map(sem, ("pre_ps", "pre_tab", "pre_st", "pre_iota"))
        pre_done, map_init, map_idx, map_dma = map(sem, ("pre_done", "map_init", "map_idx", "map_dma"))
        pre_pe = sem("pre_pe")
        map_read = sem("map_read")
        turn = {e: sem(f"turn_{e}") for e in ("pe", "act", "dve", "pool", "sp")}

        def enter(eng, name):
            for step, value in plan.before[name].values():
                wait(eng, S[step], value)

        def stored(eng, name, rings):
            for ring in rings:
                for i, value in enumerate(plan.stores[name].get(ring, [])):
                    wait(eng, R[ring][i], value)

        def own(eng, e):
            eng.sem_inc(turn[e], 1)

        def left(eng, name, ring, j, c):
            k = plan.ring_k[name, ring]
            wait(eng, R[ring][plan.slot(name, ring, c)], plan.full(name, ring, j, c) - 16 * k)

        b1s = (w["L0_gnn_b1"], w["L1_gnn_b1"][0:P], w["L1_gnn_b1"][P:2 * P], w["L2_gnn_b1"])
        a1s = (w["L1_gnn_a1_src"][0:P], w["L1_gnn_a1_src"][P:2 * P], w["L1_gnn_a1_dst"][0:P],
               w["L1_gnn_a1_dst"][P:2 * P], w["L2_gnn_a1_src"], w["L2_gnn_a1_dst"])
        att = w["L3_gnn_att"]
        weight_loads = [
            (W1[0][:, 0, :], w["L0_gnn_W1"]), (W2[0][:, 0, :], w["L0_gnn_W2"]),
            (W1[1][:].rearrange("p a d -> p (a d)"), w["L1_gnn_W1"]),
            (W2[1][:], w["L1_gnn_W2"].rearrange("(a p) d -> p a d", p=P)),
            (W1[2][:, 0, :], w["L2_gnn_W1"]), (W2[2][:, 0, :], w["L2_gnn_W2"]), (W3[:], w["L3_gnn_W"]),
        ]
        weight_loads += [(B1[:, i:i + 1], b.rearrange("(p o) -> p o", o=1)) for i, b in enumerate(b1s)]
        weight_loads += [(acol[:, i, :], a.rearrange("(p o) -> p o", o=1)) for i, a in enumerate(a1s)]
        weight_loads += [(BB[:, i, 0, :], w[n].rearrange("(o d) -> o d", o=1).to_broadcast([P, P]))
                         for i, n in enumerate(("L0_gnn_b2", "L1_gnn_b2", "L2_gnn_b2", "L3_gnn_bias"))]
        weight_loads += [(VB[:, i, :], w[n].rearrange("(o d) -> o d", o=1).to_broadcast([P, P]))
                         for i, n in ((2, "L1_gnn_a2_src"), (3, "L1_gnn_a2_dst"), (6, "L2_gnn_a2_src"),
                                      (7, "L2_gnn_a2_dst"))]
        weight_loads += [(A5[:, s, 32 * h:32 * h + 32], att[h:h + 1, 32 * s:32 * s + 32].to_broadcast([P, 32]))
                         for s in range(2) for h in range(4)]

        TAIL = EDGES - (TILES - 1) * P
        index_loads = []
        for i, (a, shift) in enumerate(((dst, 0), (dst, 1), (src, 0))):
            index_loads += [
                (pi[:, i, 0, :], a[shift:shift + TB * P].rearrange("(t i) -> t i", i=P)),
                (pi[0:TB - 1, i, 1, :], a[TB * P + shift:(TILES - 1) * P + shift].rearrange("(t i) -> t i", i=P)),
                (pi[TB - 1:TB, i, 1, 0:TAIL - shift],
                 a[(TILES - 1) * P + shift:EDGES].rearrange("(t i) -> t i", t=1)),
            ]

        block = ctx.enter_context(nc.Block())

        @block.sync
        def _(sp):
            for to, a in weight_loads:
                sp.dma_start(to, a, allow_slow_non_contiguous=True).then_inc(w_load, 16)
            sp.wait_ge(pre_fill, 3)
            for to, a in index_loads:
                sp.dma_start(to, a).then_inc(pre_load, 16)
            sp.wait_ge(pre_tab, 1)
            for b in range(2):
                sp.dma_start(dst_f[TB * b:TB * b + TB, :], pf[:, 0, b, :]).then_inc(pre_st, 16)
                sp.dma_start(pens[TB * b:TB * b + TB, :, :], ppen[:, b, :, :]).then_inc(pre_st, 16)
            sp.wait_ge(pre_st, 64)

            def first_row(name, j, c, start=0):
                return start + P * MR * c + j * (P * MR * plan.group[name])

            def local(k):
                name = f"L{k}"
                enter(sp, name)
                rings = ("ulo", "own_out") if k == 0 else ("ulo",)

                def load(j, c):
                    early = isinstance(j, int) and j == 0 and c < 2
                    if not early:
                        sp.wait_ge(S["sel_ready"], plan.seen(name, "sel_ready", j, c, back=2))
                        own(sp, "sp")
                    t = MR * c + j * (MR * MR)
                    s = plan.slot(name, "dstb", c)
                    sp.dma_start(dstb[:, s, :, :],
                                 dst_f[bass.ds(t, MR), :].rearrange("(o t) i -> o t i", o=1)
                                 .to_broadcast([P, MR, P])).then_inc(R["dstb"][s], 16)
                    if k == 0:
                        s = plan.slot(name, "ea", c)
                        if isinstance(j, int) and MR * j + c == EDGE_MACROS - 1:
                            whole = (EDGES - (EDGE_MACROS - 1) * MR * P) // P
                            r0 = (EDGE_MACROS - 1) * MR * P
                            assert whole == MR - 1
                            sp.dma_start(eab[:, s, 0:whole, :],
                                         ea[r0:r0 + whole * P, :].rearrange("(u p) d -> p u d", p=P)
                                         ).then_inc(R["ea"][s], 16)
                            sp.dma_start(eab[0:TAIL, s, whole, :], ea[r0 + whole * P:EDGES, :]
                                         ).then_inc(R["ea"][s], 16)
                        else:
                            sp.dma_start(eab[:, s, :, :], edge_rows(ea, first_row(name, j, c))
                                         ).then_inc(R["ea"][s], 16)
                    else:
                        if not early:
                            sp.wait_ge(S["scans"], plan.seen(name, "scans", j, c, back=2))
                            own(sp, "sp")
                        s = plan.slot(name, "pen", c)
                        for h in range(HEADS[k]):
                            sp.dma_start(pen[MR * h:MR * h + MR, s, :, :], pens[bass.ds(t, MR), :, :]
                                         ).then_inc(R["pen"][s], 16)

                def store(j, c):
                    sp.wait_ge(S["u_out"], plan.seen(name, "u_out", j, c))
                    own(sp, "sp")
                    s = plan.slot(name, "ulo", c)
                    sp.dma_start(edge_rows(tile_sums, first_row(name, j, c)), ulo[:, s, :, :]).then_inc(R["ulo"][s], 16)
                    if k == 0:
                        sp.wait_ge(R["own_in"][plan.slot(name, "own_in", c)], plan.full(name, "own_in", j, c))
                        own(sp, "sp")
                        s = plan.slot(name, "own_out", c)
                        sp.dma_start(edge_rows(x0_own, first_row(name, j, c)), own_in[:, s, :, :]
                                     ).then_inc(R["own_out"][s], 16)
                def slot(at):
                    for j, c in at(0):
                        load(j, c)
                    for j, c in at(2):
                        store(j, c)
                pipeline(sp, plan, name, 2, slot)

            def dense(i):
                name = f"D{i}"
                enter(sp, name)
                stored(sp, name, ("xst", "gst"))
                source = (x, table["x1"], table["x2"], table["x3"])[i]
                x_to = (table["x1"], table["x2"], table["x3"], out)[i]
                g_to = (None, table["g2"], table["g3"], table["g5"])[i]
                last_parts = (NODES - (NODE_MACROS - 1) * P * MR) // MR

                def load(j, c):
                    if not before(j, c, XIN):
                        sp.wait_ge(S["y_used" if i == 0 else "res2" if i == 3 else "res1"],
                                   plan.seen(name, "y_used" if i == 0 else "res2" if i == 3 else "res1", j, c, back=XIN))
                        own(sp, "sp")
                        sp.wait_ge(S["xT_ps"], plan.seen(name, "xT_ps", j, c, back=XIN))
                        own(sp, "sp")
                    s = plan.slot(name, "xin", c)
                    if i == 0 and isinstance(j, int) and 2 * MR * j + c == NODE_MACROS - 1:
                        sp.dma_start(xin[0:last_parts, s, :, :],
                                     x[NODES - last_parts * MR:NODES, :].rearrange("(p u) d -> p u d", u=MR)
                                     ).then_inc(R["xin"][s], 16)
                    else:
                        sp.dma_start(xin[:, s, :, :], table_rows(source, first_row(name, j, c), MR)
                                     ).then_inc(R["xin"][s], 16)

                def store_g(j, c):
                    sp.wait_ge(S["y_used"], plan.seen(name, "y_used", j, c))
                    own(sp, "sp")
                    s = plan.slot(name, "gst", c)
                    sp.dma_start(table_rows(g_to, first_row(name, j, c), MR), gst[:, s, :, :]
                                 ).then_inc(R["gst"][s], 16)

                def store_x(j, c):
                    sp.wait_ge(S["x_ready"], plan.seen(name, "x_ready", j, c))
                    own(sp, "sp")
                    s = plan.slot(name, "xst", c)
                    if i == 3 and isinstance(j, int) and 2 * MR * j + c == NODE_MACROS - 1:
                        sp.dma_start(out[NODES - last_parts * MR:NODES, :].rearrange("(p u) d -> p u d", u=MR),
                                     xst[0:last_parts, s, :, :]).then_inc(R["xst"][s], 16)
                    else:
                        sp.dma_start(table_rows(x_to, first_row(name, j, c), MR), xst[:, s, :, :]
                                     ).then_inc(R["xst"][s], 16)
                def slot(at):
                    for j, c in at(0):
                        load(j, c)
                    if i:
                        for j, c in at(5):
                            store_g(j, c)
                    for j, c in at(7):
                        store_x(j, c)
                pipeline(sp, plan, name, 7, slot)

            def combine(k):
                name = f"C{k}"
                enter(sp, name)
                stored(sp, name, ("ulo", "own_out") if k == 0 else ("ulo",))
                sums = tile_sums.rearrange("(t p) w -> t p w", p=P)
                for d in range(2):
                    for b in range(2):
                        row = P - 1 if d == 0 else 0
                        sp.dma_start(ends[:, d, b, :], sums[TB * b:TB * b + TB, row, :]).then_inc(R["c_in"][0], 16)
                for d in range(2):
                    sp.wait_ge(S["c_sum"], plan.seen(name, "c_sum", 0, 0, 4 * HEADS[k] - 1))
                    for b in range(2):
                        sp.dma_start(carry[d, TB * b:TB * b + TB, :], csum[:, d, b, :]).then_inc(R["c_car"][0], 16)
                for h in range(HEADS[k]):
                    for b in range(2):
                        r = 2 * h + b
                        sp.wait_ge(S["c_exp"], plan.seen(name, "c_exp", 0, 0, r))
                        sp.dma_start(carry_w[:, TB * b:TB * b + TB, h, :].rearrange("d t i -> t d i"),
                                     coef[:, r % 2, 1:3, :]).then_inc(R[f"c_w{r % 2}"][0], 16)

            def post(k):
                name = f"P{k}"
                enter(sp, name)
                stored(sp, name, ("xst", "gst"))
                stored(sp, name, ("c_car", "c_w0", "c_w1"))

                def load(j, c):
                    if not before(j, c, 4):
                        sp.wait_ge(S["p_used"], plan.seen(name, "p_used", j, c, back=4))
                        own(sp, "sp")
                    s = plan.slot(name, "uin", c)
                    sp.dma_start(uin[:, s, :, :], edge_rows(tile_sums, first_row(name, j, c))).then_inc(R["uin"][s], 16)
                    if k < 5:
                        if not before(j, c, 8):
                            sp.wait_ge(S["y_used" if k == 0 else "selfed"],
                                       plan.seen(name, "y_used" if k == 0 else "selfed", j, c, back=8))
                            own(sp, "sp")
                        s = plan.slot(name, "xs", c)
                        sp.dma_start(xs[:, s, :, 0:P], edge_rows(OWN_FROM[k], first_row(name, j, c))
                                     ).then_inc(R["xs"][s], 16)
                    if k in RES_FROM:
                        if not before(j, c, 4):
                            sp.wait_ge(S["res1"], plan.seen(name, "res1", j, c, back=4))
                            own(sp, "sp")
                        s = plan.slot(name, "xr", c)
                        sp.dma_start(xr[:, s, :, :], edge_rows(RES_FROM[k], first_row(name, j, c))
                                     ).then_inc(R["xr"][s], 16)

                def load_carries(j, c):
                    ring, weights = car_ring(k)
                    slots = plan.ring_size[ring]
                    if not before(j, c, slots):
                        sp.wait_ge(S["p_used"], plan.seen(name, "p_used", j, c, back=slots))
                        own(sp, "sp")
                    t = MR * c + j * (MR * plan.group[name])
                    s = plan.slot(name, ring, c)
                    sp.dma_start(weights[:, s, :, :, :], carry_w[:, bass.ds(t, MR), 0:HEADS[k], :]
                                 ).then_inc(R[ring][s], 16)
                    sp.dma_start(car[:, s, :, :], carry[:, bass.ds(t, MR), :]).then_inc(R[ring][s], 16)

                def store_x(j, c):
                    sp.wait_ge(S["x_ready"], plan.seen(name, "x_ready", j, c))
                    own(sp, "sp")
                    s = plan.slot(name, "xst", c)
                    sp.dma_start(edge_rows(table[X_TO[k]], first_row(name, j, c, NODE_ROWS)), xst[:, s, :, :]
                                 ).then_inc(R["xst"][s], 16)

                def store_g(j, c):
                    sp.wait_ge(S["y_used"], plan.seen(name, "y_used", j, c))
                    own(sp, "sp")
                    s = plan.slot(name, "gst", c)
                    sp.dma_start(edge_rows(table[G_TO[k]], first_row(name, j, c, NODE_ROWS)), gst[:, s, :, :]
                                 ).then_inc(R["gst"][s], 16)

                x_lag, g_lag = {0: 8, 2: 6, 4: 6}.get(k), {1: 6, 3: 6, 4: 8}.get(k)

                def slot(at):
                    for j, c in at(0):
                        load(j, c)
                        load_carries(j, c)
                    if k in X_TO:
                        for j, c in at(x_lag):
                            store_x(j, c)
                    if k in G_TO:
                        for j, c in at(g_lag):
                            store_g(j, c)
                pipeline(sp, plan, name, max(x_lag or 0, g_lag or 0), slot)

            local(0)
            dense(0)
            combine(0)
            post(0)
            for i in (1, 2, 3):
                dense(i)
            for k in range(1, PHASES):
                local(k)
                combine(k)
                post(k)
            for slots in (R["xst"], R["gst"], R["ulo"], R["own_out"], R["out_sc"]):
                for i, q in enumerate(slots):
                    ring = next(r for r in R if R[r] is slots)
                    wait(sp, q, plan.now_full[ring][i])

        @block.gpsimd
        def _(pool):
            nc.gpsimd.iota(id_i[:], pattern=[[1, P]], base=0, channel_multiplier=-1).then_inc(pre_iota, 1)
            nc.gpsimd.iota(ti_i[:], pattern=[[1, TILES]], base=0, channel_multiplier=0).then_inc(pre_iota, 1)
            nc.gpsimd.iota(tc_i[:], pattern=[[1, 1]], base=0, channel_multiplier=1).then_inc(pre_iota, 1)
            nc.gpsimd.iota(row_i[:], pattern=[[P, TILES]], base=NODE_ROWS, channel_multiplier=1).then_inc(pre_iota, 1)
            nc.gpsimd.iota(map_i[:], pattern=[[1, NODE_ROWS // P]], base=0, channel_multiplier=NODE_ROWS // P
                           ).then_inc(pre_iota, 1)
            pool.wait_ge(pre_iota, 5)
            pool.dma_start(node_map.rearrange("(p n) o -> p (n o)", p=P), map_i[:]).then_inc(map_init, 16)
            pool.wait_ge(pre_done, 1)

            def gathers(k):
                name = f"L{k}"
                index = src_i if k == 0 else src_row
                if k:
                    stored(pool, name, ("xst", "gst"))
                    own(pool, "pool")

                def body(j, cs):
                    for c in range(cs):
                        cols = bass.ds(MR * c + j * (MR * MR), MR)
                        s = plan.slot(name, "gat", c)
                        if not before(j, c, 4):
                            pool.wait_ge(S["u_done"], plan.seen(name, "u_done", j, c, back=4))
                        if k == 0:
                            left(pool, name, "own_out", j, c)
                        own(pool, "pool")
                        nc.gpsimd.tensor_copy(idx_st[:, s, :], index[:, cols]).then_inc(S["idx_up"], 1)
                        if k == 0:
                            s2 = plan.slot(name, "own_in", c)
                            nc.gpsimd.tensor_copy(idx_st2[:, s2, :], dstm_i[:, cols]).then_inc(S["idx_up"], 1)
                        pool.wait_ge(S["idx_up"], plan.seen(name, "idx_up", j, c))
                        own(pool, "pool")
                        for u in range(MR):
                            nc.gpsimd.indirect_dma_start(
                                out=gat[:, s, u, 0:P], out_offset=None, in_=GATHER_FROM[k],
                                in_offset=bass.IndirectOffsetOnAxis(ap=idx_st[:, s, u:u + 1], axis=0)
                            ).then_inc(R["gat"][s], 16)
                        if k == 0:
                            for u in range(MR):
                                nc.gpsimd.indirect_dma_start(
                                    out=own_in[:, s2, u, :], out_offset=None, in_=x,
                                    in_offset=bass.IndirectOffsetOnAxis(ap=idx_st2[:, s2, u:u + 1], axis=0)
                                ).then_inc(R["own_in"][s2], 16)
                groups(pool, EDGE_MACROS, body, name in FIRST)

            def scatter_out():
                name = "P5"

                def scatter(j, c):
                    s = plan.slot(name, "out_sc", c)
                    pool.wait_ge(S["x_ready"], plan.seen(name, "x_ready", j, c))
                    left(pool, name, "out_sc", j, c)
                    own(pool, "pool")
                    nc.gpsimd.tensor_copy(idx_st[:, s, :], scat_i[:, bass.ds(MR * c + j * (MR * plan.group[name]), MR)]
                                          ).then_inc(S["idx_up"], 1)
                    pool.wait_ge(S["idx_up"], plan.seen(name, "idx_up", j, c))
                    own(pool, "pool")
                    for u in range(MR):
                        nc.gpsimd.indirect_dma_start(
                            out=out, out_offset=bass.IndirectOffsetOnAxis(ap=idx_st[:, s, u:u + 1], axis=0),
                            in_=xst[:, s, u, :], in_offset=None, bounds_check=NODES - 1, oob_is_err=False
                        ).then_inc(R["out_sc"][s], 16)
                
                def slot(at):
                    for j, c in at(0):
                        scatter(j, c)
                pipeline(pool, plan, name, 0, slot)

            def map_round(scatter, start, n, done):
                cols = bass.ds(start, n)
                index = scat_i if scatter else src_i
                nc.gpsimd.tensor_copy(map_ix[:, 0:n], index[:, cols]).then_inc(map_idx, 1)
                if scatter:
                    nc.gpsimd.tensor_copy(map_v[:, 0:n], row_i[:, cols]).then_inc(map_idx, 1)
                k = 2 if scatter else 1
                pool.wait_ge(map_idx, done * k + (0 if scatter else 2 * ROUNDS) + k)
                own(pool, "pool")
                for u in range(n):
                    off = bass.IndirectOffsetOnAxis(ap=map_ix[:, u:u + 1], axis=0)
                    if scatter:
                        nc.gpsimd.indirect_dma_start(out=node_map, out_offset=off, in_=map_v[:, u:u + 1],
                                                     in_offset=None, bounds_check=NODE_ROWS - 1, oob_is_err=False
                                                     ).then_inc(map_dma, 16)
                    else:
                        nc.gpsimd.indirect_dma_start(out=map_v[:, u:u + 1], out_offset=None, in_=node_map,
                                                     in_offset=off).then_inc(map_dma, 16)
                pool.wait_ge(map_dma, done * (256) + 16 * n + (0 if scatter else 16 * TILES))
                own(pool, "pool")
                if not scatter:
                    nc.gpsimd.tensor_copy(src_row[:, cols], map_v[:, 0:n]).then_inc(map_read, 1)

            ROUNDS = TILES // 16 + 1
            gathers(0)
            pool.wait_ge(map_init, 16)
            for scatter in (True, False):
                with pool.Fori(0, ROUNDS - 1) as r:
                    map_round(scatter, r * 16, 16, r)
                map_round(scatter, (ROUNDS - 1) * 16, TILES - 16 * (ROUNDS - 1), ROUNDS - 1)
            pool.wait_ge(map_read, ROUNDS)
            for k in range(1, PHASES):
                gathers(k)
            stored(pool, "P5", ("xst",))
            scatter_out()

        @block.tensor
        def _(pe):
            pe.wait_ge(pre_v, 1)
            pe.wait_ge(w_load, 16 * len(weight_loads))
            for i in range(2):
                nc.tensor.transpose(psH[0][:, P * i:P * i + P], W1[1][:, i, :], ident[:])
            nc.tensor.transpose(psH[0][:, 2 * P:3 * P], W1[2][:, 0, :], ident[:]).then_inc(pre_ps, 1)
            pe.wait_ge(pre_v, 2)
            for i in range(4):
                o = psH[1][:, P * i:P * i + P]
                if i < 2:
                    nc.tensor.matmul(o, ab[:, 2 * i, :], w1T[:, 0, :], start=True, stop=False)
                    last = nc.tensor.matmul(o, ab[:, 2 * i + 1, :], w1T[:, 1, :], start=False, stop=True)
                else:
                    last = nc.tensor.matmul(o, ab[:, 2 + i, :], w1T[:, 2, :], start=True, stop=True)
            last.then_inc(pre_ps, 1)
            pe.wait_ge(pre_v, 3)
            for i in range(4):
                for b in range(2):
                    last = nc.tensor.transpose(psT[i // 2][:, TILES * (i % 2) + TB * b:TILES * (i % 2) + TB * b + TB],
                                               pf[:, i, b, :], ident[0:TB, 0:TB])
            last.then_inc(pre_ps, 1)
            for d in range(2):
                pe.wait_ge(pre_v, 4 + d)
                for b in range(2):
                    last = nc.tensor.matmul(psY[d][0:TB, TB * b:TB * b + TB], colb[:, b, :],
                                            ident[0:TB, 0:TB], start=True, stop=True)
                last.then_inc(pre_ps, 1)
            pe.wait_ge(pre_done, 1)

            def local(k):
                name = f"L{k}"
                H, hw, wid = HEADS[k], HW[k], WID[k]
                enter(pe, name)

                def body(j, cs):
                    for c in range(cs):
                        s2 = c % 2
                        if k:
                            pe.wait_ge(S["e_ready"], plan.seen(name, "e_ready", j, c))
                            own(pe, "pe")
                            nc.tensor.transpose(psS[0:MR * H, 0:P], eb[:, 0:H, :, 0].rearrange("p h u -> p (h u)"),
                                                ident[:]).then_inc(S["eT"], 1)
                            pe.wait_ge(S["mrow"], plan.seen(name, "mrow", j, c))
                            own(pe, "pe")
                            nc.tensor.transpose(psS[:, P:P + MR * H], mrow[0:MR * H, :],
                                                ident[0:MR * H, 0:MR * H]).then_inc(S["mT"], 1)
                        pe.wait_ge(S["sel_ready"], plan.seen(name, "sel_ready", j, c))
                        g = plan.slot(name, "gat", c)
                        for q in range(2):
                            if not (isinstance(j, int) and j == 0 and c == 0):
                                pe.wait_ge(S["u_out"], plan.seen(name, "u_out", j, c, i=q, back=1))
                            for i in range(2):
                                u = 2 * q + i
                                rhs = gw[:, s2, u, 0:wid] if k == 5 else gat[:, g, u, 0:wid]
                                last = nc.tensor.matmul(psU[q][:, ROW * i:ROW * i + wid], sel[:, s2, u, :], rhs,
                                                        start=True, stop=True)
                            last.then_inc(S["u_done"], 1)
                groups(pe, EDGE_MACROS, body, name in FIRST)

            def mlp(name, layer, source):
                nh = HALVES[layer]

                def turn_rows(j, c):
                    s = plan.parity(name, "xT_ps", c)
                    if name[0] == "D":
                        pe.wait_ge(R["xin"][plan.slot(name, "xin", c)], plan.full(name, "xin", j, c))
                    elif name == "P4":
                        pe.wait_ge(S["x_ready"], plan.seen(name, "x_ready", j, c))
                    else:
                        pe.wait_ge(S["u_ready"], plan.seen(name, "u_ready", j, c))
                    if not before(j, c, 2):
                        pe.wait_ge(S["xT"], plan.seen(name, "xT", j, c, back=2))
                    for u in range(MR):
                        last = nc.tensor.transpose(psT[s][:, P * u:P * u + P], source(c, u), ident[:])
                    last.then_inc(S["xT_ps"], 1)

                def hidden(j, c):
                    s = plan.parity(name, "xT_ps", c)
                    pe.wait_ge(S["xT"], plan.seen(name, "xT", j, c))
                    for half in range(nh):
                        off = nh * c + half
                        if not before(j, off, 2):
                            pe.wait_ge(S["hT"], plan.base[name, "hT"] + off - 1 + j * (nh * plan.group[name]))
                        nc.tensor.matmul(psH[(plan.base[name, "h_ps"] + off) % 2][:], W1[layer][:, half, :],
                                         xT[:, s, :], start=True, stop=True).then_inc(S["h_ps"], 1)

                def second(j, c):
                    s = plan.parity(name, "xT_ps", c)
                    y = psY[plan.parity(name, "y_ps", c)]
                    pe.wait_ge(S["hT" if nh else "xT"], plan.seen(name, "hT" if nh else "xT", j, c))
                    if not before(j, c, 2):
                        pe.wait_ge(S["y_used"], plan.seen(name, "y_used", j, c, back=2))
                    for u in range(MR):
                        cols = slice(P * u, P * u + P)
                        if nh:
                            for half in range(nh):
                                last = nc.tensor.matmul(y[:, cols], hT[:, s, half, cols], W2[layer][:, half, :],
                                                        start=half == 0, stop=half == nh - 1)
                        else:
                            last = nc.tensor.matmul(y[:, cols], xT[:, s, cols], W3[:], start=True, stop=True)
                    last.then_inc(S["y_ps"], 1)

                return turn_rows, hidden, second

            def dense(i):
                name = f"D{i}"
                enter(pe, name)
                turn_rows, hidden, second = mlp(name, i, lambda c, u: xin[:, plan.slot(name, "xin", c), u, :])

                def slot(at):
                    for j, c in at(0):
                        turn_rows(j, c)
                    if i < 3:
                        for j, c in at(1):
                            hidden(j, c)
                    for j, c in at(2 if i < 3 else 1):
                        second(j, c)
                pipeline(pe, plan, name, 2 if i < 3 else 1, slot)

            def combine(k):
                name = f"C{k}"
                H, hw = HEADS[k], HW[k]
                enter(pe, name)
                if k:
                    for h in list(range(H)) + ([4] if k < 5 else []):
                        r = h if h < 4 else H
                        if r >= 2:
                            pe.wait_ge(S["c_mT"], plan.seen(name, "c_mT", 0, 0, r - 2))
                        for b in range(2):
                            a = e_self[:, TB * b:TB * b + TB] if h == 4 else m_loc[:, h, TB * b:TB * b + TB]
                            last = nc.tensor.transpose(psT[r % 2][0:TB, P * b:P * b + P], a, ident[:])
                        last.then_inc(S["c_mT_ps"], 1)
                pe.wait_ge(R["c_in"][0], plan.full(name, "c_in", 0, 0))
                for r in range(2 * H):
                    h, d = r // 2, r % 2
                    pe.wait_ge(S["c_colb"], plan.seen(name, "c_colb", 0, 0, r))
                    for b in range(2):
                        last = nc.tensor.matmul(psS[0:TB, TB * b:TB * b + TB], colb[:, b, :], ident[0:TB, 0:TB],
                                                start=True, stop=True)
                    last.then_inc(S["c_row"], 1)
                    pe.wait_ge(S["c_wt"], plan.seen(name, "c_wt", 0, 0, r))
                    for bt in range(2):
                        for b in range(2):
                            last = nc.tensor.transpose(psT[bt][0:TB, TB * b:TB * b + TB], wt[:, bt, TB * b:TB * b + TB],
                                                       ident[0:TB, 0:TB])
                    last.then_inc(S["c_wtT_ps"], 1)
                    pe.wait_ge(S["c_wtT"], plan.seen(name, "c_wtT", 0, 0, r))
                    for bt in range(2):
                        if r:
                            pe.wait_ge(S["c_sum"], plan.seen(name, "c_sum", 0, 0, 2 * (r - 1) + bt))
                        o = psH[bt][0:TB, 0:hw]
                        for b in range(2):
                            last = nc.tensor.matmul(o, wtT[:, bt, b, :], ends[:, d, b, hw * h:hw * h + hw],
                                                    start=b == 0, stop=b == 1)
                        last.then_inc(S["c_sum_ps"], 1)
                if k:
                    for r in range(2 * H):
                        pe.wait_ge(S["c_exp"], plan.seen(name, "c_exp", 0, 0, r))
                        if r >= 2:
                            pe.wait_ge(S["c_back"], plan.seen(name, "c_back", 0, 0, r - 2))
                        last = nc.tensor.transpose(psT[r % 2][:, 0:TB], coef[:, r % 2, 0, :], ident[0:TB, 0:TB])
                        if k < 5:
                            last = nc.tensor.transpose(psT[r % 2][:, P:P + TB], coef[:, r % 2, 3, :],
                                                       ident[0:TB, 0:TB])
                        last.then_inc(S["c_back_ps"], 1)

            def post(k):
                name = f"P{k}"
                H, hw, wid = HEADS[k], HW[k], WID[k]
                enter(pe, name)

                def carries(j, c):
                    ring, weights = car_ring(k)
                    pe.wait_ge(R[ring][plan.slot(name, ring, c)], plan.full(name, ring, j, c))
                    s = plan.slot(name, ring, c)
                    for q in range(2):
                        if not before(j, c, 1):
                            pe.wait_ge(S["p_used"], plan.seen(name, "p_used", j, c, i=q, back=1))
                        own(pe, "pe")
                        for i in range(2):
                            u = 2 * q + i
                            for h in range(H):
                                last = nc.tensor.matmul(
                                    psU[q][:, ROW * i + hw * h:ROW * i + hw * h + hw], weights[:, s, u, h, :],
                                    car[:, s, u, hw * h:hw * h + hw], start=True, stop=True)
                        last.then_inc(S["p_ps"], 1)

                if k in (0, 1, 3):
                    turn_rows, hidden, second = mlp(name, MLP_LAYER[k], lambda c, u: xin[:, c % 4, u, :])
                if k == 4:
                    turn_rows, hidden, second = mlp(name, 3, lambda c, u: xst[:, plan.slot(name, "xst", c), u, :])

                def slot(at):
                    for j, c in at(0):
                        carries(j, c)
                    if k in (0, 1, 3):
                        for j, c in at(1):
                            turn_rows(j, c)
                        for j, c in at(2):
                            hidden(j, c)
                        for j, c in at(3):
                            second(j, c)
                    if k == 4:
                        for j, c in at(4):
                            turn_rows(j, c)
                        for j, c in at(5):
                            second(j, c)
                pipeline(pe, plan, name, {0: 3, 1: 3, 3: 3, 4: 5}.get(k, 0), slot)

            local(0)
            dense(0)
            combine(0)
            post(0)
            for i in (1, 2, 3):
                dense(i)
            for k in range(1, PHASES):
                local(k)
                combine(k)
                post(k)

        @block.scalar
        def _(act):
            nc.scalar.preload_act_table_set("natural_log_exp_and_others")
            act.wait_ge(w_load, 16 * len(weight_loads))
            act.wait_ge(pre_v, 1)

            def local(k):
                name = f"L{k}"
                H, wid = HEADS[k], WID[k]
                enter(act, name)

                def body(j, cs):
                    for c in range(cs):
                        if k:
                            act.wait_ge(S["d_ready"], plan.seen(name, "d_ready", j, c))
                            nc.scalar.activation(wb[:, 0:H, :, :], db[:, 0:H, :, :], ACT.Exp
                                                 ).then_inc(S["w_ready"], 1)
                        s = plan.slot(name, "ulo", c)
                        for q in range(2):
                            if q == 0 and not (isinstance(j, int) and j == 0 and c < 2):
                                left(act, name, "ulo", j, c)
                            act.wait_ge(S["u_done"], plan.seen(name, "u_done", j, c, i=q))
                            nc.scalar.copy(ulo[:, s, 2 * q:2 * q + 2, 0:wid],
                                           psU[q][:, 0:2 * ROW].rearrange("p (u w) -> p u w", u=2)[:, :, 0:wid]
                                           ).then_inc(S["u_out"], 1)
                groups(act, EDGE_MACROS, body, name in FIRST)

            def mlp(name, layer, g_free):
                nh = HALVES[layer]

                def turned(j, c):
                    s = plan.parity(name, "xT_ps", c)
                    act.wait_ge(S["xT_ps"], plan.seen(name, "xT_ps", j, c))
                    if not before(j, c, 2):
                        act.wait_ge(S["h_ps" if nh else "y_ps"],
                                    plan.seen(name, "h_ps" if nh else "y_ps", j, c, back=2))
                    nc.scalar.copy(xT[:, s, :], psT[s][:]).then_inc(S["xT"], 1)

                def hidden(j, c):
                    s = plan.parity(name, "xT_ps", c)
                    for half in range(nh):
                        off = nh * c + half
                        act.wait_ge(S["h_ps"], plan.seen(name, "h_ps", j, c, i=half))
                        if half == 0 and not before(j, c, 2):
                            act.wait_ge(S["hT" if layer == 0 else "y_ps"],
                                        plan.seen(name, "hT" if layer == 0 else "y_ps", j, c, back=2))
                        bank = psH[(plan.base[name, "h_ps"] + off) % 2]
                        bias = B1[:, BCOL[layer] + half:BCOL[layer] + half + 1]
                        if layer == 0:
                            nc.scalar.activation(zb[:, s, :], bank[:], ACT.Identity, bias=bias, scale=2.0
                                                 ).then_inc(S["z"], 1)
                        else:
                            nc.scalar.activation(hT[:, s, half, :], bank[:], ACT.Relu, bias=bias, scale=1.0
                                                 ).then_inc(S["hT"], 1)

                def second(j, c):
                    s = plan.slot(name, "gst", c)
                    if not before(j, c, 4):
                        g_free(j, c)
                    left(act, name, "gst", j, c)
                    act.wait_ge(S["y_ps"], plan.seen(name, "y_ps", j, c))
                    nc.scalar.copy(gst[:, s, :, :], psY[plan.parity(name, "y_ps", c)][:].rearrange(
                        "p (u d) -> p u d", u=MR)).then_inc(S["y_used"], 1)

                return turned, hidden, second

            def norm(name, ring):
                def root(j, c):
                    act.wait_ge(S["aggr"], plan.seen(name, "aggr", j, c))
                    nc.scalar.activation(lnv[:, c % 4, :], mv[:, c % 4, :, 1], ACT.Ln, bias=eps_c[:],
                                         scale=1.0).then_inc(S["lnv"], 1)
                    act.wait_ge(S["lnv"], plan.seen(name, "lnv", j, c))
                    nc.scalar.activation(rstd[:, c % 4, :, 0], lnv[:, c % 4, :], ACT.Exp, scale=-0.5
                                         ).then_inc(S["rstd"], 1)

                def rows(j, c):
                    s = plan.slot(name, ring, c)
                    left(act, name, ring, j, c)
                    if not before(j, c, 4):
                        if name == "P4":
                            act.wait_ge(S["xT_ps"], plan.seen(name, "xT_ps", j, c, back=4))
                        if name in ("P0", "P2"):
                            act.wait_ge(S["own_sc"], plan.seen(name, "own_sc", j, c, back=4))
                    act.wait_ge(S["shift"], plan.seen(name, "shift", j, c))
                    for u in range(MR):
                        last = nc.scalar.activation(xst[:, s, u, :], rb[:, c % 4, u, :], ACT.Identity,
                                                    bias=neg_mean[:, c % 4, u, :], scale=rstd[:, c % 4, u, :])
                    last.then_inc(S["x_ready"], 1)
                return root, rows

            def dense(i):
                name = f"D{i}"
                enter(act, name)

                def g_free(j, c):
                    if i < 3:
                        act.wait_ge(S["res1"], plan.seen(name, "res1", j, c, back=4))

                turned, hidden, second = mlp(name, i, g_free)
                root, rows = norm(name, "xst")

                def slot(at):
                    for j, c in at(4):
                        root(j, c)
                    for j, c in at(0):
                        turned(j, c)
                    if i < 3:
                        for j, c in at(1):
                            hidden(j, c)
                    for j, c in at(5):
                        rows(j, c)
                    if i:
                        for j, c in at(2 if i < 3 else 1):
                            second(j, c)
                pipeline(act, plan, name, 5, slot)

            def combine(k):
                name = f"C{k}"
                H = HEADS[k]
                enter(act, name)
                for r in range(2 * H):
                    act.wait_ge(S["c_dm"], plan.seen(name, "c_dm", 0, 0, r))
                    nc.scalar.activation(wt[:], mm[:], ACT.Exp).then_inc(S["c_wt"], 1)
                for r in range(2 * H):
                    act.wait_ge(S["c_arg"], plan.seen(name, "c_arg", 0, 0, r))
                    if r >= 2:
                        if k:
                            act.wait_ge(S["c_back_ps"], plan.seen(name, "c_back_ps", 0, 0, r - 2))
                        ring = f"c_w{r % 2}"
                        act.wait_ge(R[ring][0], plan.full(name, ring, 0, 0) - 16 * H + 16 * (r // 2))
                    lo, hi = (1, 3) if k == 0 else (0, 3) if k == 5 else (0, 4)
                    nc.scalar.activation(coef[:, r % 2, lo:hi, :], arg[:, lo:hi, :], ACT.Exp).then_inc(S["c_exp"], 1)

            def post(k):
                name = f"P{k}"
                enter(act, name)

                def g_free(j, c):
                    act.wait_ge(S["own_prod" if k == 4 else "own_sc"],
                                plan.seen(name, "own_prod" if k == 4 else "own_sc", j, c, back=4))

                root, rows = norm(name, "out_sc" if k == 5 else "xst")
                if k == 5:
                    stored(act, name, ("xst",))
                if k in MLP_LAYER:
                    turned, hidden, second = mlp(name, MLP_LAYER[k], g_free)

                def slot(at):
                    if k in (0, 2, 4, 5):
                        for j, c in at(5 if k == 0 else 2):
                            root(j, c)
                        for j, c in at(6 if k == 0 else 3):
                            rows(j, c)
                    if k in MLP_LAYER:
                        for j, c in at(4 if k == 4 else 1):
                            turned(j, c)
                        if k < 4:
                            for j, c in at(2):
                                hidden(j, c)
                        if k:
                            for j, c in at(5 if k == 4 else 3):
                                second(j, c)
                pipeline(act, plan, name, {0: 6, 1: 3, 2: 3, 3: 3, 4: 5, 5: 3}[k], slot)

            local(0)
            dense(0)
            combine(0)
            post(0)
            for i in (1, 2, 3):
                dense(i)
            for k in range(1, PHASES):
                local(k)
                combine(k)
                post(k)

        @block.vector
        def _(dve):
            vec = nc.vector
            vec.memset(pi[:, 0:2, :, :], NODES)
            vec.memset(pi[:, 2, :, :], 0)
            vec.memset(ulo[:], 0.0).then_inc(pre_fill, 3)
            vec.memset(gat[:, :, :, P:ROW], 1.0)
            vec.memset(xs[:, :, :, P:ROW], 1.0)
            vec.memset(mT[:], 0.0)
            vec.memset(csum[:], 0.0)
            vec.memset(ppen, -BIG)
            vec.memset(eps_c[:], EPS)
            dve.wait_ge(pre_iota, 5)
            vec.tensor_copy(id_f, id_i[:])
            vec.tensor_copy(ti[:], ti_i[:])
            vec.tensor_copy(tcf[:, 0:1], tc_i[:]).then_inc(pre_f, 1)
            dve.wait_ge(pre_f, 1)
            vec.tensor_scalar(tcf[:, 1:2], tcf[:, 0:1], float(TB), None, ALU.add).then_inc(pre_f, 1)
            vec.tensor_scalar(ident[:], id_f, 0.0, None, ALU.is_equal).then_inc(pre_v, 1)
            dve.wait_ge(w_load, 16 * len(weight_loads))
            vec.tensor_copy(ab, acol[:].to_broadcast([P, 6, P]))
            dve.wait_ge(pre_ps, 1)
            vec.tensor_copy(w1T.rearrange("p a d -> p (a d)"), psH[0][:, 0:3 * P]).then_inc(pre_v, 1)
            dve.wait_ge(pre_ps, 2)
            vec.tensor_copy(VB[:, 0:2, :].rearrange("p a d -> p (a d)"), psH[1][:, 0:2 * P])
            vec.tensor_copy(VB[:, 4:6, :].rearrange("p a d -> p (a d)"), psH[1][:, 2 * P:4 * P]).then_inc(pre_f, 1)
            dve.wait_ge(pre_load, 16 * len(index_loads))
            dve.wait_ge(pre_f, 3)
            vec.tensor_copy(pf[:, 0, :, :], pi[:, 0, :, :])
            vec.tensor_copy(pf[:, 1, :, :], pi[:, 1, :, :])
            vec.tensor_copy(pf[:, 3, :, :], pi[:, 2, :, :]).then_inc(pre_f, 1)
            dve.wait_ge(pre_f, 4)
            vec.tensor_tensor(peq[:, 0, :, :], pf[:, 0, :, :], pf[:, 1, :, :], ALU.is_equal).then_inc(pre_f, 1)
            dve.wait_ge(pre_f, 5)
            vec.scalar_tensor_tensor(out=pf[:, 1, :, :], in0=peq[:, 0, :, :], scalar=SKIP, in1=pf[:, 0, :, :],
                                     op0=ALU.mult, op1=ALU.add)
            vec.tensor_scalar(pf[:, 2, :, :], pf[:, 0, :, :], float(NODES - 1), None, ALU.min).then_inc(pre_v, 1)
            vec.tensor_tensor(peq[:, 1, :, 1:P], pf[:, 0, :, 1:P], pf[:, 0, :, 0:P - 1], ALU.not_equal
                              ).then_inc(pre_f, 1)
            dve.wait_ge(pre_f, 6)
            vec.tensor_scalar(ppen[:, :, 0, 1:P], peq[:, 1, :, 1:P], -BIG, None, ALU.mult)
            vec.tensor_scalar(ppen[:, :, 1, 0:P - 1], peq[:, 1, :, 1:P], -BIG, None, ALU.mult).then_inc(pre_tab, 1)
            for d in range(2):
                col = 0 if d == 0 else P - 1
                for b in range(2):
                    vec.tensor_scalar(seg[:, d, b, :], pf[:, 0, b, :], pf[:, 0, b, col:col + 1], -BIG,
                                      ALU.not_equal, ALU.mult)
            dve.wait_ge(pre_ps, 3)
            vec.tensor_copy(dcol[:], psT[0][:, 0:TILES])
            vec.tensor_copy(scat_i[:], psT[0][:, TILES:2 * TILES])
            vec.tensor_copy(dstm_i[:], psT[1][:, 0:TILES])
            vec.tensor_copy(src_i[:], psT[1][:, TILES:2 * TILES]).then_inc(pre_f, 1)
            for d in range(2):
                col = P - 1 if d == 0 else 0
                for b in range(2):
                    last = vec.tensor_copy(colb[:, b, :], pf[:, 0, b, col:col + 1].to_broadcast([TB, TB]))
                last.then_inc(pre_v, 1)
                dve.wait_ge(pre_ps, 4 + d)
                bank = psY[d]
                other = 0 if d == 0 else P - 1
                for b in range(2):
                    vec.tensor_scalar(mm[:, b, :], bank[0:TB, 0:TILES], pf[:, 0, b, other:other + 1], -BIG,
                                      ALU.not_equal, ALU.mult)
                    last = vec.tensor_scalar(wt[:, b, :], ti[:], tcf[:, b:b + 1], -BIG,
                                             ALU.is_ge if d == 0 else ALU.is_le, ALU.mult)
                last.then_inc(pre_f, 1)
                dve.wait_ge(pre_f, 8 + 2 * d)
                vec.tensor_tensor(cross[:, d, :, :], mm[:], wt[:], ALU.add).then_inc(pre_f, 1)
                dve.wait_ge(pre_f, 9 + 2 * d)
            vec.memset(id_f[:, 0:1], 0.0).then_inc(pre_done, 1)

            def local(k):
                name = f"L{k}"
                H = HEADS[k]
                enter(dve, name)

                def body(j, cs):
                    for c in range(cs):
                        g = plan.slot(name, "gat", c)
                        s2 = c % 2
                        cols = bass.ds(MR * c + j * (MR * MR), MR)
                        early = isinstance(j, int) and j == 0
                        dve.wait_ge(R["gat"][plan.slot(name, "gat", c)], plan.full(name, "gat", j, c))
                        if k == 0:
                            dve.wait_ge(R["ea"][plan.slot(name, "ea", c)], plan.full(name, "ea", j, c))
                            if isinstance(j, int) and MR * j + c == EDGE_MACROS - 1:
                                s = plan.slot(name, "ea", c)
                                dve.wait_ge(R["ea"][s], plan.full(name, "ea", j, c) + 16)
                            vec.tensor_tensor(gat[:, g, :, 0:P], gat[:, g, :, 0:P],
                                              eab[:, plan.slot(name, "ea", c), :, :], ALU.add
                                              ).then_inc(S["ea_added"], 1)
                            dve.wait_ge(S["ea_added"], plan.seen(name, "ea_added", j, c))
                        elif k < 5:
                            for u in range(MR):
                                last = vec.tensor_tensor_reduce(junk[:, u, :], gat[:, g, u, 0:P],
                                                                VB[:, 2 * (k - 1), :], 1.0, 0.0, ALU.mult, ALU.add,
                                                                sc[:, 0, u, :])
                            last.then_inc(S["sc"], 1)
                        else:
                            vec.tensor_tensor(junk[:, 0:MR, :], gat[:, g, :, 0:P], A5[:, 0:1, :].to_broadcast([P, MR, P]),
                                              ALU.mult).then_inc(S["prod"], 1)
                            dve.wait_ge(S["prod"], plan.seen(name, "prod", j, c))
                            vec.tensor_reduce(sc[:, :, :, 0].rearrange("p h u -> p u h"),
                                              junk[:, 0:MR, :].rearrange("p u (h e) -> p u h e", h=4), AX.X, ALU.add
                                              ).then_inc(S["sc"], 1)
                        if k:
                            dve.wait_ge(S["sc"], plan.seen(name, "sc", j, c))
                            vec.tensor_tensor(es[:, 0:H, :, 0], sc[:, 0:H, :, 0], a_dst[:, 0:H, cols], ALU.add
                                              ).then_inc(S["esum"], 1)
                            dve.wait_ge(S["esum"], plan.seen(name, "esum", j, c))
                            vec.scalar_tensor_tensor(out=eb[:, 0:H, :, 0], in0=es[:, 0:H, :, 0], scalar=SLOPE,
                                                     in1=es[:, 0:H, :, 0], op0=ALU.mult, op1=ALU.max
                                                     ).then_inc(S["e_ready"], 1)
                            dve.wait_ge(R["pen"][plan.slot(name, "pen", c)], plan.full(name, "pen", j, c))
                            dve.wait_ge(S["eT"], plan.seen(name, "eT", j, c))
                            sp_ = plan.slot(name, "pen", c)
                            n = MR * H
                            vec.tensor_tensor_scan(scan[0:n, 0, :], pen[0:n, sp_, 0, :], psS[0:n, 0:P], -BIG,
                                                   ALU.add, ALU.max)
                            vec.tensor_tensor_scan(scan[0:n, 1, ::-1], pen[0:n, sp_, 1, ::-1], psS[0:n, 0:P][:, ::-1],
                                                   -BIG, ALU.add, ALU.max).then_inc(S["scans"], 1)
                            dve.wait_ge(S["scans"], plan.seen(name, "scans", j, c))
                            vec.tensor_tensor(mrow[0:n, :], scan[0:n, 0, :], scan[0:n, 1, :], ALU.max
                                              ).then_inc(S["mrow"], 1)
                            dve.wait_ge(S["mT"], plan.seen(name, "mT", j, c))
                            back = psS[:, P:P + n].rearrange("p (h u) -> p h u", h=H)
                            vec.tensor_tensor(db[:, 0:H, :, 0], eb[:, 0:H, :, 0], back, ALU.subtract
                                              ).then_inc(S["d_ready"], 1)
                            vec.tensor_scalar(m_loc[:, 0:H, cols], back, 0.0, None, ALU.add).then_inc(S["m_kept"], 1)
                        dve.wait_ge(R["dstb"][plan.slot(name, "dstb", c)], plan.full(name, "dstb", j, c))
                        if not (early and c < 2):
                            dve.wait_ge(S["u_done"], plan.seen(name, "u_done", j, c, back=2))
                        if k:
                            dve.wait_ge(S["w_ready"], plan.seen(name, "w_ready", j, c))
                        sd = plan.slot(name, "dstb", c)
                        if k == 5:
                            o = gw[:, s2, :, :].rearrange("p u (h e) -> p u h e", h=4)
                            vec.tensor_tensor(o[:, :, :, 0:32],
                                              gat[:, g, :, 0:P].rearrange("p u (h e) -> p u h e", h=4),
                                              wb[:].rearrange("p h u o -> p u h o").to_broadcast([P, MR, 4, 32]),
                                              ALU.mult)
                            vec.tensor_copy(o[:, :, :, 32:33], wb[:].rearrange("p h u o -> p u h o"))
                        for u in range(MR):
                            col = dcol[:, bass.ds(MR * c + u + j * (MR * MR), 1)]
                            if k in (0, 5):
                                last = vec.tensor_scalar(sel[:, s2, u, :], dstb[:, sd, u, :], col, None, ALU.is_equal)
                            else:
                                last = vec.tensor_scalar(sel[:, s2, u, :], dstb[:, sd, u, :], col, wb[:, 0, u, :],
                                                         ALU.is_equal, ALU.mult)
                        last.then_inc(S["sel_ready"], 1)
                groups(dve, EDGE_MACROS, body, name in FIRST)

            def norm(name):
                def stats(j, c):
                    dve.wait_ge(S["res2"], plan.seen(name, "res2", j, c))
                    for u in range(MR):
                        last = vec.bn_stats(st[:, c % 4, u, :], rb[:, c % 4, u, :])
                    last.then_inc(S["stats"], 1)

                def mean_variance(j, c):
                    dve.wait_ge(S["stats"], plan.seen(name, "stats", j, c))
                    own(dve, "dve")
                    for u in range(MR):
                        last = vec.bn_aggr(mv[:, c % 4, u, :], st[:, c % 4, u, :])
                    last.then_inc(S["aggr"], 1)

                def shift_rows(j, c):
                    dve.wait_ge(S["rstd"], plan.seen(name, "rstd", j, c))
                    vec.scalar_tensor_tensor(out=neg_mean[:, c % 4, :, 0], in0=mv[:, c % 4, :, 0], scalar=-1.0,
                                             in1=rstd[:, c % 4, :, 0], op0=ALU.mult, op1=ALU.mult
                                             ).then_inc(S["shift"], 1)
                return shift_rows, stats, mean_variance

            def rows_free(name, j, c):
                if not before(j, c, 4):
                    dve.wait_ge(S["x_ready"], plan.seen(name, "x_ready", j, c, back=4))

            def leaky(name):
                def step(j, c):
                    s = plan.parity(name, "xT_ps", c)
                    dve.wait_ge(S["z"], plan.seen(name, "z", j, c))
                    if not before(j, c, 2):
                        dve.wait_ge(S["y_ps"], plan.seen(name, "y_ps", j, c, back=2))
                    vec.scalar_tensor_tensor(out=hT[:, s, 0, :], in0=zb[:, s, :], scalar=0.01, in1=zb[:, s, :],
                                             op0=ALU.mult, op1=ALU.max).then_inc(S["hT"], 1)
                return step

            def add_bias(name, layer):
                def step(j, c):
                    r = rb[:, c % 4, :, :]
                    if name == "D3":
                        rows_free(name, j, c)
                        dve.wait_ge(R["xin"][plan.slot(name, "xin", c)], plan.full(name, "xin", j, c))
                        source = xin[:, plan.slot(name, "xin", c), :, :]
                    else:
                        dve.wait_ge(S["y_used" if layer == 0 else "res1"],
                                    plan.seen(name, "y_used" if layer == 0 else "res1", j, c))
                        source = r
                    vec.tensor_tensor(r, source, BB[:, layer, :, :].to_broadcast([P, MR, P]), ALU.add
                                      ).then_inc(S["res2"], 1)
                return step

            def add_product(name, own_rows):
                def step(j, c):
                    rows_free(name, j, c)
                    dve.wait_ge(S["y_ps"], plan.seen(name, "y_ps", j, c))
                    vec.tensor_tensor(rb[:, c % 4, :, :], psY[plan.parity(name, "y_ps", c)][:].rearrange(
                        "p (u d) -> p u d", u=MR), own_rows(c), ALU.add).then_inc(S["y_used"], 1)
                return step

            def dense(i):
                name = f"D{i}"
                enter(dve, name)

                def rows_in(c):
                    return xin[:, plan.slot(name, "xin", c), :, :]

                def add_g(j, c):
                    rows_free(name, j, c)
                    dve.wait_ge(S["y_used"], plan.seen(name, "y_used", j, c))
                    vec.tensor_tensor(rb[:, c % 4, :, :], gst[:, plan.slot(name, "gst", c), :, :], rows_in(c), ALU.add
                                      ).then_inc(S["res1"], 1)

                shift_rows, stats, mean_variance = norm(name)
                bias, leak, add_y = add_bias(name, i), leaky(name), add_product(name, rows_in)

                def slot_0(at):
                    for j, c in at(4):
                        shift_rows(j, c)
                    for j, c in at(1):
                        leak(j, c)
                    for j, c in at(2):
                        add_y(j, c)
                    for j, c in at(2):
                        bias(j, c)
                    for j, c in at(2):
                        stats(j, c)
                    for j, c in at(2):
                        mean_variance(j, c)

                def slot_1_2(at):
                    for j, c in at(4):
                        shift_rows(j, c)
                    for j, c in at(2):
                        add_g(j, c)
                    for j, c in at(2):
                        bias(j, c)
                    for j, c in at(2):
                        stats(j, c)
                    for j, c in at(2):
                        mean_variance(j, c)

                def slot_3(at):
                    for j, c in at(4):
                        shift_rows(j, c)
                    for j, c in at(2):
                        bias(j, c)
                    for j, c in at(2):
                        stats(j, c)
                    for j, c in at(2):
                        mean_variance(j, c)
                pipeline(dve, plan, name, 5, (slot_0, slot_1_2, slot_1_2, slot_3)[i])

            def combine(k):
                name = f"C{k}"
                H, hw = HEADS[k], HW[k]
                enter(dve, name)

                def at(step, r):
                    dve.wait_ge(S[step], plan.seen(name, step, 0, 0, r))

                if k:
                    for h in list(range(H)) + ([4] if k < 5 else []):
                        r = h if h < 4 else H
                        at("c_mT_ps", r)
                        vec.tensor_copy(mT[:, h, :, :].rearrange("p b i -> p (b i)"), psT[r % 2][0:TB, 0:2 * P]
                                        ).then_inc(S["c_mT"], 1)
                    if k == 5:
                        vec.memset(mT[:, 4, :, :], -BIG).then_inc(S["c_mT"], 1)
                    at("c_mT", H)
                else:
                    vec.memset(mT[:], 0.0).then_inc(S["c_mT"], 2)
                    at("c_mT", H)
                for r in range(2 * H):
                    h, d = r // 2, r % 2
                    col = P - 1 if d == 0 else 0
                    for b in range(2):
                        last = vec.tensor_copy(colb[:, b, :], mT[:, h, b, col:col + 1].to_broadcast([TB, TB]))
                    last.then_inc(S["c_colb"], 1)
                    at("c_row", r)
                    for bt in range(2):
                        last = vec.tensor_tensor(mm[:, bt, :], psS[0:TB, 0:TILES], cross[:, d, bt, :], ALU.add)
                    last.then_inc(S["c_mm"], 1)
                    at("c_mm", r)
                    if k:
                        vec.tensor_reduce(mB[:, d, :, h:h + 1], mm[:], AX.X, ALU.max).then_inc(S["c_mb"], 1)
                    else:
                        vec.memset(mB[:, d, :, h:h + 1], 0.0).then_inc(S["c_mb"], 1)
                    at("c_mb", r)
                    for bt in range(2):
                        last = vec.tensor_scalar(mm[:, bt, :], mm[:, bt, :], mB[:, d, bt, h:h + 1], None, ALU.subtract)
                    last.then_inc(S["c_dm"], 1)
                    at("c_wtT_ps", r)
                    for bt in range(2):
                        last = vec.tensor_copy(wtT[:, bt, :, :].rearrange("p b t -> p (b t)"), psT[bt][0:TB, 0:2 * TB])
                    last.then_inc(S["c_wtT"], 1)
                    for bt in range(2):
                        at("c_sum_ps", 2 * r + bt)
                        vec.tensor_copy(csum[:, d, bt, hw * h:hw * h + hw], psH[bt][0:TB, 0:hw]
                                        ).then_inc(S["c_sum"], 1)
                for r in range(2 * H):
                    h, b = r // 2, r % 2
                    if r:
                        at("c_exp", r - 1)
                    if k == 0:
                        last = vec.tensor_copy(arg[:, 1, :], seg[:, 0, b, :])
                        vec.tensor_copy(arg[:, 2, :], seg[:, 1, b, :]).then_inc(S["c_arg"], 1)
                        continue
                    for d in range(2):
                        last = vec.tensor_scalar(tmax[:, d, :], seg[:, d, b, :], mB[:, d, b, h:h + 1], None, ALU.add)
                    last.then_inc(S["c_t"], 1)
                    at("c_t", 4 * r)
                    for i, other in enumerate((tmax[:, 0, :], tmax[:, 1, :], mT[:, 4, b, :])):
                        vec.tensor_tensor(tmax[:, 2, :], mT[:, h, b, :] if i == 0 else tmax[:, 2, :], other, ALU.max
                                          ).then_inc(S["c_t"], 1)
                        at("c_t", 4 * r + 1 + i)
                    vec.tensor_tensor(arg[:, 0, :], mT[:, h, b, :], tmax[:, 2, :], ALU.subtract)
                    if k < 5:
                        vec.tensor_tensor(arg[:, 3, :], mT[:, 4, b, :], tmax[:, 2, :], ALU.subtract)
                    vec.tensor_tensor(arg[:, 1, :], tmax[:, 0, :], tmax[:, 2, :], ALU.subtract)
                    vec.tensor_tensor(arg[:, 2, :], tmax[:, 1, :], tmax[:, 2, :], ALU.subtract).then_inc(S["c_arg"], 1)
                    at("c_back_ps", r)
                    if k < 5:
                        vec.tensor_copy(c_self[:, TB * b:TB * b + TB], psT[r % 2][:, P:P + TB])
                    vec.tensor_copy(c_loc[:, h, TB * b:TB * b + TB], psT[r % 2][:, 0:TB]).then_inc(S["c_back"], 1)

            def post(k):
                name = f"P{k}"
                H, hw, wid = HEADS[k], HW[k], WID[k]
                layer = {0: 0, 2: 1, 4: 2, 5: 3}.get(k)
                enter(dve, name)

                def tcol(a, j, c, u):
                    return a[:, bass.ds(MR * c + u + j * (MR * plan.group[name]), 1)]

                def add_carries(j, c):
                    su = plan.slot(name, "uin", c)
                    dve.wait_ge(R["uin"][plan.slot(name, "uin", c)], plan.full(name, "uin", j, c))
                    for q in range(2):
                        dve.wait_ge(S["p_ps"], plan.seen(name, "p_ps", j, c, i=q))
                        for i in range(2):
                            u = 2 * q + i
                            for h in range(H):
                                a, z = hw * h, hw * h + hw
                                if k == 0:
                                    last = vec.tensor_tensor(t1[:, c % 2, u, a:z], uin[:, su, u, a:z],
                                                             psU[q][:, ROW * i + a:ROW * i + z], ALU.add)
                                else:
                                    last = vec.scalar_tensor_tensor(
                                        out=t1[:, c % 2, u, a:z], in0=uin[:, su, u, a:z],
                                        scalar=tcol(c_loc[:, h, :], j, c, u), in1=psU[q][:, ROW * i + a:ROW * i + z],
                                        op0=ALU.mult, op1=ALU.add)
                        last.then_inc(S["p_used"], 1)

                def layer0_rows(j, c):
                    dve.wait_ge(R["xs"][plan.slot(name, "xs", c)], plan.full(name, "xs", j, c))
                    dve.wait_ge(S["p_used"], plan.seen(name, "p_used", j, c))
                    if not before(j, c, 4):
                        dve.wait_ge(S["xT_ps"], plan.seen(name, "xT_ps", j, c, back=4))
                    vec.scalar_tensor_tensor(out=xin[:, c % 4, :, :], in0=t1[:, c % 2, :, 0:P], scalar=0.5,
                                             in1=xs[:, plan.slot(name, "xs", c), :, 0:P], op0=ALU.mult, op1=ALU.add
                                             ).then_inc(S["u_ready"], 1)

                def add_self(j, c):
                    dve.wait_ge(R["xs"][plan.slot(name, "xs", c)], plan.full(name, "xs", j, c))
                    dve.wait_ge(S["p_used"], plan.seen(name, "p_used", j, c))
                    for u in range(MR):
                        last = vec.scalar_tensor_tensor(
                            out=t1[:, c % 2, u, 0:wid], in0=xs[:, plan.slot(name, "xs", c), u, 0:wid],
                            scalar=tcol(c_self, j, c, u), in1=t1[:, c % 2, u, 0:wid], op0=ALU.mult, op1=ALU.add)
                    last.then_inc(S["selfed"], 1)

                def guard(j, c):
                    dve.wait_ge(S["p_used"], plan.seen(name, "p_used", j, c))
                    t = t1[:, c % 2, :, :].rearrange("p u (h e) -> p u h e", h=4)
                    vec.tensor_scalar(rz[:], t[:, :, :, 32:33], 1e-9, None, ALU.max).then_inc(S["zmax"], 1)

                def invert(j, c):
                    if k < 5:
                        dve.wait_ge(S["selfed"], plan.seen(name, "selfed", j, c))
                        vec.reciprocal(rz[:, :, 0, :], t1[:, c % 2, :, P:P + 1]).then_inc(S["rz"], 1)
                    else:
                        dve.wait_ge(S["zmax"], plan.seen(name, "zmax", j, c))
                        vec.reciprocal(rz[:], rz[:]).then_inc(S["rz"], 1)

                def divide(j, c):
                    if k not in (1, 3):
                        rows_free(name, j, c)
                    dve.wait_ge(S["rz"], plan.seen(name, "rz", j, c))
                    if k in (1, 3):
                        if not before(j, c, 4):
                            dve.wait_ge(S["xT_ps"], plan.seen(name, "xT_ps", j, c, back=4))
                        vec.tensor_tensor(xin[:, c % 4, :, :], t1[:, c % 2, :, 0:P],
                                          rz[:, :, 0, :].to_broadcast([P, MR, P]), ALU.mult
                                          ).then_inc(S["u_ready"], 1)
                    elif k < 5:
                        vec.tensor_tensor(rb[:, c % 4, :, :], t1[:, c % 2, :, 0:P],
                                          rz[:, :, 0, :].to_broadcast([P, MR, P]), ALU.mult).then_inc(S["un"], 1)
                    else:
                        t = t1[:, c % 2, :, :].rearrange("p u (h e) -> p u h e", h=4)
                        vec.tensor_tensor(rb[:, c % 4, :, :].rearrange("p u (h e) -> p u h e", h=4), t[:, :, :, 0:32],
                                          rz[:].to_broadcast([P, MR, 4, 32]), ALU.mult).then_inc(S["un"], 1)

                def add_rows(j, c):
                    dve.wait_ge(R["xr"][plan.slot(name, "xr", c)], plan.full(name, "xr", j, c))
                    dve.wait_ge(S["un"], plan.seen(name, "un", j, c))
                    vec.tensor_tensor(rb[:, c % 4, :, :], rb[:, c % 4, :, :], xr[:, plan.slot(name, "xr", c), :, :],
                                      ALU.add).then_inc(S["res1"], 1)

                def score_products(j, c):
                    if k in (0, 2):
                        dve.wait_ge(S["x_ready"], plan.seen(name, "x_ready", j, c))
                        rows = xst[:, plan.slot(name, "xst", c), :, :]
                    else:
                        dve.wait_ge(S["y_used"], plan.seen(name, "y_used", j, c))
                        rows = gst[:, plan.slot(name, "gst", c), :, :]
                    for i in range(2):
                        for u in range(MR):
                            last = vec.tensor_tensor_reduce(junk[:, MR * i + u, :], rows[:, u, :], VB[:, 2 * k + i, :],
                                                            1.0, 0.0, ALU.mult, ALU.add, own_s[:, i, u:u + 1])
                    last.then_inc(S["own_sc"], 1)

                def score_sum(j, c):
                    cols = bass.ds(MR * c + j * (MR * plan.group[name]), MR)
                    dve.wait_ge(S["own_sc"], plan.seen(name, "own_sc", j, c))
                    vec.tensor_scalar(a_dst[:, 0, cols], own_s[:, 1, :], 0.0, None, ALU.add)
                    vec.tensor_tensor(own_m[:, 0, :], own_s[:, 0, :], own_s[:, 1, :], ALU.add).then_inc(S["own_sum"], 1)

                def self_score(j, c):
                    cols = bass.ds(MR * c + j * (MR * plan.group[name]), MR)
                    dve.wait_ge(S["own_sum"], plan.seen(name, "own_sum", j, c))
                    vec.scalar_tensor_tensor(out=e_self[:, cols], in0=own_m[:, 0, :], scalar=SLOPE,
                                             in1=own_m[:, 0, :], op0=ALU.mult, op1=ALU.max)

                def head_products(j, c):
                    dve.wait_ge(S["y_used"], plan.seen(name, "y_used", j, c))
                    vec.tensor_tensor(junk[:, 0:MR, :], gst[:, plan.slot(name, "gst", c), :, :],
                                      A5[:, 1:2, :].to_broadcast([P, MR, P]), ALU.mult).then_inc(S["own_prod"], 1)

                def head_sums(j, c):
                    dve.wait_ge(S["own_prod"], plan.seen(name, "own_prod", j, c))
                    vec.tensor_reduce(own_m[:].rearrange("p h u -> p u h"),
                                      junk[:, 0:MR, :].rearrange("p u (h e) -> p u h e", h=4), AX.X, ALU.add
                                      ).then_inc(S["own_sc"], 1)

                def head_scores(j, c):
                    dve.wait_ge(S["own_sc"], plan.seen(name, "own_sc", j, c))
                    vec.tensor_scalar(a_dst[:, :, bass.ds(MR * c + j * (MR * plan.group[name]), MR)], own_m[:], 0.0,
                                      None, ALU.add).then_inc(S["own_sum"], 1)

                shift_rows, stats, mean_variance = norm(name)
                bias, leak = add_bias(name, layer), leaky(name)
                add_y = add_product(name, lambda c: xs[:, plan.slot(name, "xs", c), :, 0:P])

                def slot_0(at):
                    for j, c in at(5):
                        shift_rows(j, c)
                    for j, c in at(0):
                        add_carries(j, c)
                    for j, c in at(2):
                        leak(j, c)
                    for j, c in at(0):
                        layer0_rows(j, c)
                    for j, c in at(3):
                        add_y(j, c)
                    for j, c in at(3):
                        bias(j, c)
                    for j, c in at(3):
                        stats(j, c)
                    for j, c in at(7):
                        score_products(j, c)
                    for j, c in at(3):
                        mean_variance(j, c)
                    for j, c in at(7):
                        score_sum(j, c)
                    for j, c in at(7):
                        self_score(j, c)

                def slot_1_3(at):
                    for j, c in at(0):
                        add_carries(j, c)
                    for j, c in at(4):
                        score_products(j, c)
                    for j, c in at(0):
                        add_self(j, c)
                    for j, c in at(4):
                        score_sum(j, c)
                    for j, c in at(0):
                        invert(j, c)
                    for j, c in at(4):
                        self_score(j, c)
                    for j, c in at(0):
                        divide(j, c)

                def slot_2(at):
                    for j, c in at(2):
                        shift_rows(j, c)
                    for j, c in at(0):
                        add_carries(j, c)
                    for j, c in at(0):
                        add_self(j, c)
                    for j, c in at(0):
                        invert(j, c)
                    for j, c in at(4):
                        score_products(j, c)
                    for j, c in at(0):
                        divide(j, c)
                    for j, c in at(4):
                        score_sum(j, c)
                    for j, c in at(0):
                        add_rows(j, c)
                    for j, c in at(4):
                        self_score(j, c)
                    for j, c in at(0):
                        bias(j, c)
                    for j, c in at(0):
                        stats(j, c)
                    for j, c in at(0):
                        mean_variance(j, c)

                def slot_4(at):
                    for j, c in at(2):
                        shift_rows(j, c)
                    for j, c in at(0):
                        add_carries(j, c)
                    for j, c in at(0):
                        add_self(j, c)
                    for j, c in at(0):
                        invert(j, c)
                    for j, c in at(6):
                        head_products(j, c)
                    for j, c in at(0):
                        divide(j, c)
                    for j, c in at(6):
                        head_sums(j, c)
                    for j, c in at(0):
                        add_rows(j, c)
                    for j, c in at(6):
                        head_scores(j, c)
                    for j, c in at(0):
                        bias(j, c)
                    for j, c in at(0):
                        stats(j, c)
                    for j, c in at(0):
                        mean_variance(j, c)

                def slot_5(at):
                    for j, c in at(2):
                        shift_rows(j, c)
                    for j, c in at(0):
                        add_carries(j, c)
                    for j, c in at(0):
                        guard(j, c)
                    for j, c in at(0):
                        invert(j, c)
                    for j, c in at(0):
                        divide(j, c)
                    for j, c in at(0):
                        add_rows(j, c)
                    for j, c in at(0):
                        bias(j, c)
                    for j, c in at(0):
                        stats(j, c)
                    for j, c in at(0):
                        mean_variance(j, c)

                pipeline(dve, plan, name, (7, 4, 4, 4, 6, 3)[k], (slot_0, slot_1_3, slot_2, slot_1_3, slot_4, slot_5)[k])

            local(0)
            dense(0)
            combine(0)
            post(0)
            for i in (1, 2, 3):
                dense(i)
            for k in range(1, PHASES):
                local(k)
                combine(k)
                post(k)


_WEIGHTS = ["L0_gnn_W1", "L0_gnn_b1", "L0_gnn_W2", "L0_gnn_b2",
            "L1_gnn_W1", "L1_gnn_a1_src", "L1_gnn_a1_dst", "L1_gnn_b1",
            "L1_gnn_W2", "L1_gnn_a2_src", "L1_gnn_a2_dst", "L1_gnn_b2",
            "L2_gnn_W1", "L2_gnn_a1_src", "L2_gnn_a1_dst", "L2_gnn_b1",
            "L2_gnn_W2", "L2_gnn_a2_src", "L2_gnn_a2_dst", "L2_gnn_b2",
            "L3_gnn_W", "L3_gnn_att", "L3_gnn_bias"]


def kernel(**inputs):
    import numpy as _np
    import concourse.bacc as _bacc
    from concourse import mybir as _mybir
    from concourse.bass_utils import run_bass_kernel_spmd as _run

    nc = _bacc.Bacc("TRN2", target_bir_lowering=False, num_devices=1)
    arrays, aps = {}, {}
    for name in ["x", "src", "dst", "edge_attr_128"] + _WEIGHTS:
        a = _np.ascontiguousarray(inputs[name])
        arrays[f"in_{name}"] = a
        aps[name] = nc.dram_tensor(f"in_{name}", a.shape, _mybir.dt.from_np(a.dtype), kind="ExternalInput").ap()
    w = {name: aps[name] for name in _WEIGHTS}
    w["out"] = nc.dram_tensor("out_0", (NODES, D), F32, kind="ExternalOutput").ap()
    build(nc, aps["x"], aps["src"], aps["dst"], aps["edge_attr_128"], w)
    r = _run(nc, [arrays], core_ids=[0])
    return r.results[0]["out_0"]
```

```python
import concourse.bass as bass
from concourse import mybir
from contextlib import ExitStack

F32 = mybir.dt.float32
I32 = mybir.dt.int32
ALU = mybir.AluOpType
ACT = mybir.ActivationFunctionType
AX = mybir.AxisListType

P = 128
D = 128
NODES = 50000
EDGES = 25000
MR = 4
NODE_MACROS = -(-NODES // (P * MR))
NODE_ROWS = NODE_MACROS * P * MR
TILES = -(-EDGES // (P * MR)) * MR
EDGE_MACROS = TILES // MR
SLOTS = TILES * P
TB = TILES // 2
BIG = 1.0e30
SKIP = 1.0e6
EPS = 1e-5
SLOPE = 0.2

PHASES = 6
HEADS = [1, 1, 1, 1, 1, 4]
HW = [D, D + 1, D + 1, D + 1, D + 1, D // 4 + 1]
WID = [HEADS[k] * HW[k] for k in range(PHASES)]
ROW = 132
MLP_LAYER = {0: 0, 1: 1, 3: 2, 4: 3}
HALVES = [1, 2, 1, 0]
DENSE_LAYER = [0, 1, 2, 3]
XIN = 8


class Plan:

    def __init__(self):
        self.base, self.per, self.n, self.group = {}, {}, {}, {}
        self.last, self.before, self.stores = {}, {}, {}
        self.total = {}
        self.ring_size, self.ring_seq, self.ring_full, self.ring_k = {}, {}, {}, {}
        self.now_seq, self.now_full = {}, {}

    def loop(self, name, n, steps, rings, last, group=MR, beside=None):
        self.group[name] = group
        self.before[name] = self.before[beside] if beside else self.last
        self.stores[name] = {r: list(v) for r, v in self.now_full.items()}
        self.n[name] = n
        for step, k in steps:
            self.base[name, step] = self.total.get(step, 0)
            self.per[name, step] = k
            self.total[step] = self.total.get(step, 0) + n * k
        for ring, size, k in rings:
            self.ring_size[ring] = size
            seq = self.now_seq.get(ring, 0)
            full = self.now_full.get(ring, [0] * size)
            self.ring_seq[name, ring], self.ring_full[name, ring] = seq, list(full)
            self.ring_k[name, ring] = k
            for i in range(n):
                full[(seq + i) % size] += 16 * k
            self.now_seq[ring], self.now_full[ring] = seq + n, full
        together = self.last if beside else {}
        self.last = {**{(beside, e): v for e, v in together.items()},
                     **{e: (s, self.total[s]) for e, s in last.items()}}

    def seen(self, name, step, j, c, i=None, back=0):
        k = self.per[name, step]
        i = k - 1 if i is None else i
        return self.base[name, step] + k * c + i + 1 - k * back + j * (self.group[name] * k)

    def slot(self, name, ring, c):
        return (self.ring_seq[name, ring] + c) % self.ring_size[ring]

    def full(self, name, ring, j, c):
        size, k = self.ring_size[ring], self.ring_k[name, ring]
        s = self.slot(name, ring, c)
        first = (s - self.ring_seq[name, ring]) % size
        return self.ring_full[name, ring][s] + 16 * k * ((c - first) // size + 1) + j * (16 * k * (self.group[name] // size))

    def parity(self, name, step, c):
        return (self.base[name, step] + c) % 2


def make_plan():
    plan = Plan()

    def local(k):
        steps = [("sel_ready", 1), ("u_done", 2), ("u_out", 2), ("idx_up", 2 if k == 0 else 1)]
        rings = [("gat", 4, MR), ("dstb", 4, 1), ("ulo", 2, 1)]
        last = dict(pe="u_done", act="u_out", dve="sel_ready")
        if k == 0:
            steps += [("ea_added", 1)]
            rings += [("ea", 4, 1), ("own_in", 4, MR), ("own_out", 4, 1)]
        else:
            steps += [("sc", 1), ("esum", 1), ("e_ready", 1), ("eT", 1), ("scans", 1), ("mrow", 1),
                      ("mT", 1), ("d_ready", 1), ("w_ready", 1), ("m_kept", 1)]
            rings += [("pen", 4, HEADS[k])]
            if k == 5:
                steps += [("prod", 1)]
        plan.loop(f"L{k}", EDGE_MACROS, steps, rings, last)

    def mlp(layer):
        nh = HALVES[layer]
        return ([("xT_ps", 1), ("xT", 1), ("y_ps", 1), ("y_used", 1)] + ([("h_ps", nh), ("hT", nh)] if nh else [])
                + ([("z", 1)] if layer == 0 else []))

    norm = [("res2", 1), ("stats", 1), ("aggr", 1), ("lnv", 1), ("rstd", 1), ("shift", 1), ("x_ready", 1)]

    def dense(i):
        steps = mlp(i) + norm
        rings = [("xin", XIN, 1), ("xst", 4, 1)]
        if i > 0:
            steps += [("res1", 1)] if i < 3 else []
            rings += [("gst", 4, 1)]
        plan.loop(f"D{i}", NODE_MACROS, steps, rings, dict(pe="y_ps", act="x_ready", dve="shift"), 2 * MR,
                  beside=f"L{i}")

    def post(k):
        steps = [("p_ps", 2), ("p_used", 2)]
        slots = 4 if HEADS[k] == 1 else 2
        rings = [("uin", 4, 1), (f"car{slots}", slots, 2)]
        last = dict(pe="p_ps", dve="own_sum")
        if k < 5:
            rings += [("xs", 8, 1)]
        if k in (1, 2, 3, 4):
            steps += [("selfed", 1), ("rz", 1)]
        if k == 5:
            steps += [("zmax", 1), ("rz", 1)]
            last["dve"] = "shift"
        if k in (2, 4, 5):
            rings += [("xr", 4, 1)]
            steps += [("biased", 1)] + ([("un", 1)] if k == 5 else [])
        if k in (0, 1, 3):
            steps += [("u_ready", 1)]
        if k in MLP_LAYER:
            steps += mlp(MLP_LAYER[k])
            last.update(pe="y_ps", act="y_used" if k else "x_ready")
        if k in (0, 2, 4, 5):
            steps += norm
            if k != 4:
                last["act"] = "x_ready"
            if k < 5:
                rings += [("xst", 4, 1)]
            else:
                rings += [("out_sc", 4, MR)]
                steps += [("idx_up", 1)]
        if k in (1, 3, 4):
            rings += [("gst", 4, 1)]
        if k == 4:
            steps += [("own_prod", 1)]
        if k < 5:
            steps += [("own_sc", 1), ("own_sum", 1)]
        plan.loop(f"P{k}", EDGE_MACROS, steps, rings, last, 2 * MR)

    def combine(k):
        h = HEADS[k]
        steps = [("c_colb", 2 * h), ("c_row", 2 * h), ("c_mm", 2 * h), ("c_mb", 2 * h), ("c_dm", 2 * h),
                 ("c_wt", 2 * h), ("c_wtT_ps", 2 * h), ("c_wtT", 2 * h), ("c_sum_ps", 4 * h), ("c_sum", 4 * h),
                 ("c_mT", h + 1), ("c_arg", 2 * h), ("c_exp", 2 * h)]
        if k:
            steps += [("c_mT_ps", h + (k < 5)), ("c_t", 8 * h), ("c_back_ps", 2 * h), ("c_back", 2 * h)]
        plan.loop(f"C{k}", 1, steps, [("c_in", 1, 4), ("c_car", 1, 4), ("c_w0", 1, h), ("c_w1", 1, h)],
                  dict(pe="c_back_ps" if k else "c_sum_ps", act="c_exp", dve="c_back" if k else "c_arg"))

    local(0)
    dense(0)
    combine(0)
    post(0)
    for k in range(1, PHASES):
        local(k)
        if k < 4:
            dense(k)
        combine(k)
        post(k)
    return plan


def table_rows(table, first, count_per_partition):
    return table[bass.ds(first, P * MR), :].rearrange("(p u) d -> p u d", u=count_per_partition)


def edge_rows(table, first):
    return table[bass.ds(first, P * MR), :].rearrange("(u p) d -> p u d", p=P)


def wait(eng, semaphore, value):
    if isinstance(value, int) and value <= 0:
        return
    eng.wait_ge(semaphore, value)


def groups(eng, n, body, peel):
    whole = n // MR
    if peel:
        body(0, MR)
    with eng.Fori(1 if peel else 0, whole) as j:
        body(j, MR)
    if n % MR:
        body(whole, n % MR)


def pipeline(eng, plan, name, depth, slot, edges=None):
    n, size = plan.n[name], plan.group[name]
    first = 2 if name in ("D0", "P0") or depth > size else 1

    def step(at, edge):
        slot(at, edge) if edges else slot(at)

    def peeled(t):
        def at(lag):
            return [((t - lag) // size, (t - lag) % size)] if 0 <= t - lag < n else []

        def edge(lag):
            m = (t - lag) // 2
            return [(m // MR, m % MR)] if (t - lag) % 2 == 0 and 0 <= m < plan.n[edges] else []
        step(at, edge)

    def looped(j, t):
        def at(lag):
            return [(j, t - lag)]

        def edge(lag):
            return [(j, (t - lag) // 2)] if (t - lag) % 2 == 0 else []
        step(at, edge)

    for t in range(first * size):
        peeled(t)
    with eng.Fori(first, n // size) as j:
        for t in range(size):
            looped(j, t)
    for t in range(n // size * size, n + depth):
        peeled(t)


def before(j, c, n):
    return isinstance(j, int) and j == 0 and c < n


FIRST = {"L0", "L1", "L5"}


def build(nc, x, src, dst, ea, w):
    plan = make_plan()
    out = w["out"]

    with ExitStack() as ctx:
        def sb(name, shape, dt=F32):
            return ctx.enter_context(nc.sbuf_tensor(name, shape, dt))

        def ps(name, shape):
            return ctx.enter_context(nc.psum_tensor(name, shape, F32))

        def sem(name):
            return ctx.enter_context(nc.semaphore(name))

        def dram(name, shape, dt=F32):
            return nc.dram_tensor(name, shape, dt, kind="Internal").ap()

        table = {n: dram(f"table_{n}", (NODE_ROWS + SLOTS, D)) for n in ("x1", "g2", "x2", "g3", "x3", "g5")}
        x0_own = dram("x0_own", (SLOTS, D))
        node_map = dram("node_map", (NODE_ROWS, 1), I32)
        dst_f = dram("dst_f", (TILES, P))
        pens = dram("pens", (TILES, 2, P))
        tile_sums = dram("tile_sums", (SLOTS, ROW))
        carry = dram("carry", (2, TILES, ROW))
        carry_w = dram("carry_w", (2, TILES, 4, P))
        GATHER_FROM = [x, table["x1"], table["g2"], table["x2"], table["g3"], table["g5"]]
        OWN_FROM = [x0_own] + [table[n][NODE_ROWS:NODE_ROWS + SLOTS, :] for n in ("x1", "g2", "x2", "g3")]
        RES_FROM = {k: table[n][NODE_ROWS:NODE_ROWS + SLOTS, :] for k, n in ((2, "x1"), (4, "x2"), (5, "x3"))}
        X_TO = {0: "x1", 2: "x2", 4: "x3"}
        G_TO = {1: "g2", 3: "g3", 4: "g5"}

        ident = sb("ident", [P, P])
        W1 = {0: sb("w1_0", [P, 1, P]), 1: sb("w1_1", [P, 2, P]), 2: sb("w1_2", [P, 1, P])}
        W2 = {0: sb("w2_0", [P, 1, P]), 1: sb("w2_1", [P, 2, P]), 2: sb("w2_2", [P, 1, P])}
        W3 = sb("w3", [P, P])
        B1 = sb("b1", [P, 4])
        BCOL = {0: 0, 1: 1, 2: 3}
        BB = sb("bb", [P, 4, 1, P])
        VB = sb("vb", [P, 8, P])
        A5 = sb("a5", [P, 2, P])
        src_i = sb("src_i", [P, TILES], I32)
        dstm_i = sb("dstm_i", [P, TILES], I32)
        scat_i = sb("scat_i", [P, TILES], I32)
        row_i = sb("row_i", [P, TILES], I32)
        src_row = sb("src_row", [P, TILES], I32)
        dcol = sb("dcol", [P, TILES])
        a_dst = sb("a_dst", [P, 4, TILES])
        e_self = sb("e_self", [P, TILES])
        m_loc = sb("m_loc", [P, 4, TILES])
        c_loc = sb("c_loc", [P, 4, TILES])
        c_self = sb("c_self", [P, TILES])
        seg = sb("seg", [TB, 2, 2, P])
        cross = sb("cross", [TB, 2, 2, TILES])
        mT = sb("mT", [TB, 5, 2, P])
        ends = sb("ends", [TB, 2, 2, ROW])
        csum = sb("csum", [TB, 2, 2, ROW])
        colb = sb("colb", [TB, 2, TB])
        mm = sb("mm", [TB, 2, TILES])
        mB = sb("mB", [TB, 2, 2, 4])
        wt = sb("wt", [TB, 2, TILES])
        wtT = sb("wtT", [TB, 2, 2, TB])
        tmax = sb("tmax", [TB, 3, P])
        arg = sb("arg", [TB, 4, P])
        coef = sb("coef", [TB, 2, 4, P])
        gat = sb("gat", [P, 4, MR, ROW])
        sel = sb("sel", [P, 2, MR, P])
        junk = sb("junk", [P, 2 * MR, P])
        sc = sb("sc", [P, 4, MR, 1])
        es = sb("es", [P, 4, MR, 1])
        eb = sb("eb", [P, 2, 4, MR, 1])
        db = sb("db", [P, 4, MR, 1])
        wb = sb("wb", [P, 4, MR, 1])
        scan = sb("scan", [MR * 4, 2, P])
        mrow = sb("mrow", [MR * 4, P])
        ulo = sb("ulo", [P, 2, MR, ROW])
        xin = sb("xin", [P, XIN, MR, P])
        xT = sb("xT", [P, 2, MR * P])
        zb = sb("zb", [P, 2, MR * P])
        hT = sb("hT", [P, 2, 2, MR * P])
        gst = sb("gst", [P, 4, MR, P])
        rb = sb("rb", [P, 4, MR, P])
        st = sb("st", [P, 4, MR, 6])
        eps_c = sb("eps_c", [P, 1])
        mv = sb("mv", [P, 4, MR, 2])
        lnv = sb("lnv", [P, 4, MR])
        rstd = sb("rstd", [P, 4, MR, 1])
        neg_mean = sb("neg_mean", [P, 4, MR, 1])
        xst = sb("xst", [P, 4, MR, P])
        uin = sb("uin", [P, 4, MR, ROW])
        xs = sb("xs", [P, 8, MR, ROW])
        xr = sb("xr", [P, 4, MR, P])
        car_w = sb("car_w", [2, 2 * MR * 4 * P])
        car = sb("car", [2, 4, MR, ROW])
        t1 = sb("t1", [P, 2, MR, ROW])
        own_in, eab, dstb, gw = uin[:, :, :, 0:P], xs[:, 0:4, :, 0:P], xr, t1
        pen = zb[0:4 * MR].rearrange("t a (s b i) -> t (a s) b i", s=2, b=2)

        def car_ring(k):
            slots = 4 if HEADS[k] == 1 else 2
            return f"car{slots}", car_w[:, 0:slots * MR * HEADS[k] * P].rearrange(
                "d (s u h i) -> d s u h i", s=slots, u=MR, h=HEADS[k])
        rz = sb("rz", [P, MR, 4, 1])
        own_s = sb("own_s", [P, 2, MR])
        own_m = sb("own_m", [P, 4, MR])
        idx_st = sb("idx_st", [P, 4, MR], I32)
        idx_st2 = sb("idx_st2", [P, 4, MR], I32)
        map_ix = sb("map_ix", [P, 16], I32)
        map_v = sb("map_v", [P, 16], I32)
        pi = sb("pi", [TB, 3, 2, P], I32)
        pf = sb("pf", [TB, 4, 2, P])
        peq = xin[0:TB, 3].rearrange("t (a b) i -> t a b i", a=2)
        ppen = xin[0:TB, 4].rearrange("t (a b) i -> t a b i", a=2)
        w1T = xin[:, 0, 0:3, :]
        acol = sb("acol", [P, 6, 1])
        ab = xin[:, 1:3, :, :].rearrange("p s u d -> p (s u) d")[:, 0:6, :]
        ti_i = sb("ti_i", [TB, TILES], I32)
        tc_i = sb("tc_i", [TB, 1], I32)
        id_i = sb("id_i", [P, P], I32)
        map_i = sb("map_i", [P, NODE_ROWS // P], I32)
        ti = sb("ti", [TB, TILES])
        tcf = sb("tcf", [TB, 2])
        id_f = xin[:, 5, 0, :]

        psT = [ps(f"psT{i}", [P, 512]) for i in range(2)]
        psH = [ps(f"psH{i}", [P, 512]) for i in range(2)]
        psU = [ps(f"psU{i}", [P, 512]) for i in range(2)]
        psS, psY1 = ps("psS", [P, 512]), ps("psY1", [P, 512])
        psY = [psS, psY1]
        score_rows, score_cols = psT[1][:, 0:P], psT[1][:, P:P + 4 * MR]

        names = sorted({s for _, s in plan.base})
        S = {n: sem(n) for n in names}
        R = {r: [sem(f"{r}_full{i}") for i in range(size)] for r, size in plan.ring_size.items()}
        pre_fill, pre_load, w_load, pre_f, pre_v = map(sem, ("pre_fill", "pre_load", "w_load", "pre_f", "pre_v"))
        pre_ps, pre_tab, pre_st, pre_iota = map(sem, ("pre_ps", "pre_tab", "pre_st", "pre_iota"))
        pre_done, map_init, map_idx, map_dma = map(sem, ("pre_done", "map_init", "map_idx", "map_dma"))
        pre_pe = sem("pre_pe")
        map_read = sem("map_read")
        turn = {e: sem(f"turn_{e}") for e in ("pe", "act", "dve", "pool", "sp")}

        def enter(eng, name):
            for step, value in plan.before[name].values():
                wait(eng, S[step], value)

        def stored(eng, name, rings):
            for ring in rings:
                for i, value in enumerate(plan.stores[name].get(ring, [])):
                    wait(eng, R[ring][i], value)

        def own(eng, e):
            eng.sem_inc(turn[e], 1)

        def left(eng, name, ring, j, c):
            k = plan.ring_k[name, ring]
            wait(eng, R[ring][plan.slot(name, ring, c)], plan.full(name, ring, j, c) - 16 * k)

        b1s = (w["L0_gnn_b1"], w["L1_gnn_b1"][0:P], w["L1_gnn_b1"][P:2 * P], w["L2_gnn_b1"])
        a1s = (w["L1_gnn_a1_src"][0:P], w["L1_gnn_a1_src"][P:2 * P], w["L1_gnn_a1_dst"][0:P],
               w["L1_gnn_a1_dst"][P:2 * P], w["L2_gnn_a1_src"], w["L2_gnn_a1_dst"])
        att = w["L3_gnn_att"]
        weight_loads = [
            (W1[0][:, 0, :], w["L0_gnn_W1"]), (W2[0][:, 0, :], w["L0_gnn_W2"]),
            (W1[1][:].rearrange("p a d -> p (a d)"), w["L1_gnn_W1"]),
            (W2[1][:], w["L1_gnn_W2"].rearrange("(a p) d -> p a d", p=P)),
            (W1[2][:, 0, :], w["L2_gnn_W1"]), (W2[2][:, 0, :], w["L2_gnn_W2"]), (W3[:], w["L3_gnn_W"]),
        ]
        weight_loads += [(B1[:, i:i + 1], b.rearrange("(p o) -> p o", o=1)) for i, b in enumerate(b1s)]
        weight_loads += [(acol[:, i, :], a.rearrange("(p o) -> p o", o=1)) for i, a in enumerate(a1s)]
        weight_loads += [(BB[:, i, 0, :], w[n].rearrange("(o d) -> o d", o=1).to_broadcast([P, P]))
                         for i, n in enumerate(("L0_gnn_b2", "L1_gnn_b2", "L2_gnn_b2", "L3_gnn_bias"))]
        weight_loads += [(VB[:, i, :], w[n].rearrange("(o d) -> o d", o=1).to_broadcast([P, P]))
                         for i, n in ((2, "L1_gnn_a2_src"), (3, "L1_gnn_a2_dst"), (6, "L2_gnn_a2_src"),
                                      (7, "L2_gnn_a2_dst"))]
        weight_loads += [(A5[:, s, 32 * h:32 * h + 32], att[h:h + 1, 32 * s:32 * s + 32].to_broadcast([P, 32]))
                         for s in range(2) for h in range(4)]

        TAIL = EDGES - (TILES - 1) * P
        index_loads = []
        for i, (a, shift) in enumerate(((dst, 0), (dst, 1), (src, 0))):
            index_loads += [
                (pi[:, i, 0, :], a[shift:shift + TB * P].rearrange("(t i) -> t i", i=P)),
                (pi[0:TB - 1, i, 1, :], a[TB * P + shift:(TILES - 1) * P + shift].rearrange("(t i) -> t i", i=P)),
                (pi[TB - 1:TB, i, 1, 0:TAIL - shift],
                 a[(TILES - 1) * P + shift:EDGES].rearrange("(t i) -> t i", t=1)),
            ]

        block = ctx.enter_context(nc.Block())

        @block.sync
        def _(sp):
            for to, a in weight_loads:
                sp.dma_start(to, a, allow_slow_non_contiguous=True).then_inc(w_load, 16)
            sp.wait_ge(pre_fill, 3)
            for to, a in index_loads:
                sp.dma_start(to, a).then_inc(pre_load, 16)
            sp.wait_ge(pre_tab, 1)
            for b in range(2):
                sp.dma_start(dst_f[TB * b:TB * b + TB, :], pf[:, 0, b, :]).then_inc(pre_st, 16)
                sp.dma_start(pens[TB * b:TB * b + TB, :, :], ppen[:, b, :, :]).then_inc(pre_st, 16)
            sp.wait_ge(pre_st, 64)

            def first_row(name, j, c, start=0):
                return start + P * MR * c + j * (P * MR * plan.group[name])

            def local(k):
                name = f"L{k}"
                enter(sp, name)
                def load(j, c):
                    if not before(j, c, 4):
                        sp.wait_ge(S["sel_ready"], plan.seen(name, "sel_ready", j, c, back=4))
                        own(sp, "sp")
                    t = MR * c + j * (MR * MR)
                    s = plan.slot(name, "dstb", c)
                    sp.dma_start(dstb[:, s, :, :],
                                 dst_f[bass.ds(t, MR), :].rearrange("(o t) i -> o t i", o=1)
                                 .to_broadcast([P, MR, P])).then_inc(R["dstb"][s], 16)
                    if k == 0:
                        s = plan.slot(name, "ea", c)
                        if isinstance(j, int) and MR * j + c == EDGE_MACROS - 1:
                            whole = (EDGES - (EDGE_MACROS - 1) * MR * P) // P
                            r0 = (EDGE_MACROS - 1) * MR * P
                            assert whole == MR - 1
                            sp.dma_start(eab[:, s, 0:whole, :],
                                         ea[r0:r0 + whole * P, :].rearrange("(u p) d -> p u d", p=P)
                                         ).then_inc(R["ea"][s], 16)
                            sp.dma_start(eab[0:TAIL, s, whole, :], ea[r0 + whole * P:EDGES, :]
                                         ).then_inc(R["ea"][s], 16)
                        else:
                            sp.dma_start(eab[:, s, :, :], edge_rows(ea, first_row(name, j, c))
                                         ).then_inc(R["ea"][s], 16)
                    else:
                        if not before(j, c, 4):
                            sp.wait_ge(S["scans"], plan.seen(name, "scans", j, c, back=4))
                            own(sp, "sp")
                        s = plan.slot(name, "pen", c)
                        for h in range(HEADS[k]):
                            sp.dma_start(pen[MR * h:MR * h + MR, s, :, :], pens[bass.ds(t, MR), :, :]
                                         ).then_inc(R["pen"][s], 16)

                def store(j, c):
                    sp.wait_ge(S["u_out"], plan.seen(name, "u_out", j, c))
                    own(sp, "sp")
                    s = plan.slot(name, "ulo", c)
                    sp.dma_start(edge_rows(tile_sums, first_row(name, j, c)), ulo[:, s, :, :]).then_inc(R["ulo"][s], 16)
                    if k == 0:
                        sp.wait_ge(R["own_in"][plan.slot(name, "own_in", c)], plan.full(name, "own_in", j, c))
                        own(sp, "sp")
                        s = plan.slot(name, "own_out", c)
                        sp.dma_start(edge_rows(x0_own, first_row(name, j, c)), own_in[:, s, :, :]
                                     ).then_inc(R["own_out"][s], 16)
                if k < 4:
                    return load, store

                def slot(at):
                    for j, c in at(0):
                        load(j, c)
                    for j, c in at(3):
                        store(j, c)
                pipeline(sp, plan, name, 3, slot)

            def dense(i):
                name = f"D{i}"
                load_edges, store_edges = local(i)
                stored(sp, name, ("xst", "gst"))
                source = (x, table["x1"], table["x2"], table["x3"])[i]
                x_to = (table["x1"], table["x2"], table["x3"], out)[i]
                g_to = (None, table["g2"], table["g3"], table["g5"])[i]
                last_parts = (NODES - (NODE_MACROS - 1) * P * MR) // MR

                def load(j, c):
                    if not before(j, c, XIN):
                        sp.wait_ge(S["y_used" if i == 0 else "res2" if i == 3 else "res1"],
                                   plan.seen(name, "y_used" if i == 0 else "res2" if i == 3 else "res1", j, c, back=XIN))
                        own(sp, "sp")
                        sp.wait_ge(S["xT_ps"], plan.seen(name, "xT_ps", j, c, back=XIN))
                        own(sp, "sp")
                    s = plan.slot(name, "xin", c)
                    if i == 0 and isinstance(j, int) and 2 * MR * j + c == NODE_MACROS - 1:
                        sp.dma_start(xin[0:last_parts, s, :, :],
                                     x[NODES - last_parts * MR:NODES, :].rearrange("(p u) d -> p u d", u=MR)
                                     ).then_inc(R["xin"][s], 16)
                    else:
                        sp.dma_start(xin[:, s, :, :], table_rows(source, first_row(name, j, c), MR)
                                     ).then_inc(R["xin"][s], 16)

                def store_g(j, c):
                    sp.wait_ge(S["y_used"], plan.seen(name, "y_used", j, c))
                    own(sp, "sp")
                    s = plan.slot(name, "gst", c)
                    sp.dma_start(table_rows(g_to, first_row(name, j, c), MR), gst[:, s, :, :]
                                 ).then_inc(R["gst"][s], 16)

                def store_x(j, c):
                    sp.wait_ge(S["x_ready"], plan.seen(name, "x_ready", j, c))
                    own(sp, "sp")
                    s = plan.slot(name, "xst", c)
                    if i == 3 and isinstance(j, int) and 2 * MR * j + c == NODE_MACROS - 1:
                        sp.dma_start(out[NODES - last_parts * MR:NODES, :].rearrange("(p u) d -> p u d", u=MR),
                                     xst[0:last_parts, s, :, :]).then_inc(R["xst"][s], 16)
                    else:
                        sp.dma_start(table_rows(x_to, first_row(name, j, c), MR), xst[:, s, :, :]
                                     ).then_inc(R["xst"][s], 16)
                def slot(at, edge):
                    for j, c in at(0):
                        load(j, c)
                    for j, c in edge(0):
                        load_edges(j, c)
                    if i:
                        for j, c in at(5):
                            store_g(j, c)
                    for j, c in at(7):
                        store_x(j, c)
                    for j, c in edge(10 if i else 6):
                        store_edges(j, c)
                pipeline(sp, plan, name, 10 if i else 7, slot, f"L{i}")

            def combine(k):
                name = f"C{k}"
                enter(sp, name)
                stored(sp, name, ("ulo", "own_out") if k == 0 else ("ulo",))
                sums = tile_sums.rearrange("(t p) w -> t p w", p=P)
                for d in range(2):
                    for b in range(2):
                        row = P - 1 if d == 0 else 0
                        sp.dma_start(ends[:, d, b, :], sums[TB * b:TB * b + TB, row, :]).then_inc(R["c_in"][0], 16)
                for d in range(2):
                    sp.wait_ge(S["c_sum"], plan.seen(name, "c_sum", 0, 0, 4 * HEADS[k] - 1))
                    for b in range(2):
                        sp.dma_start(carry[d, TB * b:TB * b + TB, :], csum[:, d, b, :]).then_inc(R["c_car"][0], 16)
                for h in range(HEADS[k]):
                    for b in range(2):
                        r = 2 * h + b
                        sp.wait_ge(S["c_exp"], plan.seen(name, "c_exp", 0, 0, r))
                        sp.dma_start(carry_w[:, TB * b:TB * b + TB, h, :].rearrange("d t i -> t d i"),
                                     coef[:, r % 2, 1:3, :]).then_inc(R[f"c_w{r % 2}"][0], 16)

            def post(k):
                name = f"P{k}"
                enter(sp, name)
                stored(sp, name, ("xst", "gst"))
                stored(sp, name, ("c_car", "c_w0", "c_w1"))

                def load(j, c):
                    if not before(j, c, 4):
                        sp.wait_ge(S["p_used"], plan.seen(name, "p_used", j, c, back=4))
                        own(sp, "sp")
                    s = plan.slot(name, "uin", c)
                    sp.dma_start(uin[:, s, :, :], edge_rows(tile_sums, first_row(name, j, c))).then_inc(R["uin"][s], 16)
                    if k < 5:
                        if not before(j, c, 8):
                            sp.wait_ge(S["y_used" if k == 0 else "selfed"],
                                       plan.seen(name, "y_used" if k == 0 else "selfed", j, c, back=8))
                            own(sp, "sp")
                        s = plan.slot(name, "xs", c)
                        sp.dma_start(xs[:, s, :, 0:P], edge_rows(OWN_FROM[k], first_row(name, j, c))
                                     ).then_inc(R["xs"][s], 16)
                    if k in RES_FROM:
                        if not before(j, c, 4):
                            sp.wait_ge(S["res2"], plan.seen(name, "res2", j, c, back=4))
                            own(sp, "sp")
                        s = plan.slot(name, "xr", c)
                        sp.dma_start(xr[:, s, :, :], edge_rows(RES_FROM[k], first_row(name, j, c))
                                     ).then_inc(R["xr"][s], 16)

                def load_carries(j, c):
                    ring, weights = car_ring(k)
                    slots = plan.ring_size[ring]
                    if not before(j, c, slots):
                        sp.wait_ge(S["p_used"], plan.seen(name, "p_used", j, c, back=slots))
                        own(sp, "sp")
                    t = MR * c + j * (MR * plan.group[name])
                    s = plan.slot(name, ring, c)
                    sp.dma_start(weights[:, s, :, :, :], carry_w[:, bass.ds(t, MR), 0:HEADS[k], :]
                                 ).then_inc(R[ring][s], 16)
                    sp.dma_start(car[:, s, :, :], carry[:, bass.ds(t, MR), :]).then_inc(R[ring][s], 16)

                def store_x(j, c):
                    sp.wait_ge(S["x_ready"], plan.seen(name, "x_ready", j, c))
                    own(sp, "sp")
                    s = plan.slot(name, "xst", c)
                    sp.dma_start(edge_rows(table[X_TO[k]], first_row(name, j, c, NODE_ROWS)), xst[:, s, :, :]
                                 ).then_inc(R["xst"][s], 16)

                def store_g(j, c):
                    sp.wait_ge(S["y_used"], plan.seen(name, "y_used", j, c))
                    own(sp, "sp")
                    s = plan.slot(name, "gst", c)
                    sp.dma_start(edge_rows(table[G_TO[k]], first_row(name, j, c, NODE_ROWS)), gst[:, s, :, :]
                                 ).then_inc(R["gst"][s], 16)

                x_lag, g_lag = {0: 8, 2: 6, 4: 6}.get(k), {1: 6, 3: 6, 4: 8}.get(k)

                def slot(at):
                    for j, c in at(0):
                        load(j, c)
                        load_carries(j, c)
                    if k in X_TO:
                        for j, c in at(x_lag):
                            store_x(j, c)
                    if k in G_TO:
                        for j, c in at(g_lag):
                            store_g(j, c)
                pipeline(sp, plan, name, max(x_lag or 0, g_lag or 0), slot)

            sp.wait_ge(pre_done, 1)
            for k in range(PHASES):
                dense(k) if k < 4 else local(k)
                combine(k)
                post(k)
            for slots in (R["xst"], R["gst"], R["ulo"], R["own_out"], R["out_sc"]):
                for i, q in enumerate(slots):
                    ring = next(r for r in R if R[r] is slots)
                    wait(sp, q, plan.now_full[ring][i])

        @block.gpsimd
        def _(pool):
            nc.gpsimd.iota(id_i[:], pattern=[[1, P]], base=0, channel_multiplier=-1).then_inc(pre_iota, 1)
            nc.gpsimd.iota(ti_i[:], pattern=[[1, TILES]], base=0, channel_multiplier=0).then_inc(pre_iota, 1)
            nc.gpsimd.iota(tc_i[:], pattern=[[1, 1]], base=0, channel_multiplier=1).then_inc(pre_iota, 1)
            nc.gpsimd.iota(row_i[:], pattern=[[P, TILES]], base=NODE_ROWS, channel_multiplier=1).then_inc(pre_iota, 1)
            nc.gpsimd.iota(map_i[:], pattern=[[1, NODE_ROWS // P]], base=0, channel_multiplier=NODE_ROWS // P
                           ).then_inc(pre_iota, 1)
            pool.wait_ge(pre_iota, 5)
            pool.dma_start(node_map.rearrange("(p n) o -> p (n o)", p=P), map_i[:]).then_inc(map_init, 16)
            pool.wait_ge(pre_done, 1)

            ROUNDS = TILES // 16 + 1

            def look_up(j, c):
                ix = map_ix[:, MR * (c % 4):MR * (c % 4) + MR]
                nc.gpsimd.tensor_copy(ix, src_i[:, bass.ds(MR * c + j * (MR * MR), MR)]).then_inc(map_idx, 1)
                pool.wait_ge(map_idx, j * MR + (2 * ROUNDS + c + 1))
                own(pool, "pool")
                for u in range(MR * (c % 4), MR * (c % 4) + MR):
                    nc.gpsimd.indirect_dma_start(out=map_v[:, u:u + 1], out_offset=None, in_=node_map,
                                                 in_offset=bass.IndirectOffsetOnAxis(ap=map_ix[:, u:u + 1], axis=0)
                                                 ).then_inc(map_dma, 16)

            def keep_rows(j, c):
                pool.wait_ge(map_dma, j * (16 * MR * MR) + (16 * TILES + 16 * MR * (c + 1)))
                own(pool, "pool")
                nc.gpsimd.tensor_copy(src_row[:, bass.ds(MR * c + j * (MR * MR), MR)],
                                      map_v[:, MR * (c % 4):MR * (c % 4) + MR]).then_inc(map_read, 1)

            def gathers(k):
                name = f"L{k}"
                index = src_i if k == 0 else src_row
                if k:
                    stored(pool, name, ("xst", "gst"))
                    own(pool, "pool")

                def body(j, cs):
                    for c in range(cs):
                        more = not isinstance(j, int) or MR * j + c + 1 < EDGE_MACROS
                        if k == 1 and more:
                            look_up(j, c + 1)
                        cols = bass.ds(MR * c + j * (MR * MR), MR)
                        s = plan.slot(name, "gat", c)
                        if not before(j, c, 4):
                            pool.wait_ge(S["u_done"], plan.seen(name, "u_done", j, c, back=4))
                        if k == 0:
                            left(pool, name, "own_out", j, c)
                        own(pool, "pool")
                        if k == 1:
                            pool.wait_ge(map_read, j * MR + (c + 1))
                            own(pool, "pool")
                        nc.gpsimd.tensor_copy(idx_st[:, s, :], index[:, cols]).then_inc(S["idx_up"], 1)
                        if k == 0:
                            s2 = plan.slot(name, "own_in", c)
                            nc.gpsimd.tensor_copy(idx_st2[:, s2, :], dstm_i[:, cols]).then_inc(S["idx_up"], 1)
                        pool.wait_ge(S["idx_up"], plan.seen(name, "idx_up", j, c))
                        own(pool, "pool")
                        for u in range(MR):
                            nc.gpsimd.indirect_dma_start(
                                out=gat[:, s, u, 0:P], out_offset=None, in_=GATHER_FROM[k],
                                in_offset=bass.IndirectOffsetOnAxis(ap=idx_st[:, s, u:u + 1], axis=0)
                            ).then_inc(R["gat"][s], 16)
                        if k == 0:
                            for u in range(MR):
                                nc.gpsimd.indirect_dma_start(
                                    out=own_in[:, s2, u, :], out_offset=None, in_=x,
                                    in_offset=bass.IndirectOffsetOnAxis(ap=idx_st2[:, s2, u:u + 1], axis=0)
                                ).then_inc(R["own_in"][s2], 16)
                        if k == 1 and more:
                            keep_rows(j, c + 1)
                groups(pool, EDGE_MACROS, body, name in FIRST)

            def bias_residual(k):
                name, layer = f"P{k}", {2: 1, 4: 2, 5: 3}[k]

                def step(j, c):
                    rows = xr[:, plan.slot(name, "xr", c), :, :]
                    pool.wait_ge(R["xr"][plan.slot(name, "xr", c)], plan.full(name, "xr", j, c))
                    own(pool, "pool")
                    nc.gpsimd.tensor_tensor(rows, rows, BB[:, layer, :, :].to_broadcast([P, MR, P]), ALU.add
                                            ).then_inc(S["biased"], 1)
                return step

            def residuals(k):
                name, biased = f"P{k}", bias_residual(k)

                def slot(at):
                    for j, c in at(0):
                        biased(j, c)
                pipeline(pool, plan, name, 0, slot)

            def scatter_out():
                name, biased = "P5", bias_residual(5)

                def scatter(j, c):
                    s = plan.slot(name, "out_sc", c)
                    pool.wait_ge(S["x_ready"], plan.seen(name, "x_ready", j, c))
                    left(pool, name, "out_sc", j, c)
                    own(pool, "pool")
                    nc.gpsimd.tensor_copy(idx_st[:, s, :], scat_i[:, bass.ds(MR * c + j * (MR * plan.group[name]), MR)]
                                          ).then_inc(S["idx_up"], 1)
                    pool.wait_ge(S["idx_up"], plan.seen(name, "idx_up", j, c))
                    own(pool, "pool")
                    for u in range(MR):
                        nc.gpsimd.indirect_dma_start(
                            out=out, out_offset=bass.IndirectOffsetOnAxis(ap=idx_st[:, s, u:u + 1], axis=0),
                            in_=xst[:, s, u, :], in_offset=None, bounds_check=NODES - 1, oob_is_err=False
                        ).then_inc(R["out_sc"][s], 16)

                def slot(at):
                    for j, c in at(0):
                        biased(j, c)
                    for j, c in at(3):
                        scatter(j, c)
                pipeline(pool, plan, name, 3, slot)

            def map_round(start, n, done):
                cols = bass.ds(start, n)
                nc.gpsimd.tensor_copy(map_ix[:, 0:n], scat_i[:, cols]).then_inc(map_idx, 1)
                nc.gpsimd.tensor_copy(map_v[:, 0:n], row_i[:, cols]).then_inc(map_idx, 1)
                pool.wait_ge(map_idx, done * 2 + 2)
                own(pool, "pool")
                for u in range(n):
                    off = bass.IndirectOffsetOnAxis(ap=map_ix[:, u:u + 1], axis=0)
                    nc.gpsimd.indirect_dma_start(out=node_map, out_offset=off, in_=map_v[:, u:u + 1], in_offset=None,
                                                 bounds_check=NODE_ROWS - 1, oob_is_err=False).then_inc(map_dma, 16)
                pool.wait_ge(map_dma, done * 256 + 16 * n)
                own(pool, "pool")

            gathers(0)
            pool.wait_ge(map_init, 16)
            with pool.Fori(0, ROUNDS - 1) as r:
                map_round(r * 16, 16, r)
            map_round((ROUNDS - 1) * 16, TILES - 16 * (ROUNDS - 1), ROUNDS - 1)
            look_up(0, 0)
            keep_rows(0, 0)
            for k in range(1, PHASES):
                gathers(k)
                if k in (2, 4):
                    residuals(k)
            stored(pool, "P5", ("xst",))
            scatter_out()

        @block.tensor
        def _(pe):
            pe.wait_ge(pre_v, 1)
            pe.wait_ge(w_load, 16 * len(weight_loads))
            for i in range(2):
                nc.tensor.transpose(psH[0][:, P * i:P * i + P], W1[1][:, i, :], ident[:])
            nc.tensor.transpose(psH[0][:, 2 * P:3 * P], W1[2][:, 0, :], ident[:]).then_inc(pre_ps, 1)
            pe.wait_ge(pre_v, 2)
            for i in range(4):
                o = psH[1][:, P * i:P * i + P]
                if i < 2:
                    nc.tensor.matmul(o, ab[:, 2 * i, :], w1T[:, 0, :], start=True, stop=False)
                    last = nc.tensor.matmul(o, ab[:, 2 * i + 1, :], w1T[:, 1, :], start=False, stop=True)
                else:
                    last = nc.tensor.matmul(o, ab[:, 2 + i, :], w1T[:, 2, :], start=True, stop=True)
            last.then_inc(pre_ps, 1)
            pe.wait_ge(pre_v, 3)
            for i in range(4):
                for b in range(2):
                    last = nc.tensor.transpose(psT[i // 2][:, TILES * (i % 2) + TB * b:TILES * (i % 2) + TB * b + TB],
                                               pf[:, i, b, :], ident[0:TB, 0:TB])
            last.then_inc(pre_ps, 1)
            for d in range(2):
                pe.wait_ge(pre_v, 4 + d)
                for b in range(2):
                    last = nc.tensor.matmul(psY[d][0:TB, TB * b:TB * b + TB], colb[:, b, :],
                                            ident[0:TB, 0:TB], start=True, stop=True)
                last.then_inc(pre_ps, 1)
            pe.wait_ge(pre_done, 1)

            def local(k):
                name = f"L{k}"
                H, hw, wid = HEADS[k], HW[k], WID[k]
                enter(pe, name)

                def turn_scores(j, c):
                    pe.wait_ge(S["e_ready"], plan.seen(name, "e_ready", j, c))
                    own(pe, "pe")
                    nc.tensor.transpose(score_rows[0:MR * H, :], eb[:, c % 2, 0:H, :, 0].rearrange("p h u -> p (h u)"),
                                        ident[:]).then_inc(S["eT"], 1)

                def turn_maxima(j, c):
                    pe.wait_ge(S["mrow"], plan.seen(name, "mrow", j, c))
                    own(pe, "pe")
                    nc.tensor.transpose(score_cols[:, 0:MR * H], mrow[0:MR * H, :],
                                        ident[0:MR * H, 0:MR * H]).then_inc(S["mT"], 1)

                def sums(j, c):
                    pe.wait_ge(S["sel_ready"], plan.seen(name, "sel_ready", j, c))
                    g = plan.slot(name, "gat", c)
                    if k == 0:
                        pe.wait_ge(S["ea_added"], plan.seen(name, "ea_added", j, c))
                    for q in range(2):
                        if not before(j, c, 1):
                            pe.wait_ge(S["u_out"], plan.seen(name, "u_out", j, c, i=q, back=1))
                        for i in range(2):
                            u = 2 * q + i
                            rhs = gw[:, c % 2, u, 0:wid] if k == 5 else gat[:, g, u, 0:wid]
                            last = nc.tensor.matmul(psU[q][:, ROW * i:ROW * i + wid], sel[:, c % 2, u, :], rhs,
                                                    start=True, stop=True)
                        last.then_inc(S["u_done"], 1)

                if k < 4:
                    return turn_scores, turn_maxima, sums

                def slot(at):
                    for j, c in at(0):
                        turn_scores(j, c)
                        turn_maxima(j, c)
                    for j, c in at(1):
                        sums(j, c)
                pipeline(pe, plan, name, 1, slot)

            def mlp(name, layer, source):
                nh = HALVES[layer]

                def turn_rows(j, c):
                    s = plan.parity(name, "xT_ps", c)
                    if name[0] == "D":
                        pe.wait_ge(R["xin"][plan.slot(name, "xin", c)], plan.full(name, "xin", j, c))
                    elif name == "P4":
                        pe.wait_ge(S["x_ready"], plan.seen(name, "x_ready", j, c))
                    else:
                        pe.wait_ge(S["u_ready"], plan.seen(name, "u_ready", j, c))
                    bank = psT[0] if name[0] == "D" else psT[s]
                    banks = 1 if name[0] == "D" else 2
                    if not before(j, c, banks):
                        pe.wait_ge(S["xT"], plan.seen(name, "xT", j, c, back=banks))
                    for u in range(MR):
                        last = nc.tensor.transpose(bank[:, P * u:P * u + P], source(c, u), ident[:])
                    last.then_inc(S["xT_ps"], 1)

                def hidden(j, c):
                    s = plan.parity(name, "xT_ps", c)
                    pe.wait_ge(S["xT"], plan.seen(name, "xT", j, c))
                    for half in range(nh):
                        off = nh * c + half
                        if not before(j, off, 2):
                            pe.wait_ge(S["hT"], plan.base[name, "hT"] + off - 1 + j * (nh * plan.group[name]))
                        nc.tensor.matmul(psH[(plan.base[name, "h_ps"] + off) % 2][:], W1[layer][:, half, :],
                                         xT[:, s, :], start=True, stop=True).then_inc(S["h_ps"], 1)

                def second(j, c):
                    s = plan.parity(name, "xT_ps", c)
                    y = psY[plan.parity(name, "y_ps", c)]
                    pe.wait_ge(S["hT" if nh else "xT"], plan.seen(name, "hT" if nh else "xT", j, c))
                    if not before(j, c, 2):
                        pe.wait_ge(S["y_used"], plan.seen(name, "y_used", j, c, back=2))
                    for u in range(MR):
                        cols = slice(P * u, P * u + P)
                        if nh:
                            for half in range(nh):
                                last = nc.tensor.matmul(y[:, cols], hT[:, s, half, cols], W2[layer][:, half, :],
                                                        start=half == 0, stop=half == nh - 1)
                        else:
                            last = nc.tensor.matmul(y[:, cols], xT[:, s, cols], W3[:], start=True, stop=True)
                    last.then_inc(S["y_ps"], 1)

                return turn_rows, hidden, second

            def dense(i):
                name = f"D{i}"
                turn_scores, turn_maxima, sums = local(i)
                turn_rows, hidden, second = mlp(name, i, lambda c, u: xin[:, plan.slot(name, "xin", c), u, :])

                def slot(at, edge):
                    for j, c in at(0):
                        turn_rows(j, c)
                    if i < 3:
                        for j, c in at(1):
                            hidden(j, c)
                    for j, c in at(2 if i < 3 else 1):
                        second(j, c)
                    for j, c in edge(6 if i else 2):
                        sums(j, c)
                    if i:
                        for j, c in edge(1):
                            turn_scores(j, c)
                        for j, c in edge(3):
                            turn_maxima(j, c)
                pipeline(pe, plan, name, 6 if i else 2, slot, f"L{i}")

            def combine(k):
                name = f"C{k}"
                H, hw = HEADS[k], HW[k]
                enter(pe, name)
                if k:
                    for h in list(range(H)) + ([4] if k < 5 else []):
                        r = h if h < 4 else H
                        if r >= 2:
                            pe.wait_ge(S["c_mT"], plan.seen(name, "c_mT", 0, 0, r - 2))
                        for b in range(2):
                            a = e_self[:, TB * b:TB * b + TB] if h == 4 else m_loc[:, h, TB * b:TB * b + TB]
                            last = nc.tensor.transpose(psT[r % 2][0:TB, P * b:P * b + P], a, ident[:])
                        last.then_inc(S["c_mT_ps"], 1)
                pe.wait_ge(R["c_in"][0], plan.full(name, "c_in", 0, 0))
                for r in range(2 * H):
                    h, d = r // 2, r % 2
                    pe.wait_ge(S["c_colb"], plan.seen(name, "c_colb", 0, 0, r))
                    for b in range(2):
                        last = nc.tensor.matmul(psS[0:TB, TB * b:TB * b + TB], colb[:, b, :], ident[0:TB, 0:TB],
                                                start=True, stop=True)
                    last.then_inc(S["c_row"], 1)
                    pe.wait_ge(S["c_wt"], plan.seen(name, "c_wt", 0, 0, r))
                    for bt in range(2):
                        for b in range(2):
                            last = nc.tensor.transpose(psT[bt][0:TB, TB * b:TB * b + TB], wt[:, bt, TB * b:TB * b + TB],
                                                       ident[0:TB, 0:TB])
                    last.then_inc(S["c_wtT_ps"], 1)
                    pe.wait_ge(S["c_wtT"], plan.seen(name, "c_wtT", 0, 0, r))
                    for bt in range(2):
                        if r:
                            pe.wait_ge(S["c_sum"], plan.seen(name, "c_sum", 0, 0, 2 * (r - 1) + bt))
                        o = psH[bt][0:TB, 0:hw]
                        for b in range(2):
                            last = nc.tensor.matmul(o, wtT[:, bt, b, :], ends[:, d, b, hw * h:hw * h + hw],
                                                    start=b == 0, stop=b == 1)
                        last.then_inc(S["c_sum_ps"], 1)
                if k:
                    for r in range(2 * H):
                        pe.wait_ge(S["c_exp"], plan.seen(name, "c_exp", 0, 0, r))
                        if r >= 2:
                            pe.wait_ge(S["c_back"], plan.seen(name, "c_back", 0, 0, r - 2))
                        last = nc.tensor.transpose(psT[r % 2][:, 0:TB], coef[:, r % 2, 0, :], ident[0:TB, 0:TB])
                        if k < 5:
                            last = nc.tensor.transpose(psT[r % 2][:, P:P + TB], coef[:, r % 2, 3, :],
                                                       ident[0:TB, 0:TB])
                        last.then_inc(S["c_back_ps"], 1)

            def post(k):
                name = f"P{k}"
                H, hw, wid = HEADS[k], HW[k], WID[k]
                enter(pe, name)

                def carries(j, c):
                    ring, weights = car_ring(k)
                    pe.wait_ge(R[ring][plan.slot(name, ring, c)], plan.full(name, ring, j, c))
                    s = plan.slot(name, ring, c)
                    for q in range(2):
                        if not before(j, c, 1):
                            pe.wait_ge(S["p_used"], plan.seen(name, "p_used", j, c, i=q, back=1))
                        own(pe, "pe")
                        for i in range(2):
                            u = 2 * q + i
                            for h in range(H):
                                last = nc.tensor.matmul(
                                    psU[q][:, ROW * i + hw * h:ROW * i + hw * h + hw], weights[:, s, u, h, :],
                                    car[:, s, u, hw * h:hw * h + hw], start=True, stop=True)
                        last.then_inc(S["p_ps"], 1)

                if k in (0, 1, 3):
                    turn_rows, hidden, second = mlp(name, MLP_LAYER[k], lambda c, u: xin[:, c % 4, u, :])
                if k == 4:
                    turn_rows, hidden, second = mlp(name, 3, lambda c, u: xst[:, plan.slot(name, "xst", c), u, :])

                def slot(at):
                    for j, c in at(0):
                        carries(j, c)
                    if k in (0, 1, 3):
                        for j, c in at(1):
                            turn_rows(j, c)
                        for j, c in at(2):
                            hidden(j, c)
                        for j, c in at(3):
                            second(j, c)
                    if k == 4:
                        for j, c in at(4):
                            turn_rows(j, c)
                        for j, c in at(5):
                            second(j, c)
                pipeline(pe, plan, name, {0: 3, 1: 3, 3: 3, 4: 5}.get(k, 0), slot)

            for k in range(PHASES):
                dense(k) if k < 4 else local(k)
                combine(k)
                post(k)

        @block.scalar
        def _(act):
            nc.scalar.preload_act_table_set("natural_log_exp_and_others")
            act.wait_ge(w_load, 16 * len(weight_loads))
            act.wait_ge(pre_v, 1)

            def local(k):
                name = f"L{k}"
                H, wid = HEADS[k], WID[k]
                enter(act, name)

                def weights(j, c):
                    act.wait_ge(S["d_ready"], plan.seen(name, "d_ready", j, c))
                    nc.scalar.activation(wb[:, 0:H, :, :], db[:, 0:H, :, :], ACT.Exp).then_inc(S["w_ready"], 1)

                def move_sums(j, c):
                    s = plan.slot(name, "ulo", c)
                    if not before(j, c, 2):
                        left(act, name, "ulo", j, c)
                    for q in range(2):
                        act.wait_ge(S["u_done"], plan.seen(name, "u_done", j, c, i=q))
                        nc.scalar.copy(ulo[:, s, 2 * q:2 * q + 2, 0:wid],
                                       psU[q][:, 0:2 * ROW].rearrange("p (u w) -> p u w", u=2)[:, :, 0:wid]
                                       ).then_inc(S["u_out"], 1)

                if k < 4:
                    return weights, move_sums

                def slot(at):
                    for j, c in at(0):
                        weights(j, c)
                    for j, c in at(1):
                        move_sums(j, c)
                pipeline(act, plan, name, 1, slot)

            def mlp(name, layer, g_free):
                nh = HALVES[layer]

                def turned(j, c):
                    s = plan.parity(name, "xT_ps", c)
                    act.wait_ge(S["xT_ps"], plan.seen(name, "xT_ps", j, c))
                    if not before(j, c, 2):
                        act.wait_ge(S["h_ps" if nh else "y_ps"],
                                    plan.seen(name, "h_ps" if nh else "y_ps", j, c, back=2))
                    nc.scalar.copy(xT[:, s, :], psT[0 if name[0] == "D" else s][:]).then_inc(S["xT"], 1)

                def hidden(j, c):
                    s = plan.parity(name, "xT_ps", c)
                    for half in range(nh):
                        off = nh * c + half
                        act.wait_ge(S["h_ps"], plan.seen(name, "h_ps", j, c, i=half))
                        if half == 0 and not before(j, c, 2):
                            act.wait_ge(S["hT" if layer == 0 else "y_ps"],
                                        plan.seen(name, "hT" if layer == 0 else "y_ps", j, c, back=2))
                        bank = psH[(plan.base[name, "h_ps"] + off) % 2]
                        bias = B1[:, BCOL[layer] + half:BCOL[layer] + half + 1]
                        if layer == 0:
                            nc.scalar.activation(zb[:, s, :], bank[:], ACT.Identity, bias=bias, scale=2.0
                                                 ).then_inc(S["z"], 1)
                        else:
                            nc.scalar.activation(hT[:, s, half, :], bank[:], ACT.Relu, bias=bias, scale=1.0
                                                 ).then_inc(S["hT"], 1)

                def second(j, c):
                    s = plan.slot(name, "gst", c)
                    if not before(j, c, 4):
                        g_free(j, c)
                    left(act, name, "gst", j, c)
                    act.wait_ge(S["y_ps"], plan.seen(name, "y_ps", j, c))
                    nc.scalar.copy(gst[:, s, :, :], psY[plan.parity(name, "y_ps", c)][:].rearrange(
                        "p (u d) -> p u d", u=MR)).then_inc(S["y_used"], 1)

                return turned, hidden, second

            def norm(name, ring):
                def root(j, c):
                    act.wait_ge(S["aggr"], plan.seen(name, "aggr", j, c))
                    nc.scalar.activation(lnv[:, c % 4, :], mv[:, c % 4, :, 1], ACT.Ln, bias=eps_c[:],
                                         scale=1.0).then_inc(S["lnv"], 1)
                    act.wait_ge(S["lnv"], plan.seen(name, "lnv", j, c))
                    nc.scalar.activation(rstd[:, c % 4, :, 0], lnv[:, c % 4, :], ACT.Exp, scale=-0.5
                                         ).then_inc(S["rstd"], 1)

                def rows(j, c):
                    s = plan.slot(name, ring, c)
                    left(act, name, ring, j, c)
                    if not before(j, c, 4):
                        if name == "P4":
                            act.wait_ge(S["xT_ps"], plan.seen(name, "xT_ps", j, c, back=4))
                        if name in ("P0", "P2"):
                            act.wait_ge(S["own_sc"], plan.seen(name, "own_sc", j, c, back=4))
                    act.wait_ge(S["shift"], plan.seen(name, "shift", j, c))
                    for u in range(MR):
                        last = nc.scalar.activation(xst[:, s, u, :], rb[:, c % 4, u, :], ACT.Identity,
                                                    bias=neg_mean[:, c % 4, u, :], scale=rstd[:, c % 4, u, :])
                    last.then_inc(S["x_ready"], 1)
                return root, rows

            def dense(i):
                name = f"D{i}"
                weights, move_sums = local(i)

                def g_free(j, c):
                    if i < 3:
                        act.wait_ge(S["res1"], plan.seen(name, "res1", j, c, back=4))

                turned, hidden, second = mlp(name, i, g_free)
                root, rows = norm(name, "xst")

                def slot(at, edge):
                    for j, c in at(4):
                        root(j, c)
                    for j, c in edge(7 if i else 3):
                        move_sums(j, c)
                    for j, c in at(0):
                        turned(j, c)
                    if i < 3:
                        for j, c in at(1):
                            hidden(j, c)
                    if i:
                        for j, c in edge(5):
                            weights(j, c)
                    for j, c in at(5):
                        rows(j, c)
                    if i:
                        for j, c in at(2 if i < 3 else 1):
                            second(j, c)
                pipeline(act, plan, name, 7 if i else 5, slot, f"L{i}")

            def combine(k):
                name = f"C{k}"
                H = HEADS[k]
                enter(act, name)
                for r in range(2 * H):
                    act.wait_ge(S["c_dm"], plan.seen(name, "c_dm", 0, 0, r))
                    nc.scalar.activation(wt[:], mm[:], ACT.Exp).then_inc(S["c_wt"], 1)
                for r in range(2 * H):
                    act.wait_ge(S["c_arg"], plan.seen(name, "c_arg", 0, 0, r))
                    if r >= 2:
                        if k:
                            act.wait_ge(S["c_back_ps"], plan.seen(name, "c_back_ps", 0, 0, r - 2))
                        ring = f"c_w{r % 2}"
                        act.wait_ge(R[ring][0], plan.full(name, ring, 0, 0) - 16 * H + 16 * (r // 2))
                    lo, hi = (1, 3) if k == 0 else (0, 3) if k == 5 else (0, 4)
                    nc.scalar.activation(coef[:, r % 2, lo:hi, :], arg[:, lo:hi, :], ACT.Exp).then_inc(S["c_exp"], 1)

            def post(k):
                name = f"P{k}"
                enter(act, name)

                def g_free(j, c):
                    act.wait_ge(S["own_prod" if k == 4 else "own_sc"],
                                plan.seen(name, "own_prod" if k == 4 else "own_sc", j, c, back=4))

                root, rows = norm(name, "out_sc" if k == 5 else "xst")
                if k == 5:
                    stored(act, name, ("xst",))
                if k in MLP_LAYER:
                    turned, hidden, second = mlp(name, MLP_LAYER[k], g_free)

                def slot(at):
                    if k in (0, 2, 4, 5):
                        for j, c in at(5 if k == 0 else 2):
                            root(j, c)
                        for j, c in at(6 if k == 0 else 3):
                            rows(j, c)
                    if k in MLP_LAYER:
                        for j, c in at(4 if k == 4 else 1):
                            turned(j, c)
                        if k < 4:
                            for j, c in at(2):
                                hidden(j, c)
                        if k:
                            for j, c in at(5 if k == 4 else 3):
                                second(j, c)
                pipeline(act, plan, name, {0: 6, 1: 3, 2: 3, 3: 3, 4: 5, 5: 3}[k], slot)

            for k in range(PHASES):
                dense(k) if k < 4 else local(k)
                combine(k)
                post(k)

        @block.vector
        def _(dve):
            vec = nc.vector
            vec.memset(pi[:, 0:2, :, :], NODES)
            vec.memset(pi[:, 2, :, :], 0)
            vec.memset(ulo[:], 0.0).then_inc(pre_fill, 3)
            vec.memset(gat[:, :, :, P:ROW], 1.0)
            vec.memset(xs[:, :, :, P:ROW], 1.0)
            vec.memset(mT[:], 0.0)
            vec.memset(csum[:], 0.0)
            vec.memset(ppen, -BIG)
            vec.memset(eps_c[:], EPS)
            dve.wait_ge(pre_iota, 5)
            vec.tensor_copy(id_f, id_i[:])
            vec.tensor_copy(ti[:], ti_i[:])
            vec.tensor_copy(tcf[:, 0:1], tc_i[:]).then_inc(pre_f, 1)
            dve.wait_ge(pre_f, 1)
            vec.tensor_scalar(tcf[:, 1:2], tcf[:, 0:1], float(TB), None, ALU.add).then_inc(pre_f, 1)
            vec.tensor_scalar(ident[:], id_f, 0.0, None, ALU.is_equal).then_inc(pre_v, 1)
            dve.wait_ge(w_load, 16 * len(weight_loads))
            vec.tensor_copy(ab, acol[:].to_broadcast([P, 6, P]))
            dve.wait_ge(pre_ps, 1)
            vec.tensor_copy(w1T.rearrange("p a d -> p (a d)"), psH[0][:, 0:3 * P]).then_inc(pre_v, 1)
            dve.wait_ge(pre_ps, 2)
            vec.tensor_copy(VB[:, 0:2, :].rearrange("p a d -> p (a d)"), psH[1][:, 0:2 * P])
            vec.tensor_copy(VB[:, 4:6, :].rearrange("p a d -> p (a d)"), psH[1][:, 2 * P:4 * P]).then_inc(pre_f, 1)
            dve.wait_ge(pre_load, 16 * len(index_loads))
            dve.wait_ge(pre_f, 3)
            vec.tensor_copy(pf[:, 0, :, :], pi[:, 0, :, :])
            vec.tensor_copy(pf[:, 1, :, :], pi[:, 1, :, :])
            vec.tensor_copy(pf[:, 3, :, :], pi[:, 2, :, :]).then_inc(pre_f, 1)
            dve.wait_ge(pre_f, 4)
            vec.tensor_tensor(peq[:, 0, :, :], pf[:, 0, :, :], pf[:, 1, :, :], ALU.is_equal).then_inc(pre_f, 1)
            dve.wait_ge(pre_f, 5)
            vec.scalar_tensor_tensor(out=pf[:, 1, :, :], in0=peq[:, 0, :, :], scalar=SKIP, in1=pf[:, 0, :, :],
                                     op0=ALU.mult, op1=ALU.add)
            vec.tensor_scalar(pf[:, 2, :, :], pf[:, 0, :, :], float(NODES - 1), None, ALU.min).then_inc(pre_v, 1)
            vec.tensor_tensor(peq[:, 1, :, 1:P], pf[:, 0, :, 1:P], pf[:, 0, :, 0:P - 1], ALU.not_equal
                              ).then_inc(pre_f, 1)
            dve.wait_ge(pre_f, 6)
            vec.tensor_scalar(ppen[:, :, 0, 1:P], peq[:, 1, :, 1:P], -BIG, None, ALU.mult)
            vec.tensor_scalar(ppen[:, :, 1, 0:P - 1], peq[:, 1, :, 1:P], -BIG, None, ALU.mult).then_inc(pre_tab, 1)
            for d in range(2):
                col = 0 if d == 0 else P - 1
                for b in range(2):
                    vec.tensor_scalar(seg[:, d, b, :], pf[:, 0, b, :], pf[:, 0, b, col:col + 1], -BIG,
                                      ALU.not_equal, ALU.mult)
            dve.wait_ge(pre_ps, 3)
            vec.tensor_copy(dcol[:], psT[0][:, 0:TILES])
            vec.tensor_copy(scat_i[:], psT[0][:, TILES:2 * TILES])
            vec.tensor_copy(dstm_i[:], psT[1][:, 0:TILES])
            vec.tensor_copy(src_i[:], psT[1][:, TILES:2 * TILES]).then_inc(pre_f, 1)
            for d in range(2):
                col = P - 1 if d == 0 else 0
                for b in range(2):
                    last = vec.tensor_copy(colb[:, b, :], pf[:, 0, b, col:col + 1].to_broadcast([TB, TB]))
                last.then_inc(pre_v, 1)
                dve.wait_ge(pre_ps, 4 + d)
                bank = psY[d]
                other = 0 if d == 0 else P - 1
                for b in range(2):
                    vec.tensor_scalar(mm[:, b, :], bank[0:TB, 0:TILES], pf[:, 0, b, other:other + 1], -BIG,
                                      ALU.not_equal, ALU.mult)
                    last = vec.tensor_scalar(wt[:, b, :], ti[:], tcf[:, b:b + 1], -BIG,
                                             ALU.is_ge if d == 0 else ALU.is_le, ALU.mult)
                last.then_inc(pre_f, 1)
                dve.wait_ge(pre_f, 8 + 2 * d)
                vec.tensor_tensor(cross[:, d, :, :], mm[:], wt[:], ALU.add).then_inc(pre_f, 1)
                dve.wait_ge(pre_f, 9 + 2 * d)
            vec.memset(id_f[:, 0:1], 0.0).then_inc(pre_done, 1)

            def local(k):
                name = f"L{k}"
                H = HEADS[k]
                enter(dve, name)

                def add_edges(j, c):
                    g = plan.slot(name, "gat", c)
                    dve.wait_ge(R["gat"][g], plan.full(name, "gat", j, c))
                    dve.wait_ge(R["ea"][plan.slot(name, "ea", c)], plan.full(name, "ea", j, c))
                    if isinstance(j, int) and MR * j + c == EDGE_MACROS - 1:
                        s = plan.slot(name, "ea", c)
                        dve.wait_ge(R["ea"][s], plan.full(name, "ea", j, c) + 16)
                    vec.tensor_tensor(gat[:, g, :, 0:P], gat[:, g, :, 0:P], eab[:, plan.slot(name, "ea", c), :, :],
                                      ALU.add).then_inc(S["ea_added"], 1)

                def scores(j, c):
                    g = plan.slot(name, "gat", c)
                    cols = bass.ds(MR * c + j * (MR * MR), MR)
                    dve.wait_ge(R["gat"][g], plan.full(name, "gat", j, c))
                    if k < 5:
                        for u in range(MR):
                            last = vec.tensor_tensor_reduce(junk[:, u, :], gat[:, g, u, 0:P], VB[:, 2 * (k - 1), :],
                                                            1.0, 0.0, ALU.mult, ALU.add, sc[:, 0, u, :])
                        last.then_inc(S["sc"], 1)
                    else:
                        vec.tensor_tensor(junk[:, 0:MR, :], gat[:, g, :, 0:P],
                                          A5[:, 0:1, :].to_broadcast([P, MR, P]), ALU.mult).then_inc(S["prod"], 1)
                        dve.wait_ge(S["prod"], plan.seen(name, "prod", j, c))
                        vec.tensor_reduce(sc[:, :, :, 0].rearrange("p h u -> p u h"),
                                          junk[:, 0:MR, :].rearrange("p u (h e) -> p u h e", h=4), AX.X, ALU.add
                                          ).then_inc(S["sc"], 1)
                    dve.wait_ge(S["sc"], plan.seen(name, "sc", j, c))
                    vec.tensor_tensor(es[:, 0:H, :, 0], sc[:, 0:H, :, 0], a_dst[:, 0:H, cols], ALU.add
                                      ).then_inc(S["esum"], 1)
                    dve.wait_ge(S["esum"], plan.seen(name, "esum", j, c))
                    vec.scalar_tensor_tensor(out=eb[:, c % 2, 0:H, :, 0], in0=es[:, 0:H, :, 0], scalar=SLOPE,
                                             in1=es[:, 0:H, :, 0], op0=ALU.mult, op1=ALU.max
                                             ).then_inc(S["e_ready"], 1)

                def maxima(j, c):
                    n, s = MR * H, plan.slot(name, "pen", c)
                    dve.wait_ge(R["pen"][s], plan.full(name, "pen", j, c))
                    dve.wait_ge(S["eT"], plan.seen(name, "eT", j, c))
                    rows = score_rows[0:n, :]
                    vec.tensor_tensor_scan(scan[0:n, 0, :], pen[0:n, s, 0, :], rows, -BIG, ALU.add, ALU.max)
                    vec.tensor_tensor_scan(scan[0:n, 1, ::-1], pen[0:n, s, 1, ::-1], rows[:, ::-1], -BIG,
                                           ALU.add, ALU.max).then_inc(S["scans"], 1)
                    dve.wait_ge(S["scans"], plan.seen(name, "scans", j, c))
                    vec.tensor_tensor(mrow[0:n, :], scan[0:n, 0, :], scan[0:n, 1, :], ALU.max
                                      ).then_inc(S["mrow"], 1)

                def less_maximum(j, c):
                    cols = bass.ds(MR * c + j * (MR * MR), MR)
                    dve.wait_ge(S["mT"], plan.seen(name, "mT", j, c))
                    back = score_cols[:, 0:MR * H].rearrange("p (h u) -> p h u", h=H)
                    vec.tensor_tensor(db[:, 0:H, :, 0], eb[:, c % 2, 0:H, :, 0], back, ALU.subtract
                                      ).then_inc(S["d_ready"], 1)
                    vec.tensor_scalar(m_loc[:, 0:H, cols], back, 0.0, None, ALU.add).then_inc(S["m_kept"], 1)

                def selection(j, c):
                    g, sd = plan.slot(name, "gat", c), plan.slot(name, "dstb", c)
                    dve.wait_ge(R["dstb"][sd], plan.full(name, "dstb", j, c))
                    if not before(j, c, 2):
                        dve.wait_ge(S["u_done"], plan.seen(name, "u_done", j, c, back=2))
                    if k:
                        dve.wait_ge(S["w_ready"], plan.seen(name, "w_ready", j, c))
                    if k == 5:
                        o = gw[:, c % 2, :, :].rearrange("p u (h e) -> p u h e", h=4)
                        vec.tensor_tensor(o[:, :, :, 0:32], gat[:, g, :, 0:P].rearrange("p u (h e) -> p u h e", h=4),
                                          wb[:].rearrange("p h u o -> p u h o").to_broadcast([P, MR, 4, 32]),
                                          ALU.mult)
                        vec.tensor_copy(o[:, :, :, 32:33], wb[:].rearrange("p h u o -> p u h o"))
                    for u in range(MR):
                        col = dcol[:, bass.ds(MR * c + u + j * (MR * MR), 1)]
                        if k in (0, 5):
                            last = vec.tensor_scalar(sel[:, c % 2, u, :], dstb[:, sd, u, :], col, None, ALU.is_equal)
                        else:
                            last = vec.tensor_scalar(sel[:, c % 2, u, :], dstb[:, sd, u, :], col, wb[:, 0, u, :],
                                                     ALU.is_equal, ALU.mult)
                    last.then_inc(S["sel_ready"], 1)

                if k < 4:
                    return add_edges, scores, maxima, less_maximum, selection

                def slot(at):
                    for j, c in at(0):
                        scores(j, c)
                    for j, c in at(1):
                        selection(j, c)
                    for j, c in at(0):
                        maxima(j, c)
                        less_maximum(j, c)
                pipeline(dve, plan, name, 1, slot)

            def norm(name):
                def stats(j, c):
                    dve.wait_ge(S["res2"], plan.seen(name, "res2", j, c))
                    for u in range(MR):
                        last = vec.bn_stats(st[:, c % 4, u, :], rb[:, c % 4, u, :])
                    last.then_inc(S["stats"], 1)

                def mean_variance(j, c):
                    dve.wait_ge(S["stats"], plan.seen(name, "stats", j, c))
                    own(dve, "dve")
                    for u in range(MR):
                        last = vec.bn_aggr(mv[:, c % 4, u, :], st[:, c % 4, u, :])
                    last.then_inc(S["aggr"], 1)

                def shift_rows(j, c):
                    dve.wait_ge(S["rstd"], plan.seen(name, "rstd", j, c))
                    vec.scalar_tensor_tensor(out=neg_mean[:, c % 4, :, 0], in0=mv[:, c % 4, :, 0], scalar=-1.0,
                                             in1=rstd[:, c % 4, :, 0], op0=ALU.mult, op1=ALU.mult
                                             ).then_inc(S["shift"], 1)
                return shift_rows, stats, mean_variance

            def rows_free(name, j, c):
                if not before(j, c, 4):
                    dve.wait_ge(S["x_ready"], plan.seen(name, "x_ready", j, c, back=4))

            def leaky(name):
                def step(j, c):
                    s = plan.parity(name, "xT_ps", c)
                    dve.wait_ge(S["z"], plan.seen(name, "z", j, c))
                    if not before(j, c, 2):
                        dve.wait_ge(S["y_ps"], plan.seen(name, "y_ps", j, c, back=2))
                    vec.scalar_tensor_tensor(out=hT[:, s, 0, :], in0=zb[:, s, :], scalar=0.01, in1=zb[:, s, :],
                                             op0=ALU.mult, op1=ALU.max).then_inc(S["hT"], 1)
                return step

            def add_bias(name, layer):
                def step(j, c):
                    r = rb[:, c % 4, :, :]
                    if name == "D3":
                        rows_free(name, j, c)
                        dve.wait_ge(R["xin"][plan.slot(name, "xin", c)], plan.full(name, "xin", j, c))
                        source = xin[:, plan.slot(name, "xin", c), :, :]
                    else:
                        dve.wait_ge(S["y_used" if layer == 0 else "res1"],
                                    plan.seen(name, "y_used" if layer == 0 else "res1", j, c))
                        source = r
                    vec.tensor_tensor(r, source, BB[:, layer, :, :].to_broadcast([P, MR, P]), ALU.add
                                      ).then_inc(S["res2"], 1)
                return step

            def add_product(name, own_rows):
                def step(j, c):
                    rows_free(name, j, c)
                    dve.wait_ge(S["y_ps"], plan.seen(name, "y_ps", j, c))
                    vec.tensor_tensor(rb[:, c % 4, :, :], psY[plan.parity(name, "y_ps", c)][:].rearrange(
                        "p (u d) -> p u d", u=MR), own_rows(c), ALU.add).then_inc(S["y_used"], 1)
                return step

            def dense(i):
                name = f"D{i}"
                add_edges, scores, maxima, less_maximum, selection = local(i)

                def rows_in(c):
                    return xin[:, plan.slot(name, "xin", c), :, :]

                def add_g(j, c):
                    rows_free(name, j, c)
                    dve.wait_ge(S["y_used"], plan.seen(name, "y_used", j, c))
                    vec.tensor_tensor(rb[:, c % 4, :, :], gst[:, plan.slot(name, "gst", c), :, :], rows_in(c), ALU.add
                                      ).then_inc(S["res1"], 1)

                shift_rows, stats, mean_variance = norm(name)
                bias, leak, add_y = add_bias(name, i), leaky(name), add_product(name, rows_in)

                def slot_0(at):
                    for j, c in at(4):
                        shift_rows(j, c)
                    for j, c in at(1):
                        leak(j, c)
                    for j, c in at(2):
                        add_y(j, c)
                    for j, c in at(2):
                        bias(j, c)
                    for j, c in at(2):
                        stats(j, c)
                    for j, c in at(2):
                        mean_variance(j, c)

                def slot_1_2(at):
                    for j, c in at(4):
                        shift_rows(j, c)
                    for j, c in at(2):
                        add_g(j, c)
                    for j, c in at(2):
                        bias(j, c)
                    for j, c in at(2):
                        stats(j, c)
                    for j, c in at(2):
                        mean_variance(j, c)

                def slot_3(at):
                    for j, c in at(4):
                        shift_rows(j, c)
                    for j, c in at(2):
                        bias(j, c)
                    for j, c in at(2):
                        stats(j, c)
                    for j, c in at(2):
                        mean_variance(j, c)

                def slot(at, edge):
                    if i:
                        for j, c in edge(4):
                            less_maximum(j, c)
                        for j, c in edge(2):
                            maxima(j, c)
                        for j, c in edge(0):
                            scores(j, c)
                        for j, c in edge(5):
                            selection(j, c)
                    else:
                        for j, c in edge(1):
                            selection(j, c)
                    (slot_0, slot_1_2, slot_1_2, slot_3)[i](at)
                    if i == 0:
                        for j, c in edge(0):
                            add_edges(j, c)
                pipeline(dve, plan, name, 5, slot, f"L{i}")

            def combine(k):
                name = f"C{k}"
                H, hw = HEADS[k], HW[k]
                enter(dve, name)

                def at(step, r):
                    dve.wait_ge(S[step], plan.seen(name, step, 0, 0, r))

                if k:
                    for h in list(range(H)) + ([4] if k < 5 else []):
                        r = h if h < 4 else H
                        at("c_mT_ps", r)
                        vec.tensor_copy(mT[:, h, :, :].rearrange("p b i -> p (b i)"), psT[r % 2][0:TB, 0:2 * P]
                                        ).then_inc(S["c_mT"], 1)
                    if k == 5:
                        vec.memset(mT[:, 4, :, :], -BIG).then_inc(S["c_mT"], 1)
                    at("c_mT", H)
                else:
                    vec.memset(mT[:], 0.0).then_inc(S["c_mT"], 2)
                    at("c_mT", H)
                for r in range(2 * H):
                    h, d = r // 2, r % 2
                    col = P - 1 if d == 0 else 0
                    for b in range(2):
                        last = vec.tensor_copy(colb[:, b, :], mT[:, h, b, col:col + 1].to_broadcast([TB, TB]))
                    last.then_inc(S["c_colb"], 1)
                    at("c_row", r)
                    for bt in range(2):
                        last = vec.tensor_tensor(mm[:, bt, :], psS[0:TB, 0:TILES], cross[:, d, bt, :], ALU.add)
                    last.then_inc(S["c_mm"], 1)
                    at("c_mm", r)
                    if k:
                        vec.tensor_reduce(mB[:, d, :, h:h + 1], mm[:], AX.X, ALU.max).then_inc(S["c_mb"], 1)
                    else:
                        vec.memset(mB[:, d, :, h:h + 1], 0.0).then_inc(S["c_mb"], 1)
                    at("c_mb", r)
                    for bt in range(2):
                        last = vec.tensor_scalar(mm[:, bt, :], mm[:, bt, :], mB[:, d, bt, h:h + 1], None, ALU.subtract)
                    last.then_inc(S["c_dm"], 1)
                    at("c_wtT_ps", r)
                    for bt in range(2):
                        last = vec.tensor_copy(wtT[:, bt, :, :].rearrange("p b t -> p (b t)"), psT[bt][0:TB, 0:2 * TB])
                    last.then_inc(S["c_wtT"], 1)
                    for bt in range(2):
                        at("c_sum_ps", 2 * r + bt)
                        vec.tensor_copy(csum[:, d, bt, hw * h:hw * h + hw], psH[bt][0:TB, 0:hw]
                                        ).then_inc(S["c_sum"], 1)
                for r in range(2 * H):
                    h, b = r // 2, r % 2
                    if r:
                        at("c_exp", r - 1)
                    if k == 0:
                        last = vec.tensor_copy(arg[:, 1, :], seg[:, 0, b, :])
                        vec.tensor_copy(arg[:, 2, :], seg[:, 1, b, :]).then_inc(S["c_arg"], 1)
                        continue
                    for d in range(2):
                        last = vec.tensor_scalar(tmax[:, d, :], seg[:, d, b, :], mB[:, d, b, h:h + 1], None, ALU.add)
                    last.then_inc(S["c_t"], 1)
                    at("c_t", 4 * r)
                    for i, other in enumerate((tmax[:, 0, :], tmax[:, 1, :], mT[:, 4, b, :])):
                        vec.tensor_tensor(tmax[:, 2, :], mT[:, h, b, :] if i == 0 else tmax[:, 2, :], other, ALU.max
                                          ).then_inc(S["c_t"], 1)
                        at("c_t", 4 * r + 1 + i)
                    vec.tensor_tensor(arg[:, 0, :], mT[:, h, b, :], tmax[:, 2, :], ALU.subtract)
                    if k < 5:
                        vec.tensor_tensor(arg[:, 3, :], mT[:, 4, b, :], tmax[:, 2, :], ALU.subtract)
                    vec.tensor_tensor(arg[:, 1, :], tmax[:, 0, :], tmax[:, 2, :], ALU.subtract)
                    vec.tensor_tensor(arg[:, 2, :], tmax[:, 1, :], tmax[:, 2, :], ALU.subtract).then_inc(S["c_arg"], 1)
                    at("c_back_ps", r)
                    if k < 5:
                        vec.tensor_copy(c_self[:, TB * b:TB * b + TB], psT[r % 2][:, P:P + TB])
                    vec.tensor_copy(c_loc[:, h, TB * b:TB * b + TB], psT[r % 2][:, 0:TB]).then_inc(S["c_back"], 1)

            def post(k):
                name = f"P{k}"
                H, hw, wid = HEADS[k], HW[k], WID[k]
                layer = {0: 0, 2: 1, 4: 2, 5: 3}.get(k)
                enter(dve, name)

                def tcol(a, j, c, u):
                    return a[:, bass.ds(MR * c + u + j * (MR * plan.group[name]), 1)]

                def add_carries(j, c):
                    su = plan.slot(name, "uin", c)
                    dve.wait_ge(R["uin"][plan.slot(name, "uin", c)], plan.full(name, "uin", j, c))
                    for q in range(2):
                        dve.wait_ge(S["p_ps"], plan.seen(name, "p_ps", j, c, i=q))
                        for i in range(2):
                            u = 2 * q + i
                            for h in range(H):
                                a, z = hw * h, hw * h + hw
                                if k == 0:
                                    last = vec.tensor_tensor(t1[:, c % 2, u, a:z], uin[:, su, u, a:z],
                                                             psU[q][:, ROW * i + a:ROW * i + z], ALU.add)
                                else:
                                    last = vec.scalar_tensor_tensor(
                                        out=t1[:, c % 2, u, a:z], in0=uin[:, su, u, a:z],
                                        scalar=tcol(c_loc[:, h, :], j, c, u), in1=psU[q][:, ROW * i + a:ROW * i + z],
                                        op0=ALU.mult, op1=ALU.add)
                        last.then_inc(S["p_used"], 1)

                def layer0_rows(j, c):
                    dve.wait_ge(R["xs"][plan.slot(name, "xs", c)], plan.full(name, "xs", j, c))
                    dve.wait_ge(S["p_used"], plan.seen(name, "p_used", j, c))
                    if not before(j, c, 4):
                        dve.wait_ge(S["xT_ps"], plan.seen(name, "xT_ps", j, c, back=4))
                    vec.scalar_tensor_tensor(out=xin[:, c % 4, :, :], in0=t1[:, c % 2, :, 0:P], scalar=0.5,
                                             in1=xs[:, plan.slot(name, "xs", c), :, 0:P], op0=ALU.mult, op1=ALU.add
                                             ).then_inc(S["u_ready"], 1)

                def add_self(j, c):
                    dve.wait_ge(R["xs"][plan.slot(name, "xs", c)], plan.full(name, "xs", j, c))
                    dve.wait_ge(S["p_used"], plan.seen(name, "p_used", j, c))
                    for u in range(MR):
                        last = vec.scalar_tensor_tensor(
                            out=t1[:, c % 2, u, 0:wid], in0=xs[:, plan.slot(name, "xs", c), u, 0:wid],
                            scalar=tcol(c_self, j, c, u), in1=t1[:, c % 2, u, 0:wid], op0=ALU.mult, op1=ALU.add)
                    last.then_inc(S["selfed"], 1)

                def guard(j, c):
                    dve.wait_ge(S["p_used"], plan.seen(name, "p_used", j, c))
                    t = t1[:, c % 2, :, :].rearrange("p u (h e) -> p u h e", h=4)
                    vec.tensor_scalar(rz[:], t[:, :, :, 32:33], 1e-9, None, ALU.max).then_inc(S["zmax"], 1)

                def invert(j, c):
                    if k < 5:
                        dve.wait_ge(S["selfed"], plan.seen(name, "selfed", j, c))
                        vec.reciprocal(rz[:, :, 0, :], t1[:, c % 2, :, P:P + 1]).then_inc(S["rz"], 1)
                    else:
                        dve.wait_ge(S["zmax"], plan.seen(name, "zmax", j, c))
                        vec.reciprocal(rz[:], rz[:]).then_inc(S["rz"], 1)

                def divide(j, c):
                    if k not in (1, 3):
                        rows_free(name, j, c)
                    dve.wait_ge(S["rz"], plan.seen(name, "rz", j, c))
                    if k in (1, 3):
                        if not before(j, c, 4):
                            dve.wait_ge(S["xT_ps"], plan.seen(name, "xT_ps", j, c, back=4))
                        vec.tensor_tensor(xin[:, c % 4, :, :], t1[:, c % 2, :, 0:P],
                                          rz[:, :, 0, :].to_broadcast([P, MR, P]), ALU.mult
                                          ).then_inc(S["u_ready"], 1)
                    elif k < 5:
                        s = plan.slot(name, "xr", c)
                        dve.wait_ge(S["biased"], plan.seen(name, "biased", j, c))
                        for u in range(MR):
                            last = vec.scalar_tensor_tensor(
                                out=rb[:, c % 4, u, :], in0=t1[:, c % 2, u, 0:P], scalar=rz[:, u, 0, :],
                                in1=xr[:, s, u, :], op0=ALU.mult, op1=ALU.add)
                        last.then_inc(S["res2"], 1)
                    else:
                        t = t1[:, c % 2, :, :].rearrange("p u (h e) -> p u h e", h=4)
                        vec.tensor_tensor(rb[:, c % 4, :, :].rearrange("p u (h e) -> p u h e", h=4), t[:, :, :, 0:32],
                                          rz[:].to_broadcast([P, MR, 4, 32]), ALU.mult).then_inc(S["un"], 1)

                def add_rows(j, c):
                    dve.wait_ge(S["biased"], plan.seen(name, "biased", j, c))
                    dve.wait_ge(S["un"], plan.seen(name, "un", j, c))
                    vec.tensor_tensor(rb[:, c % 4, :, :], rb[:, c % 4, :, :], xr[:, plan.slot(name, "xr", c), :, :],
                                      ALU.add).then_inc(S["res2"], 1)

                def score_products(j, c):
                    if k in (0, 2):
                        dve.wait_ge(S["x_ready"], plan.seen(name, "x_ready", j, c))
                        rows = xst[:, plan.slot(name, "xst", c), :, :]
                    else:
                        dve.wait_ge(S["y_used"], plan.seen(name, "y_used", j, c))
                        rows = gst[:, plan.slot(name, "gst", c), :, :]
                    for i in range(2):
                        for u in range(MR):
                            last = vec.tensor_tensor_reduce(junk[:, MR * i + u, :], rows[:, u, :], VB[:, 2 * k + i, :],
                                                            1.0, 0.0, ALU.mult, ALU.add, own_s[:, i, u:u + 1])
                    last.then_inc(S["own_sc"], 1)

                def score_sum(j, c):
                    cols = bass.ds(MR * c + j * (MR * plan.group[name]), MR)
                    dve.wait_ge(S["own_sc"], plan.seen(name, "own_sc", j, c))
                    vec.tensor_scalar(a_dst[:, 0, cols], own_s[:, 1, :], 0.0, None, ALU.add)
                    vec.tensor_tensor(own_m[:, 0, :], own_s[:, 0, :], own_s[:, 1, :], ALU.add).then_inc(S["own_sum"], 1)

                def self_score(j, c):
                    cols = bass.ds(MR * c + j * (MR * plan.group[name]), MR)
                    dve.wait_ge(S["own_sum"], plan.seen(name, "own_sum", j, c))
                    vec.scalar_tensor_tensor(out=e_self[:, cols], in0=own_m[:, 0, :], scalar=SLOPE,
                                             in1=own_m[:, 0, :], op0=ALU.mult, op1=ALU.max)

                def head_products(j, c):
                    dve.wait_ge(S["y_used"], plan.seen(name, "y_used", j, c))
                    vec.tensor_tensor(junk[:, 0:MR, :], gst[:, plan.slot(name, "gst", c), :, :],
                                      A5[:, 1:2, :].to_broadcast([P, MR, P]), ALU.mult).then_inc(S["own_prod"], 1)

                def head_sums(j, c):
                    dve.wait_ge(S["own_prod"], plan.seen(name, "own_prod", j, c))
                    vec.tensor_reduce(own_m[:].rearrange("p h u -> p u h"),
                                      junk[:, 0:MR, :].rearrange("p u (h e) -> p u h e", h=4), AX.X, ALU.add
                                      ).then_inc(S["own_sc"], 1)

                def head_scores(j, c):
                    dve.wait_ge(S["own_sc"], plan.seen(name, "own_sc", j, c))
                    vec.tensor_scalar(a_dst[:, :, bass.ds(MR * c + j * (MR * plan.group[name]), MR)], own_m[:], 0.0,
                                      None, ALU.add).then_inc(S["own_sum"], 1)

                shift_rows, stats, mean_variance = norm(name)
                bias, leak = add_bias(name, layer), leaky(name)
                add_y = add_product(name, lambda c: xs[:, plan.slot(name, "xs", c), :, 0:P])

                def slot_0(at):
                    for j, c in at(5):
                        shift_rows(j, c)
                    for j, c in at(0):
                        add_carries(j, c)
                    for j, c in at(2):
                        leak(j, c)
                    for j, c in at(0):
                        layer0_rows(j, c)
                    for j, c in at(3):
                        add_y(j, c)
                    for j, c in at(3):
                        bias(j, c)
                    for j, c in at(3):
                        stats(j, c)
                    for j, c in at(7):
                        score_products(j, c)
                    for j, c in at(3):
                        mean_variance(j, c)
                    for j, c in at(7):
                        score_sum(j, c)
                    for j, c in at(7):
                        self_score(j, c)

                def slot_1_3(at):
                    for j, c in at(0):
                        add_carries(j, c)
                    for j, c in at(4):
                        score_products(j, c)
                    for j, c in at(0):
                        add_self(j, c)
                    for j, c in at(4):
                        score_sum(j, c)
                    for j, c in at(0):
                        invert(j, c)
                    for j, c in at(4):
                        self_score(j, c)
                    for j, c in at(0):
                        divide(j, c)

                def slot_2(at):
                    for j, c in at(2):
                        shift_rows(j, c)
                    for j, c in at(0):
                        add_carries(j, c)
                    for j, c in at(0):
                        add_self(j, c)
                    for j, c in at(0):
                        invert(j, c)
                    for j, c in at(4):
                        score_products(j, c)
                    for j, c in at(0):
                        divide(j, c)
                    for j, c in at(4):
                        score_sum(j, c)
                    for j, c in at(4):
                        self_score(j, c)
                    for j, c in at(0):
                        stats(j, c)
                    for j, c in at(0):
                        mean_variance(j, c)

                def slot_4(at):
                    for j, c in at(2):
                        shift_rows(j, c)
                    for j, c in at(0):
                        add_carries(j, c)
                    for j, c in at(0):
                        add_self(j, c)
                    for j, c in at(0):
                        invert(j, c)
                    for j, c in at(6):
                        head_products(j, c)
                    for j, c in at(0):
                        divide(j, c)
                    for j, c in at(6):
                        head_sums(j, c)
                    for j, c in at(6):
                        head_scores(j, c)
                    for j, c in at(0):
                        stats(j, c)
                    for j, c in at(0):
                        mean_variance(j, c)

                def slot_5(at):
                    for j, c in at(2):
                        shift_rows(j, c)
                    for j, c in at(0):
                        add_carries(j, c)
                    for j, c in at(0):
                        guard(j, c)
                    for j, c in at(0):
                        invert(j, c)
                    for j, c in at(0):
                        divide(j, c)
                    for j, c in at(0):
                        add_rows(j, c)
                    for j, c in at(0):
                        stats(j, c)
                    for j, c in at(0):
                        mean_variance(j, c)

                pipeline(dve, plan, name, (7, 4, 4, 4, 6, 3)[k], (slot_0, slot_1_3, slot_2, slot_1_3, slot_4, slot_5)[k])

            for k in range(PHASES):
                dense(k) if k < 4 else local(k)
                combine(k)
                post(k)


_WEIGHTS = ["L0_gnn_W1", "L0_gnn_b1", "L0_gnn_W2", "L0_gnn_b2",
            "L1_gnn_W1", "L1_gnn_a1_src", "L1_gnn_a1_dst", "L1_gnn_b1",
            "L1_gnn_W2", "L1_gnn_a2_src", "L1_gnn_a2_dst", "L1_gnn_b2",
            "L2_gnn_W1", "L2_gnn_a1_src", "L2_gnn_a1_dst", "L2_gnn_b1",
            "L2_gnn_W2", "L2_gnn_a2_src", "L2_gnn_a2_dst", "L2_gnn_b2",
            "L3_gnn_W", "L3_gnn_att", "L3_gnn_bias"]


def kernel(**inputs):
    import numpy as _np
    import concourse.bacc as _bacc
    from concourse import mybir as _mybir
    from concourse.bass_utils import run_bass_kernel_spmd as _run

    nc = _bacc.Bacc("TRN2", target_bir_lowering=False, num_devices=1)
    arrays, aps = {}, {}
    for name in ["x", "src", "dst", "edge_attr_128"] + _WEIGHTS:
        a = _np.ascontiguousarray(inputs[name])
        arrays[f"in_{name}"] = a
        aps[name] = nc.dram_tensor(f"in_{name}", a.shape, _mybir.dt.from_np(a.dtype), kind="ExternalInput").ap()
    w = {name: aps[name] for name in _WEIGHTS}
    w["out"] = nc.dram_tensor("out_0", (NODES, D), F32, kind="ExternalOutput").ap()
    build(nc, aps["x"], aps["src"], aps["dst"], aps["edge_attr_128"], w)
    r = _run(nc, [arrays], core_ids=[0])
    return r.results[0]["out_0"]
```
